# Optimizing a Trainium2 kernel written in Bass

```python
import numpy as np
import jax
import jax.numpy as jnp

def _softmax(x, axis=-1):
    return jax.nn.softmax(x, axis=axis)

def _gelu(x):
    return jax.nn.gelu(x, approximate=True)

def _silu(x):
    return jax.nn.silu(x)

def _sigmoid(x):
    return jax.nn.sigmoid(x)

def _layernorm(x, axis=-1, eps=1e-05):
    m = jnp.mean(x, axis=axis, keepdims=True)
    v = jnp.var(x, axis=axis, keepdims=True)
    return (x - m) / jnp.sqrt(v + eps)

def _scatter_add(tgt, idx, src, axis=0):
    return tgt.at[idx].add(src)

def _segment_sum(src, seg, n):
    return jax.ops.segment_sum(src, seg, n)
kernel_name = 'mk_decoder_preln_d2_seqx_r4_d30413'

def setup_inputs(seed: int=0):
    np.random.seed(seed)
    _w = jnp.asarray

    def _rec_inputs():
        import jax
        import jax.numpy as jnp
        _rk = jax.random.key(seed)
        x = -0.000929 + 1 * jax.random.normal(jax.random.fold_in(_rk, 1), (8, 112, 256), jnp.float32)
        _lenS = 112 - jax.random.randint(jax.random.fold_in(_rk, 7), (8,), 0, max(1, 112 // 4) + 1, jnp.int32)
        _lenS2 = 375 - jax.random.randint(jax.random.fold_in(_rk, 8), (8,), 0, max(1, 375 // 4) + 1, jnp.int32)
        _ctx_1024P = jax.random.normal(jax.random.fold_in(_rk, 11), (8, 16, 256), jnp.float32)
        _ctx_1024c = jax.random.dirichlet(jax.random.fold_in(_rk, 511), 0.3 * jnp.ones((16,), jnp.float32), (8, 375))
        _ctx_1024t = jnp.einsum('bsk,bkd->bsd', _ctx_1024c, _ctx_1024P)
        _ctx_1024t = _ctx_1024t * jax.lax.rsqrt(jnp.mean(jnp.square(_ctx_1024t)) + 1e-12) * 0.953939
        ctx_1024 = -1.52775e-05 + 0.999936 * (_ctx_1024t + 0.3 * jax.random.normal(jax.random.fold_in(_rk, 611), (8, 375, 256), jnp.float32))
        return (x, ctx_1024)
    x, ctx_1024 = _rec_inputs()

    def _L0_attn_setup():
        import jax, jax.numpy as jnp
        import numpy as np
        D_MODEL = 256
        NHEAD = 16
        HEAD_DIM = D_MODEL // NHEAD
        B, L = (4, 1024)
        LN_EPS = 1e-05

        def _retention(v, lam):

            def step(state, v_t):
                state = lam[None, :, None] * state + v_t
                return (state, state)
            v_l_first = jnp.swapaxes(v, 0, 1)
            init = jnp.zeros(v_l_first.shape[1:], dtype=v.dtype)
            _, states = jax.lax.scan(step, init, v_l_first)
            return jnp.swapaxes(states, 0, 1)
        key = jax.random.key(seed)
        ks = jax.random.split(key, 8)
        x = jax.random.normal(ks[0], (B, L, D_MODEL), dtype=jnp.float32)
        sin = jnp.zeros((L, HEAD_DIM), dtype=jnp.float32)
        cos = jnp.zeros((L, HEAD_DIM), dtype=jnp.float32)
        decay = jax.random.uniform(ks[1], (NHEAD, 2, 1), dtype=jnp.float32)
        scale = 0.02
        Wq = jax.random.normal(ks[2], (D_MODEL, D_MODEL), dtype=jnp.float32) * scale
        Wv = jax.random.normal(ks[3], (D_MODEL, D_MODEL), dtype=jnp.float32) * scale
        Wo = jax.random.normal(ks[4], (D_MODEL, D_MODEL), dtype=jnp.float32) * scale
        Wg = jax.random.normal(ks[5], (D_MODEL, D_MODEL), dtype=jnp.float32) * scale
        ln_g = jnp.ones((D_MODEL,), dtype=jnp.float32)
        ln_b = jnp.zeros((D_MODEL,), dtype=jnp.float32)
        return {'x': x, 'sin': sin, 'cos': cos, 'decay': decay, 'Wq': Wq, 'Wv': Wv, 'Wo': Wo, 'Wg': Wg, 'ln_g': ln_g, 'ln_b': ln_b}
    _L0_attn_all = _L0_attn_setup()
    _L0_attn_in = {k: v for k, v in _L0_attn_all.items() if k in ('sin', 'cos', 'decay', 'Wq', 'Wv', 'Wo', 'Wg', 'ln_g', 'ln_b')}
    del _L0_attn_all

    def _L0_xattn_setup():
        import jax, jax.numpy as jnp
        import numpy as np
        DIM = 256
        H = 16
        D = 64
        INNER = H * D
        EPS = 1e-05

        def layernorm(x, w, b):
            mu = jnp.mean(x, axis=-1, keepdims=True)
            var = jnp.var(x, axis=-1, keepdims=True)
            return (x - mu) * jax.lax.rsqrt(var + EPS) * w + b
        key = jax.random.key(seed)
        ks = jax.random.split(key, 8)
        B, N, S = (4, 64, 2048)
        s = 1.0 / np.sqrt(DIM)
        return {'latents': jax.random.normal(ks[0], (B, N, DIM), jnp.float32), 'context': jax.random.normal(ks[1], (B, S, DIM), jnp.float32), 'ln_l_w': jnp.ones((DIM,), jnp.float32), 'ln_l_b': jnp.zeros((DIM,), jnp.float32), 'ln_c_w': jnp.ones((DIM,), jnp.float32), 'ln_c_b': jnp.zeros((DIM,), jnp.float32), 'Wq': jax.random.normal(ks[2], (DIM, INNER), jnp.float32) * s, 'Wkv': jax.random.normal(ks[3], (DIM, 2 * INNER), jnp.float32) * s, 'Wo': jax.random.normal(ks[4], (INNER, DIM), jnp.float32) * (1.0 / np.sqrt(INNER)), 'bo': jnp.zeros((DIM,), jnp.float32)}
    _L0_xattn_all = _L0_xattn_setup()
    _L0_xattn_in = {k: v for k, v in _L0_xattn_all.items() if k in ('ln_l_w', 'ln_l_b', 'ln_c_w', 'ln_c_b', 'Wq', 'Wkv', 'Wo', 'bo')}
    del _L0_xattn_all

    def _L0_ffn_setup():
        import jax, jax.numpy as jnp
        import numpy as np
        H = 16
        TOP_K = 2
        LN_EPS = 1e-05
        key = jax.random.key(seed)
        ks = jax.random.split(key, 8)
        B, S, E, NE = (2, 256, 256, 8)
        w = lambda k, shp: jax.random.normal(k, shp, dtype=jnp.float32) * 0.02
        return {'x': jax.random.normal(ks[0], (B, S, E), dtype=jnp.float32), 'rW1': w(ks[1], (E // 2, E)), 'rb1': jnp.zeros((E // 2,), jnp.float32), 'ln_g': jnp.ones((E // 2,), jnp.float32), 'ln_b': jnp.zeros((E // 2,), jnp.float32), 'rW2': w(ks[2], (NE, E // 2)), 'rb2': jnp.zeros((NE,), jnp.float32), 'qW': w(ks[3], (NE, E, E)), 'qb': jnp.zeros((NE, E), jnp.float32), 'kW': w(ks[4], (NE, E, E)), 'kb': jnp.zeros((NE, E), jnp.float32), 'vW': w(ks[5], (NE, E, E)), 'vb': jnp.zeros((NE, E), jnp.float32), 'oW': w(ks[6], (NE, E, E)), 'ob': jnp.zeros((NE, E), jnp.float32)}
    _L0_ffn_all = _L0_ffn_setup()
    _L0_ffn_in = {k: v for k, v in _L0_ffn_all.items() if k in ('rW1', 'rb1', 'ln_g', 'ln_b', 'rW2', 'rb2', 'qW', 'qb', 'kW', 'kb', 'vW', 'vb', 'oW', 'ob')}
    del _L0_ffn_all

    def _L1_attn_setup():
        import jax, jax.numpy as jnp
        import numpy as np
        KERNEL_SIZE = 16

        def _pad_amounts(kernel_size):
            side = (kernel_size - 1) // 2
            if (kernel_size - 1) % 2:
                return (side, side + 1)
            return (side, side)
        key = jax.random.key(seed)
        k1, k2, k3, k4 = jax.random.split(key, 4)
        B, T, H = (4, 512, 256)
        inputs = jax.random.normal(k1, (B, T, H), dtype=jnp.float32)
        w1 = jax.random.normal(k2, (H, H), dtype=jnp.float32) / np.sqrt(H)
        w2 = jax.random.normal(k3, (H, H), dtype=jnp.float32) / np.sqrt(H)
        v = jax.random.normal(k4, (H, 1), dtype=jnp.float32) / np.sqrt(H)
        return {'inputs': inputs, 'w1': w1, 'w2': w2, 'v': v}
    _L1_attn_all = _L1_attn_setup()
    _L1_attn_in = {k: v for k, v in _L1_attn_all.items() if k in ('w1', 'w2', 'v')}
    del _L1_attn_all

    def _L1_xattn_setup():
        import jax, jax.numpy as jnp
        import numpy as np
        B, S, D = (4, 512, 256)
        HEAD, DIM = (16, 64)
        key = jax.random.key(seed)
        ks = jax.random.split(key, 7)
        mk = lambda k, shp, scale: jax.random.normal(k, shp, dtype=jnp.float32) * scale
        w_scale = np.sqrt(2.0 / D).astype(np.float32)
        return {'query': mk(ks[0], (B, S, D), 1.0), 'key': mk(ks[1], (B, S, D), 1.0), 'value': mk(ks[2], (B, S, D), 1.0), 'Wq': mk(ks[3], (D, HEAD * DIM), w_scale), 'Wk': mk(ks[4], (D, HEAD * DIM), w_scale), 'Wv': mk(ks[5], (D, HEAD * DIM), w_scale), 'Wo': mk(ks[6], (HEAD * DIM, D), w_scale)}
    _L1_xattn_all = _L1_xattn_setup()
    _L1_xattn_in = {k: v for k, v in _L1_xattn_all.items() if k in ('Wq', 'Wk', 'Wv', 'Wo')}
    del _L1_xattn_all

    def _L1_ffn_setup():
        import math
        import jax, jax.numpy as jnp
        import numpy as np
        E = 8
        H = 256
        HP = 128
        SPARSITY = 8
        N_ROTATE = 64
        ROPE_BASE = 10000.0

        def _rope(x, pos):
            half = N_ROTATE // 2
            inv_freq = 1.0 / ROPE_BASE ** (jnp.arange(half, dtype=jnp.float32) * 2.0 / N_ROTATE)
            ang = pos.astype(jnp.float32)[..., None] * inv_freq
            sin, cos = (jnp.sin(ang), jnp.cos(ang))
            x1, x2 = (x[..., :half], x[..., half:])
            return jnp.concatenate([x1 * cos - x2 * sin, x2 * cos + x1 * sin], axis=-1)
        key = jax.random.key(seed)
        k1, k2, k3, k4 = jax.random.split(key, 4)
        B, T = (4, 2048)
        X = jax.random.normal(k1, (B, T, H), dtype=jnp.float32)
        Wr = jax.random.uniform(k2, (E, H), minval=-1 / math.sqrt(H), maxval=1 / math.sqrt(H), dtype=jnp.float32)
        bq = 1 / math.sqrt(3 * HP)
        Wqkv = jax.random.uniform(k3, (E, H, 3 * HP), minval=-bq, maxval=bq, dtype=jnp.float32)
        bo = 1 / math.sqrt(H * E)
        Wo = jax.random.uniform(k4, (E, HP, H), minval=-bo, maxval=bo, dtype=jnp.float32)
        return {'X': X, 'Wr': Wr, 'Wqkv': Wqkv, 'Wo': Wo}
    _L1_ffn_all = _L1_ffn_setup()
    _L1_ffn_in = {k: v for k, v in _L1_ffn_all.items() if k in ('Wr', 'Wqkv', 'Wo')}
    del _L1_ffn_all
    return {'x': x, 'ctx_1024': ctx_1024, 'L0_attn_sin': _L0_attn_in['sin'], 'L0_attn_cos': _L0_attn_in['cos'], 'L0_attn_decay': _L0_attn_in['decay'], 'L0_attn_Wq': _L0_attn_in['Wq'], 'L0_attn_Wv': _L0_attn_in['Wv'], 'L0_attn_Wo': _L0_attn_in['Wo'], 'L0_attn_Wg': _L0_attn_in['Wg'], 'L0_attn_ln_g': _L0_attn_in['ln_g'], 'L0_attn_ln_b': _L0_attn_in['ln_b'], 'L0_xattn_ln_l_w': _L0_xattn_in['ln_l_w'], 'L0_xattn_ln_l_b': _L0_xattn_in['ln_l_b'], 'L0_xattn_ln_c_w': _L0_xattn_in['ln_c_w'], 'L0_xattn_ln_c_b': _L0_xattn_in['ln_c_b'], 'L0_xattn_Wq': _L0_xattn_in['Wq'], 'L0_xattn_Wkv': _L0_xattn_in['Wkv'], 'L0_xattn_Wo': _L0_xattn_in['Wo'], 'L0_xattn_bo': _L0_xattn_in['bo'], 'L0_ffn_rW1': _L0_ffn_in['rW1'], 'L0_ffn_rb1': _L0_ffn_in['rb1'], 'L0_ffn_ln_g': _L0_ffn_in['ln_g'], 'L0_ffn_ln_b': _L0_ffn_in['ln_b'], 'L0_ffn_rW2': _L0_ffn_in['rW2'], 'L0_ffn_rb2': _L0_ffn_in['rb2'], 'L0_ffn_qW': _L0_ffn_in['qW'], 'L0_ffn_qb': _L0_ffn_in['qb'], 'L0_ffn_kW': _L0_ffn_in['kW'], 'L0_ffn_kb': _L0_ffn_in['kb'], 'L0_ffn_vW': _L0_ffn_in['vW'], 'L0_ffn_vb': _L0_ffn_in['vb'], 'L0_ffn_oW': _L0_ffn_in['oW'], 'L0_ffn_ob': _L0_ffn_in['ob'], 'L1_attn_w1': _L1_attn_in['w1'], 'L1_attn_w2': _L1_attn_in['w2'], 'L1_attn_v': _L1_attn_in['v'], 'L1_xattn_Wq': _L1_xattn_in['Wq'], 'L1_xattn_Wk': _L1_xattn_in['Wk'], 'L1_xattn_Wv': _L1_xattn_in['Wv'], 'L1_xattn_Wo': _L1_xattn_in['Wo'], 'L1_ffn_Wr': _L1_ffn_in['Wr'], 'L1_ffn_Wqkv': _L1_ffn_in['Wqkv'], 'L1_ffn_Wo': _L1_ffn_in['Wo']}

def reference(x, ctx_1024, L0_attn_sin, L0_attn_cos, L0_attn_decay, L0_attn_Wq, L0_attn_Wv, L0_attn_Wo, L0_attn_Wg, L0_attn_ln_g, L0_attn_ln_b, L0_xattn_ln_l_w, L0_xattn_ln_l_b, L0_xattn_ln_c_w, L0_xattn_ln_c_b, L0_xattn_Wq, L0_xattn_Wkv, L0_xattn_Wo, L0_xattn_bo, L0_ffn_rW1, L0_ffn_rb1, L0_ffn_ln_g, L0_ffn_ln_b, L0_ffn_rW2, L0_ffn_rb2, L0_ffn_qW, L0_ffn_qb, L0_ffn_kW, L0_ffn_kb, L0_ffn_vW, L0_ffn_vb, L0_ffn_oW, L0_ffn_ob, L1_attn_w1, L1_attn_w2, L1_attn_v, L1_xattn_Wq, L1_xattn_Wk, L1_xattn_Wv, L1_xattn_Wo, L1_ffn_Wr, L1_ffn_Wqkv, L1_ffn_Wo):
    import jax
    import jax.numpy as jnp

    def _L0_attn_ref(x, sin, cos, decay, Wq, Wv, Wo, Wg, ln_g, ln_b):
        import jax, jax.numpy as jnp
        import numpy as np
        D_MODEL = 256
        NHEAD = 16
        HEAD_DIM = D_MODEL // NHEAD
        B, L = (4, 1024)
        LN_EPS = 1e-05

        def _retention(v, lam):

            def step(state, v_t):
                state = lam[None, :, None] * state + v_t
                return (state, state)
            v_l_first = jnp.swapaxes(v, 0, 1)
            init = jnp.zeros(v_l_first.shape[1:], dtype=v.dtype)
            _, states = jax.lax.scan(step, init, v_l_first)
            return jnp.swapaxes(states, 0, 1)
        del sin, cos
        Bx, Lx, D = x.shape
        H = decay.shape[0]
        Dh = D // H
        q = (x @ Wq.T).reshape(Bx, Lx, H, Dh)
        v = (x @ Wv.T).reshape(Bx, Lx, H, Dh)
        lam = decay[:, 1, 0]
        state = _retention(v, lam)
        y = (q * state).reshape(Bx, Lx, D)
        mu = jnp.mean(y, axis=-1, keepdims=True)
        var = jnp.mean(jnp.square(y - mu), axis=-1, keepdims=True)
        y = (y - mu) * jax.lax.rsqrt(var + LN_EPS) * ln_g + ln_b
        gate = jax.nn.silu(x @ Wg.T)
        y = y * gate
        return y @ Wo.T

    def _L0_xattn_ref(latents, context, ln_l_w, ln_l_b, ln_c_w, ln_c_b, Wq, Wkv, Wo, bo):
        import jax, jax.numpy as jnp
        import numpy as np
        DIM = 256
        H = 16
        D = 64
        INNER = H * D
        EPS = 1e-05

        def layernorm(x, w, b):
            mu = jnp.mean(x, axis=-1, keepdims=True)
            var = jnp.var(x, axis=-1, keepdims=True)
            return (x - mu) * jax.lax.rsqrt(var + EPS) * w + b
        b, n, _ = latents.shape
        s = context.shape[1]
        lat = layernorm(latents, ln_l_w, ln_l_b)
        ctx = layernorm(context, ln_c_w, ln_c_b)
        q = (lat @ Wq).reshape(b, n, H, D).transpose(0, 2, 1, 3)
        kv = ctx @ Wkv
        k, v = jnp.split(kv, 2, axis=-1)
        k = k.reshape(b, s, H, D).transpose(0, 2, 1, 3)
        v = v.reshape(b, s, H, D).transpose(0, 2, 1, 3)
        scale = D ** (-0.5)
        attn = jnp.einsum('bhnd,bhsd->bhns', q, k) * scale
        attn = jnp.clip(attn, -11.0, 11.0)
        attn = jax.nn.softmax(attn, axis=-1)
        out = jnp.einsum('bhns,bhsd->bhnd', attn, v)
        out = out.transpose(0, 2, 1, 3).reshape(b, n, INNER)
        return out @ Wo + bo

    def _L0_ffn_ref(x, rW1, rb1, ln_g, ln_b, rW2, rb2, qW, qb, kW, kb, vW, vb, oW, ob):
        import jax, jax.numpy as jnp
        import numpy as np
        H = 16
        TOP_K = 2
        LN_EPS = 1e-05
        B, S, E = x.shape
        NE = qW.shape[0]
        Dh = E // H
        scale = 1.0 / jnp.sqrt(jnp.asarray(Dh, x.dtype))
        h = x @ rW1.T + rb1
        mu = h.mean(-1, keepdims=True)
        var = ((h - mu) ** 2).mean(-1, keepdims=True)
        h = (h - mu) * jax.lax.rsqrt(var + LN_EPS) * ln_g + ln_b
        h = jax.nn.relu(h)
        logits = h @ rW2.T + rb2
        probs = jax.nn.softmax(logits, axis=-1)
        tp, ti = jax.lax.top_k(probs, TOP_K)
        tp = tp / tp.sum(-1, keepdims=True)
        expert_mask = (jax.nn.one_hot(ti, NE, dtype=probs.dtype) * tp[..., None]).sum(-2)
        gates = jnp.moveaxis(expert_mask, -1, 0)

        def expert_step(acc, params):
            qw, qb_, kw, kb_, vw, vb_, ow, ob_, g = params
            q = (x @ qw.T + qb_).reshape(B, S, H, Dh).transpose(0, 2, 1, 3)
            k = (x @ kw.T + kb_).reshape(B, S, H, Dh).transpose(0, 2, 1, 3)
            v = (x @ vw.T + vb_).reshape(B, S, H, Dh).transpose(0, 2, 1, 3)
            scores = jnp.einsum('bhqd,bhkd->bhqk', q, k) * scale
            p = jax.nn.softmax(scores, axis=-1)
            o = jnp.einsum('bhqk,bhkd->bhqd', p, v)
            o = o.transpose(0, 2, 1, 3).reshape(B, S, E) @ ow.T + ob_
            return (acc + o * g[..., None], None)
        out, _ = jax.lax.scan(expert_step, jnp.zeros_like(x), (qW, qb, kW, kb, vW, vb, oW, ob, gates))
        return out

    def _L1_attn_ref(inputs, w1, w2, v):
        import jax, jax.numpy as jnp
        import numpy as np
        KERNEL_SIZE = 16

        def _pad_amounts(kernel_size):
            side = (kernel_size - 1) // 2
            if (kernel_size - 1) % 2:
                return (side, side + 1)
            return (side, side)
        B, T, H = inputs.shape
        K = KERNEL_SIZE
        pl, pr = _pad_amounts(K)
        x_pad = jnp.pad(inputs, ((0, 0), (pl, pr), (0, 0)))
        idx = jnp.arange(T)[:, None] + jnp.arange(K)[None, :]
        proj = x_pad @ w2
        local_proj = proj[:, idx]
        q = inputs @ w1
        score = jnp.squeeze(jnp.tanh(local_proj + q[:, :, None, :]) @ v, -1)
        weight = jax.nn.softmax(score, axis=-1)
        local = x_pad[:, idx]
        output = jnp.einsum('btk,btkh->bth', weight, local)
        return output

    def _L1_xattn_ref(query, key, value, Wq, Wk, Wv, Wo):
        import jax, jax.numpy as jnp
        import numpy as np
        B, S, D = (4, 512, 256)
        HEAD, DIM = (16, 64)
        Q = jnp.einsum('bsd,de->bse', query, Wq)
        K = jnp.einsum('bsd,de->bse', key, Wk)
        V = jnp.einsum('bsd,de->bse', value, Wv)
        scale = jnp.asarray(1.0 / np.sqrt(DIM), dtype=Q.dtype)
        scores = jnp.einsum('bqe,bke->bqk', Q, K) * scale
        attn = jax.nn.softmax(scores, axis=1)
        head = jnp.einsum('bqk,bke->bqe', attn, V)
        return jnp.einsum('bqe,ed->bqd', head, Wo)

    def _L1_ffn_ref(X, Wr, Wqkv, Wo):
        import math
        import jax, jax.numpy as jnp
        import numpy as np
        E = 8
        H = 256
        HP = 128
        SPARSITY = 8
        N_ROTATE = 64
        ROPE_BASE = 10000.0

        def _rope(x, pos):
            half = N_ROTATE // 2
            inv_freq = 1.0 / ROPE_BASE ** (jnp.arange(half, dtype=jnp.float32) * 2.0 / N_ROTATE)
            ang = pos.astype(jnp.float32)[..., None] * inv_freq
            sin, cos = (jnp.sin(ang), jnp.cos(ang))
            x1, x2 = (x[..., :half], x[..., half:])
            return jnp.concatenate([x1 * cos - x2 * sin, x2 * cos + x1 * sin], axis=-1)
        B, T, _ = X.shape
        k = min(max(T // SPARSITY, 2), T)
        logits = jax.nn.sigmoid(jnp.einsum('bth,eh->bte', X, Wr))
        topk_vals, topk_I = jax.lax.top_k(logits.transpose(0, 2, 1), k)
        idx_flat = topk_I.reshape(B, E * k)
        Xg = jnp.take_along_axis(X, idx_flat[:, :, None], axis=1).reshape(B, E, k, H)
        QKV = jnp.einsum('beki,eij->bekj', Xg, Wqkv)
        Q, K, V = jnp.split(QKV, 3, axis=-1)
        Q = jnp.concatenate([_rope(Q[..., :N_ROTATE], topk_I), Q[..., N_ROTATE:]], axis=-1)
        K = jnp.concatenate([_rope(K[..., :N_ROTATE], topk_I), K[..., N_ROTATE:]], axis=-1)
        M = topk_I[..., :, None] >= topk_I[..., None, :]
        scores = jnp.einsum('bekd,bemd->bekm', Q, K) / math.sqrt(HP)
        scores = jnp.where(M, scores, -jnp.inf)
        A = jax.nn.softmax(scores, axis=-1)
        AV = jnp.einsum('bekm,bemd->bekd', A, V)
        AV = AV * topk_vals[..., None]
        Xpre = jnp.einsum('bekj,eji->beki', AV, Wo)
        out = jnp.zeros((B, T, H), dtype=X.dtype)
        out = out.at[jnp.arange(B)[:, None], idx_flat].add(Xpre.reshape(B, E * k, H))
        return out
    x = x + _L0_attn_ref(_layernorm(x, axis=-1), L0_attn_sin, L0_attn_cos, L0_attn_decay, L0_attn_Wq, L0_attn_Wv, L0_attn_Wo, L0_attn_Wg, L0_attn_ln_g, L0_attn_ln_b)
    x = x + _L0_xattn_ref(_layernorm(x, axis=-1), ctx_1024, L0_xattn_ln_l_w, L0_xattn_ln_l_b, L0_xattn_ln_c_w, L0_xattn_ln_c_b, L0_xattn_Wq, L0_xattn_Wkv, L0_xattn_Wo, L0_xattn_bo)
    x = x + _L0_ffn_ref(_layernorm(x, axis=-1), L0_ffn_rW1, L0_ffn_rb1, L0_ffn_ln_g, L0_ffn_ln_b, L0_ffn_rW2, L0_ffn_rb2, L0_ffn_qW, L0_ffn_qb, L0_ffn_kW, L0_ffn_kb, L0_ffn_vW, L0_ffn_vb, L0_ffn_oW, L0_ffn_ob)
    x = x + _L1_attn_ref(_layernorm(x, axis=-1), L1_attn_w1, L1_attn_w2, L1_attn_v)
    x = x + _L1_xattn_ref(_layernorm(x, axis=-1), ctx_1024, ctx_1024, L1_xattn_Wq, L1_xattn_Wk, L1_xattn_Wv, L1_xattn_Wo)
    x = x + _L1_ffn_ref(_layernorm(x, axis=-1), L1_ffn_Wr, L1_ffn_Wqkv, L1_ffn_Wo)
    return x

_drawn_inputs = setup_inputs


def setup_inputs(seed=0):
    import zlib

    import numpy as np

    out = dict(_drawn_inputs(seed))
    spreads = {'L0_attn_sin': (0.0, 0.1),
     'L0_attn_cos': (0.0, 0.1),
     'L0_attn_ln_g': (1.0, 0.6),
     'L0_attn_ln_b': (0.0, 0.8),
     'L0_xattn_ln_l_w': (1.0, 0.2),
     'L0_xattn_ln_l_b': (0.0, 0.438),
     'L0_xattn_ln_c_w': (1.0, 0.2),
     'L0_xattn_ln_c_b': (0.0, 0.1),
     'L0_xattn_bo': (0.0, 0.1),
     'L0_ffn_rb1': (0.0, 0.1),
     'L0_ffn_ln_g': (1.0, 0.2),
     'L0_ffn_ln_b': (0.0, 0.1),
     'L0_ffn_rb2': (0.0, 0.1),
     'L0_ffn_qb': (0.0, 0.8),
     'L0_ffn_kb': (0.0, 0.8),
     'L0_ffn_vb': (0.0, 0.326),
     'L0_ffn_ob': (0.0, 0.1)}
    factors = {'L0_ffn_qW': 8.0, 'L0_ffn_kW': 8.0, 'L1_ffn_Wr': 8.0, 'L1_ffn_Wqkv': 8.0, 'L1_ffn_Wo': 8.0}
    for name, (base, spread) in spreads.items():
        noise = np.random.default_rng([zlib.crc32(name.encode()), seed]).standard_normal(out[name].shape)
        drawn = base * np.exp(spread * noise) if base else spread * noise
        out[name] = jnp.asarray(drawn.astype(out[name].dtype))
    for name, factor in factors.items():
        out[name] = (out[name] * factor).astype(out[name].dtype)
    return out
```

```python
from contextlib import ExitStack

import numpy as np
import concourse.bass as bass
from concourse import mybir

F32 = mybir.dt.float32
BF16 = mybir.dt.bfloat16
U32 = mybir.dt.uint32
ALU = mybir.AluOpType
ACT = mybir.ActivationFunctionType
AX = mybir.AxisListType

B, T, D = 8, 112, 256
S, KP = 375, 125
KTILES = S // KP
P = 128
C = D // P
XH, XD = 16, 64
INNER = XH * XD
IT = INNER // P
NE = 8
EH, ED = 16, 16
R1 = 128
LK, LPAD = 16, 7
TK = max(T // 8, 2)
HP = 128
ROT = 64
EPS = 1e-5
CLIP = 11.0
LNS = 6
NORMS = 10
REGION = 7296

COLS = {}
_n = 0
for _name, _w in (("lat_w", C), ("lat_b", C), ("ctx_w", C), ("ctx_b", C), ("qb", NE * C), ("kb", NE * C),
                  ("lam", C), ("v", C), ("iota", 1), ("even", 1), ("odd", 1)):
    COLS[_name] = _n
    _n += _w
NCOLS = _n
ROWS = {}
_n = 0
for _name, _w in (("ret_g", D), ("ret_b", D), ("bo", D), ("rb1", R1), ("ffn_g", R1), ("ffn_b", R1),
                  ("rb2", NE), ("vb", NE * D)):
    ROWS[_name] = (_n, _n + _w)
    _n += _w
NROWS = _n
CONST = {}
_n = 0
for _name, _w in (("ident", P), ("band", T + LK - 1), ("own", NE * TK), ("block", NE * TK), ("rope", 2 * ROT),
                  ("iota8", NE), ("sel", 4 * T)):
    CONST[_name] = (_n, _n + _w)
    _n += _w
NCONST = _n


DVE_STEPS = 100


def build(nc, a, out):
    with ExitStack() as ctx:
        def sb(name, shape, dt=F32):
            return ctx.enter_context(nc.sbuf_tensor(name, shape, dt))

        def sem(name):
            return ctx.enter_context(nc.semaphore(name))

        bank = [ctx.enter_context(nc.psum_tensor(f"bank{i}", [P, 512], F32)) for i in range(8)]

        ret_w = sb("ret_w", [P, 4, C, D])
        turns_w = sb("turns_w", [P, 2 * C * INNER])
        x_wq = turns_w[:, 0:C * INNER].rearrange("p (c n) -> p c n", c=C)
        x_wo = turns_w[:, C * INNER:].rearrange("p (i n) -> p i n", i=IT)
        c_wqk = turns_w[:, :].rearrange("p (q c n) -> p q c n", q=2 * NE, c=C)
        x_wkv = sb("x_wkv", [P, C, 2 * INNER])
        r_w1 = sb("r_w1", [P, C, R1])
        r_w2 = sb("r_w2", [P, NE])
        e_wq = sb("e_wq", [P, NE, C, D])
        e_wk = sb("e_wk", [P, NE, C, D])
        e_wv = sb("e_wv", [P, NE, C, D])
        e_wo = sb("e_wo", [P, NE, C, D])
        e_bo = sb("e_bo", [NE, D])
        l_w = sb("l_w", [P, 2, C, D])
        m_qk = sb("m_qk", [P, C, D])
        m_vo = sb("m_vo", [P, C, D])
        c_wr = sb("c_wr", [P, C, NE])
        c_wv = sb("c_wv", [P, NE, C, HP])
        c_wo = sb("c_wo", [P, NE, D])
        cols = sb("cols", [P, NCOLS])
        rows = sb("rows", [P, NROWS])
        const = sb("const", [P, NCONST])
        ident_b = sb("ident_b", [P, P], BF16)
        sel_b = sb("sel_b", [P, 4, T], BF16)
        mw_q = e_wq[:, 0:4].rearrange("p a c d -> p (a c) d")
        mw_k = e_wq[:, 4:8].rearrange("p a c d -> p (a c) d")
        mw_v = e_wk[:, 0:4].rearrange("p a c d -> p (a c) d")
        mw_o = e_wk[:, 4:8].rearrange("p a c d -> p (a c) d")

        x_in = sb("x_in", [T, D])
        x = sb("x", [T, D])
        x_out = sb("x_out", [T, D])
        xn = sb("xn", [T, D])
        xnT = sb("xnT", [P, C, T])
        stats = sb("stats", [P, KTILES, 6])
        mv = sb("mv", [P, KTILES, 2])
        var = sb("var", [P, KTILES])
        rstd = sb("rstd", [P, KTILES])
        minus_half = sb("minus_half", [P, KTILES])
        ctx_tok = sb("ctx_tok", [KP, KTILES, D])
        ctx_raw = sb("ctx_raw", [P, C, S])
        ctxnT = sb("ctxnT", [P, C, S])
        region = sb("region", [P, REGION])

        def at_word(lo, n, *dims, dt=F32):
            size = int(np.prod(dims))
            if dt == BF16:
                v = region[0:n, lo:lo + (size + 1) // 2].bitcast(BF16)
            elif dt == U32:
                v = region[0:n, lo:lo + size].bitcast(U32)
            else:
                v = region[0:n, lo:lo + size]
            spent[0] = lo + (size if dt != BF16 else (size + 1) // 2)
            assert spent[0] <= REGION, (spent[0], REGION)
            names = "abcd"[:len(dims)]
            if len(dims) == 1:
                return v
            return v.rearrange("p (" + " ".join(names) + ") -> p " + " ".join(names),
                               **{k: d for k, d in zip(names, dims)})

        spent = [0]

        def then(n, *dims, dt=F32):
            return at_word(spent[0], n, *dims, dt=dt)

        x_v = sb("x_v", [KP, KTILES, XH, XD + 1])
        x_kT = at_word(0, P, IT, S)
        after_keys = spent[0]
        state = at_word(after_keys, P, C, T)
        yT = then(P, C, T)
        gate = then(T, D)
        eg = then(T, D)
        y2 = then(T, D)
        y2T = then(P, C, T)
        ctxn = then(KP, KTILES, D)
        x_o = at_word(after_keys, T, INNER)
        x_qT = then(P, IT, T)
        x_p = then(KP, 3, KTILES, T)
        x_oT = then(P, IT, T)
        x_rc = sb("x_rc", [T, 4, 1])
        e_v = sb("e_v", [T, 2, EH, ED + 1])
        e_max = sb("e_max", [T, 4, 32], BF16)
        h1 = at_word(0, T, R1)
        h1T = then(P, T)
        lg = then(T, NE)
        pr = then(T, NE)
        top = then(T, 8)
        topi = then(T, 8, dt=U32)
        topf = then(T, 8)
        g01 = then(T, 2, NE)
        gates = then(T, NE)
        gatesT = then(NE, T)
        e_q = then(P, 2, C * 2 * T).rearrange("p e (c o t) -> p e c o t", c=C, o=2)
        e_k = then(P, 2, C, T)
        e_qb = then(P, C, 2, T, dt=BF16)
        e_kb = then(P, C, T, dt=BF16)
        e_maxT = then(P, T, dt=BF16)
        e_p = then(T, 2, 4, T)
        e_rc = then(T, EH, 1)
        e_o = then(T, EH, ED)
        e_oT = then(P, C, T)
        l_proj = sb("l_proj", [P, C, T + LK - 1])
        l_t = at_word(0, P, C, LK, T)
        l_q = then(P, C, T)
        l_w16 = then(T, LK)
        l_a = then(T, T)
        l_aT = then(T, T)
        m_z = then(KP, KTILES, D)
        m_g = at_word(0, P, C, T)
        m_e = then(KP, KTILES, T)
        m_nm = then(KP, KTILES)
        m_sum = then(KP, KTILES)
        c_s = at_word(0, NE, T)
        c_s2 = then(NE, T)
        c_top = then(NE, 16)
        c_idx = then(NE, 16, dt=U32)
        c_idxf = then(NE, 16)
        c_diag = then(NE, 2, NE, TK)
        c_pos = then(T, T)
        c_hot = then(T, T)
        c_hotT = then(T, T)
        c_iv = then(T, 2)
        c_cs = then(ROT, 2, T)
        c_xgT = then(P, C, T)
        c_qk = then(P, 2, T)
        c_rot = then(ROT, 2, T)
        c_vT = then(P, T)
        c_v = then(T, HP)
        c_pen = then(T, T)
        c_e = then(T, T)
        c_eT = then(T, T)
        c_avT = then(P, T)
        c_xpT = then(P, C, T)
        c_xp = then(T, D)
        sc1 = sb("sc1", [P, 16])
        pool_idle = sb("pool_idle", [1, 1])
        idle = sb("idle", [1, 1])
        ones8 = sb("ones8", [NE, T])

        def cst(name):
            lo, hi = CONST[name]
            return const[:, lo:hi]

        def row(name, n=T, at=0, width=None):
            lo, hi = ROWS[name]
            return rows[0:n, lo + at:(lo + at + width) if width else hi]

        def col(name, k=0, lo=0, hi=P):
            return cols[lo:hi, COLS[name] + k:COLS[name] + k + 1]

        ident = cst("ident")

        def view(bk, n, lo, *dims):
            size = int(np.prod(dims))
            v = bank[bk][0:n, lo:lo + size]
            if len(dims) == 1:
                return v
            names = "abc"[:len(dims)]
            return v.rearrange("p (" + " ".join(names) + ") -> p " + " ".join(names),
                               **{k: d for k, d in zip(names, dims)})

        def windows(ap, *dims):
            return bass.AP(ap.tensor, ap.offset, [ap.ap[0]] + [list(d) for d in dims])

        w_small = sem("w_small")
        w_ret = sem("w_ret")
        w_x = sem("w_x")
        wx_loaded = sem("wx_loaded")
        wc_loaded = sem("wc_loaded")
        w_e = sem("w_e")
        w_l = sem("w_l")
        w_m = sem("w_m")
        w_c = sem("w_c")
        consts_made = sem("consts_made")
        m_psum = sem("m_psum")
        m_made = sem("m_made")
        half_made = sem("half_made")
        x_out_free = sem("x_out_free")
        x_loaded = sem("x_loaded")
        ctx_loaded = sem("ctx_loaded")
        raw_loaded = sem("raw_loaded")
        out_stored = sem("out_stored")
        dve_done = sem("dve_done")
        var_ready = sem("var_ready")
        rstd_ready = sem("rstd_ready")
        xn_ready = sem("xn_ready")
        xt_psum = sem("xt_psum")
        xt_ready = sem("xt_ready")
        x_done = sem("x_done")
        ctxn_ready = sem("ctxn_ready")
        ctxt_psum = sem("ctxt_psum")
        ctxt_ready = sem("ctxt_ready")
        kv_psum = sem("kv_psum")
        kv_ready = sem("kv_ready")
        ret_qv = sem("ret_qv")
        ret_g = sem("ret_g")
        ret_eg = sem("ret_eg")
        ret_y = sem("ret_y")
        ret_yt = sem("ret_yt")
        ret_y2 = sem("ret_y2")
        ret_y2t_psum = sem("ret_y2t_psum")
        ret_y2t = sem("ret_y2t")
        sub_out = sem("sub_out")
        xq_psum = sem("xq_psum")
        xq_ready = sem("xq_ready")
        xs_psum = sem("xs_psum")
        xs_exp = sem("xs_exp")
        xs_clip = sem("xs_clip")
        xs_pv = sem("xs_pv")
        xo_ready = sem("xo_ready")
        xot_psum = sem("xot_psum")
        xot_ready = sem("xot_ready")
        r_h = sem("r_h")
        r_hn = sem("r_hn")
        r_ht_psum = sem("r_ht_psum")
        r_ht = sem("r_ht")
        r_lg = sem("r_lg")
        r_nm = sem("r_nm")
        r_exp = sem("r_exp")
        r_gates = sem("r_gates")
        r_gt_psum = sem("r_gt_psum")
        r_gt = sem("r_gt")
        eqk_psum = sem("eqk_psum")
        evo_psum = sem("evo_psum")
        eq_ready = sem("eq_ready")
        ek_ready = sem("ek_ready")
        ev_ready = sem("ev_ready")
        es_psum = sem("es_psum")
        es_max = sem("es_max")
        emt_psum = sem("emt_psum")
        emt_ready = sem("emt_ready")
        est_psum = sem("est_psum")
        est_exp = sem("est_exp")
        epv = sem("epv")
        eo_ready = sem("eo_ready")
        eot_ready = sem("eot_ready")
        l_psum = sem("l_psum")
        l_sum = sem("l_sum")
        l_tanh = sem("l_tanh")
        l_score = sem("l_score")
        l_nm = sem("l_nm")
        l_exp = sem("l_exp")
        l_band = sem("l_band")
        l_at_psum = sem("l_at_psum")
        l_at = sem("l_at")
        z_psum = sem("z_psum")
        z_ready = sem("z_ready")
        g_psum = sem("g_psum")
        g_ready = sem("g_ready")
        ms_psum = sem("ms_psum")
        ms_nm = sem("ms_nm")
        ms_exp = sem("ms_exp")
        ms_e = sem("ms_e")
        c_lg = sem("c_lg")
        c_en = sem("c_en")
        c_dg = sem("c_dg")
        c_rpsum = sem("c_rpsum")
        c_hots = sem("c_hots")
        c_gpsum = sem("c_gpsum")
        c_xg = sem("c_xg")
        c_qkv = sem("c_qkv")
        c_qk_ready = sem("c_qk_ready")
        c_vt_ready = sem("c_vt_ready")
        c_vpsum = sem("c_vpsum")
        c_v_ready = sem("c_v_ready")
        c_spsum = sem("c_spsum")
        c_nm = sem("c_nm")
        c_exp = sem("c_exp")
        c_en2 = sem("c_en2")
        c_etp = sem("c_etp")
        c_et = sem("c_et")
        c_avp = sem("c_avp")
        c_av = sem("c_av")
        c_xpp = sem("c_xpp")
        c_xps = sem("c_xps")
        c_xqp = sem("c_xqp")
        c_xqs = sem("c_xqs")

        NKV = IT + 2 * KTILES

        block = ctx.enter_context(nc.Block())

        @block.sync
        def _(sp):
            sp.dma_start(cols[:, :], a["cols"]).then_inc(w_small, 16)
            sp.dma_start(const[:, :], a["const"]).then_inc(w_small, 16)
            sp.dma_start(x_in[:, :], a["x"][0]).then_inc(x_loaded, 16)
            sp.dma_start(ctx_tok[:, :, :], a["ctx"][0].rearrange("(j p) d -> p j d", p=KP)).then_inc(ctx_loaded, 16)
            for i, name in enumerate(("ret_q", "ret_v", "ret_g", "ret_o")):
                sp.dma_start(ret_w[:, i], a[name]).then_inc(w_ret, 16)
            sp.dma_start(rows[:, :], a["rows"].partition_broadcast(P)).then_inc(w_small, 16)
            sp.dma_start(x_wkv[:, :, :], a["x_kv"]).then_inc(w_x, 16)
            sp.dma_start(x_wq, a["x_q"]).then_inc(wx_loaded, 16)
            sp.dma_start(x_wo, a["x_o"]).then_inc(wx_loaded, 16)
            sp.dma_start(r_w1[:, :, :], a["r_w1"]).then_inc(w_e, 16)
            sp.dma_start(r_w2[:, :], a["r_w2"]).then_inc(w_e, 16)
            sp.dma_start(e_bo[:, :], a["e_bo"]).then_inc(w_e, 16)
            sp.dma_start(e_wv[:, :, :, :], a["e_v"]).then_inc(w_e, 16)
            sp.dma_start(e_wo[:, :, :, :], a["e_o"]).then_inc(w_e, 16)
            sp.dma_start(ctx_raw[:, :, :], a["ctxT"][0].rearrange("(c p) k -> p c k", p=P)).then_inc(raw_loaded, 16)
            sp.dma_start(l_w[:, 0], a["l_w1"]).then_inc(w_l, 16)
            sp.dma_start(l_w[:, 1], a["l_w2"]).then_inc(w_l, 16)
            sp.dma_start(c_wr[:, :, :], a["c_r"]).then_inc(w_c, 16)
            sp.dma_start(c_wv[:, :, :, :], a["c_v"]).then_inc(w_c, 16)
            sp.dma_start(c_wo[:, :, :], a["c_o"]).then_inc(w_c, 16)
            sp.wait_ge(m_made, 2)
            sp.dma_start(e_wq[:, :, :, :], a["e_q"]).then_inc(w_e, 16)
            sp.dma_start(e_wk[:, :, :, :], a["e_k"]).then_inc(w_e, 16)
            with sp.Fori(0, B - 1) as b:
                sp.wait_ge(x_done, b * LNS + 1)
                sp.dma_start(x_in[:, :], a["x"][bass.ds(b + 1, 1)].rearrange("a t d -> (a t) d")).then_inc(x_loaded, 16)
                sp.wait_ge(ctxn_ready, b + 1)
                sp.dma_start(ctx_tok[:, :, :], a["ctx"][bass.ds(b + 1, 1)].rearrange("a (j p) d -> p (a j) d", p=KP)
                             ).then_inc(ctx_loaded, 16)
                sp.wait_ge(sub_out, b * LNS + 2)
                sp.dma_start(c_wqk, a["c_qk"]).then_inc(wc_loaded, 16)
                sp.wait_ge(ms_psum, b + 1)
                sp.dma_start(ctx_raw[:, :, :], a["ctxT"][bass.ds(b + 1, 1)].rearrange("a (c p) k -> p (a c) k", p=P)
                             ).then_inc(raw_loaded, 16)
                sp.wait_ge(c_qkv, b + 1)
                sp.dma_start(x_wq, a["x_q"]).then_inc(wx_loaded, 16)
                sp.dma_start(x_wo, a["x_o"]).then_inc(wx_loaded, 16)
            sp.wait_ge(sub_out, LNS * (B - 1) + 2)
            sp.dma_start(c_wqk, a["c_qk"]).then_inc(wc_loaded, 16)

        @block.gpsimd
        def _(pool):
            for i, (name, dst) in enumerate((("m_q", mw_q), ("m_k", mw_k), ("m_v", mw_v), ("m_o", mw_o))):
                pool.dma_start(dst, a[name]).then_inc(w_m, 16)
            nc.gpsimd.memset(minus_half[:, :], -0.5).then_inc(half_made, 1)
            nc.gpsimd.memset(pool_idle[:, :], 0.0).then_inc(x_out_free, 1)
            pool.wait_ge(half_made, 1)
            with pool.Fori(0, B) as b:
                for k in range(NORMS):
                    pool.wait_ge(var_ready, b * NORMS + (k + 1))
                    n, w = (KP, KTILES) if k == 1 else (T, 1)
                    nc.gpsimd.tensor_tensor(rstd[0:n, 0:w], var[0:n, 0:w], minus_half[0:n, 0:w], ALU.pow
                                            ).then_inc(rstd_ready, 1)
                pool.wait_ge(x_done, LNS * b + LNS)
                pool.dma_start(out[bass.ds(b, 1)].rearrange("a t d -> (a t) d"), x_out[:, :]).then_inc(out_stored, 16)
                pool.wait_ge(out_stored, b * 16 + 16)
                nc.gpsimd.tensor_tensor(pool_idle[:, :], minus_half[0:1, 0:1], minus_half[0:1, 0:1], ALU.mult
                                        ).then_inc(x_out_free, 1)
            pool.wait_ge(out_stored, 16 * B)

        @block.tensor
        def _(pe):
            mm = nc.tensor.matmul

            def tr(dst, src, n, idn=None):
                return nc.tensor.transpose(dst, src, (ident if idn is None else idn)[0:n, 0:n])

            pe.wait_ge(w_small, 48)
            pe.wait_ge(w_m, 64)
            for bk, l, r in ((1, mw_q, mw_k), (2, mw_v, mw_o)):
                for c in range(C):
                    for i in range(IT):
                        last = mm(bank[bk][:, c * D:(c + 1) * D], l[:, i, c * P:(c + 1) * P], r[:, i, :],
                                  start=(i == 0), stop=(i == IT - 1))
                last.then_inc(m_psum, 1)
            pe.wait_ge(m_made, 2)
            pe.wait_ge(consts_made, 1)

            with pe.Fori(0, B) as b:
                def at(s, per, k):
                    pe.wait_ge(s, b * per + (k + 1))

                def normed_T(s):
                    at(xn_ready, LNS, s)
                    for c in range(C):
                        last = tr(view(0, P, c * T, T), xn[:, c * P:(c + 1) * P], T)
                    last.then_inc(xt_psum, 1)

                def kv(n):
                    bk = 6 + n % 2
                    if n >= 2:
                        at(kv_ready, NKV, n - 2)
                    for c in range(C):
                        if n < IT:
                            last = mm(bank[bk][:, 0:S], x_wkv[:, c, n * P:(n + 1) * P], ctxnT[:, c, :],
                                      start=(c == 0), stop=(c == C - 1))
                        else:
                            j, half = (n - IT) // 2, (n - IT) % 2
                            lo = INNER + half * 512
                            last = mm(bank[bk][0:KP, :], ctxnT[:, c, j * KP:(j + 1) * KP], x_wkv[:, c, lo:lo + 512],
                                      start=(c == 0), stop=(c == C - 1))
                    last.then_inc(kv_psum, 1)

                pe.wait_ge(w_ret, 64)
                normed_T(0)
                at(ctxn_ready, 1, 0)
                for c in range(C):
                    for j in range(KTILES):
                        last = tr(bank[4 + c][:, j * KP:(j + 1) * KP], ctxn[:, j, c * P:(c + 1) * P], KP)
                    last.then_inc(ctxt_psum, 1)
                at(xt_ready, LNS, 0)
                for i in (1, 0):
                    for m in range(C):
                        for c in range(C):
                            last = mm(view(1, P, (i * C + m) * T, T), ret_w[:, i, c, m * P:(m + 1) * P], xnT[:, c, :],
                                      start=(c == 0), stop=(c == C - 1))
                last.then_inc(ret_qv, 1)
                for c in range(C):
                    last = mm(view(2, T, 0, D), xnT[:, c, :], ret_w[:, 2, c, :], start=(c == 0), stop=(c == C - 1))
                last.then_inc(ret_g, 1)
                pe.wait_ge(w_x, 16)
                at(ctxt_ready, C, C - 1)
                for n in range(0, 3):
                    kv(n)
                at(ret_y, 1, 0)
                for c in range(C):
                    last = tr(view(3, T, c * P, P), yT[:, c, :], P)
                last.then_inc(ret_yt, 1)
                for n in range(3, 8):
                    kv(n)
                at(ret_y2, 1, 0)
                for c in range(C):
                    last = tr(view(0, P, c * T, T), y2[:, c * P:(c + 1) * P], T)
                last.then_inc(ret_y2t_psum, 1)
                kv(8)
                at(ret_y2t, 1, 0)
                for c in range(C):
                    last = mm(view(1, T, 0, D), y2T[:, c, :], ret_w[:, 3, c, :], start=(c == 0), stop=(c == C - 1))
                last.then_inc(sub_out, 1)
                for n in range(9, NKV):
                    kv(n)

                normed_T(1)
                at(xt_ready, LNS, 1)
                pe.wait_ge(wx_loaded, b * 32 + 32)
                for m in range(IT):
                    for c in range(C):
                        last = mm(view(1 + m // 4, P, (m % 4) * T, T), x_wq[:, c, m * P:(m + 1) * P], xnT[:, c, :],
                                  start=(c == 0), stop=(c == C - 1))
                    if m % 4 == 3:
                        last.then_inc(xq_psum, 1)
                at(kv_ready, NKV, NKV - 1)
                for i in range(XH + 2):
                    if i < XH:
                        if i % 8 == 0:
                            at(xq_ready, 2, i // 8)
                        if i >= 2:
                            at(xs_exp, XH, i - 2)
                        lo = XD * (i % 2)
                        for j in range(KTILES):
                            last = mm(view(3 + i % 2, KP, j * T, T), x_kT[lo:lo + XD, i // 2, j * KP:(j + 1) * KP],
                                      x_qT[lo:lo + XD, i // 2, :], start=True, stop=True)
                        last.then_inc(xs_psum, 1)
                    if i >= 2:
                        h = i - 2
                        at(xs_clip, XH, h)
                        if h % 4 == 0 and h >= 8:
                            at(xo_ready, 4, h // 4 - 2)
                        for j in range(KTILES):
                            last = mm(view(5 + (h // 4) % 2, T, (h % 4) * (XD + 1), XD + 1), x_p[:, h % 3, j, :],
                                      x_v[:, j, h, :], start=(j == 0), stop=(j == KTILES - 1))
                        last.then_inc(xs_pv, 1)
                for i in range(IT):
                    if i % 4 == 0:
                        at(xo_ready, 4, i // 2 + 1)
                    last = tr(view(1 + i // 4, P, (i % 4) * T, T), x_o[:, i * P:(i + 1) * P], T)
                    if i % 4 == 3:
                        last.then_inc(xot_psum, 1)
                for i in range(IT):
                    if i % 4 == 0:
                        at(xot_ready, 2, i // 4)
                    last = mm(view(0, T, 0, D), x_oT[:, i, :], x_wo[:, i, :], start=(i == 0), stop=(i == IT - 1))
                last.then_inc(sub_out, 1)

                normed_T(2)
                at(xt_ready, LNS, 2)
                pe.wait_ge(w_e, 112)
                for c in range(C):
                    last = mm(view(1, T, 0, R1), xnT[:, c, :], r_w1[:, c, :], start=(c == 0), stop=(c == C - 1))
                last.then_inc(r_h, 1)

                def project_qk(e):
                    for w, lo in ((e_wq, 0), (e_wk, C * T)):
                        for m in range(C):
                            for c in range(C):
                                last = mm(view(5, P, lo + m * T, T), w[:, e, c, m * P:(m + 1) * P], xnT[:, c, :],
                                          start=(c == 0), stop=(c == C - 1))
                    last.then_inc(eqk_psum, 1)

                def maxima_T(e):
                    at(es_max, 4 * NE, 4 * e + 3)
                    if e:
                        at(eo_ready, NE, e - 1)
                    nc.tensor.transpose(bank[7][:, 288:288 + T // 2].bitcast(BF16),
                                        e_max[:, :, :].rearrange("p g r -> p (g r)"), ident_b[0:T, 0:T]
                                        ).then_inc(emt_psum, 1)

                def project_v(e):
                    if e:
                        at(ev_ready, NE, e - 1)
                    if e >= 3:
                        at(eot_ready, NE, e - 3)
                    for c in range(C):
                        last = mm(view(6, T, 0, D), xnT[:, c, :], e_wv[:, e, c, :], start=(c == 0), stop=(c == C - 1))
                    if e < 2:
                        last.then_inc(evo_psum, 1)

                def max_scores(e, g):
                    if g == 0:
                        at(eq_ready, NE, e)
                        at(ek_ready, NE, e)
                    if 4 * e + g >= 2:
                        at(es_max, 4 * NE, 4 * e + g - 2)
                    s = slice(32 * g, 32 * g + 32)
                    for m in range(C):
                        for o in range(2):
                            last = mm(view(1 + g % 2, T, (2 * m + o) * T, T), e_qb[s, m, o, :], e_kb[s, m, :],
                                      start=True, stop=True)
                    last.then_inc(es_psum, 1)

                def scores_T(e, g):
                    if 4 * e + g >= 2:
                        at(est_exp, 4 * NE, 4 * e + g - 2)
                    s = slice(32 * g, 32 * g + 32)
                    for m in range(C):
                        mm(view(3 + g % 2, T, 2 * m * T, 2 * T), e_k[s, e % 2, m, :],
                           e_q[s, e % 2, m, :, :].rearrange("p o t -> p (o t)"), start=True, stop=True,
                           skip_group_check=True)
                        if g == 0 and m == 0:
                            at(emt_ready, NE, e)
                        for o in range(2):
                            last = mm(view(3 + g % 2, T, (2 * m + o) * T, T), sel_b[s, 2 * m + o, :], e_maxT[s, :],
                                      start=False, stop=True, skip_group_check=True)
                    last.then_inc(est_psum, 1)

                def probs_v(e, g):
                    if g == 0:
                        at(ev_ready, NE, e)
                        if e:
                            at(eo_ready, NE, e - 1)
                    at(est_exp, 4 * NE, 4 * e + g)
                    for r in range(4):
                        h = 8 * (r // 2) + 2 * g + r % 2
                        last = mm(view(7, T, h * (ED + 1), ED + 1), e_p[:, g % 2, r, :], e_v[:, e % 2, h, :],
                                  start=True, stop=True)
                    last.then_inc(epv, 1)

                def out_T(e):
                    at(eo_ready, NE, e)
                    if e >= NE - 2:
                        at(eot_ready, NE, e - 1)
                    if e == NE - 2:
                        at(ev_ready, NE, NE - 1)
                    for c in range(C):
                        last = tr(view(6, P, D + c * T, T), e_o[:, 8 * c:8 * c + 8, :].rearrange("p h d -> p (h d)"), T)
                    last.then_inc(evo_psum, 1)

                def out_sum(e):
                    at(eot_ready, NE, e)
                    for c in range(C):
                        mm(view(0, T, 0, D), e_oT[:, c, :], e_wo[:, e, c, :], start=(e == 0 and c == 0), stop=False)

                for s in range(NE + 2):
                    if s < NE:
                        project_qk(s)
                    if 1 <= s <= NE:
                        maxima_T(s - 1)
                    if s < NE:
                        project_v(s)
                    if s >= 2:
                        out_T(s - 2)
                    if s == 0:
                        at(r_hn, 1, 0)
                        tr(view(2, P, 0, T), h1[:, :], T).then_inc(r_ht_psum, 1)
                        at(r_ht, 1, 0)
                        mm(view(1, T, R1, NE), h1T[:, :], r_w2[:, :], start=True, stop=True).then_inc(r_lg, 1)
                        at(r_nm, 1, 0)
                    for g in range(5):
                        if g < 4 and 1 <= s <= NE:
                            scores_T(s - 1, g)
                        if g >= 1 and s < NE:
                            max_scores(s, g - 1)
                        if g >= 1 and 1 <= s <= NE:
                            probs_v(s - 1, g - 1)
                        if g == 1 and s >= 2:
                            out_sum(s - 2)
                    if s == 0:
                        at(r_gates, 1, 0)
                        tr(view(3, NE, 0, T), gates[:, :], T).then_inc(r_gt_psum, 1)
                        at(r_gt, 1, 0)
                mm(view(0, T, 0, D), gatesT[:, :], e_bo[:, :], start=False, stop=True).then_inc(sub_out, 1)

                normed_T(3)
                at(xt_ready, LNS, 3)
                pe.wait_ge(w_l, 32)
                for i in range(2):
                    for m in range(C):
                        for c in range(C):
                            last = mm(view(1, P, (i * C + m) * T, T), l_w[:, i, c, m * P:(m + 1) * P], xnT[:, c, :],
                                      start=(c == 0), stop=(c == C - 1))
                last.then_inc(l_psum, 1)
                pe.wait_ge(raw_loaded, 16 * b + 16)
                for j in range(KTILES):
                    for c in range(C):
                        last = mm(view(5 + j // 2, KP, (j % 2) * D, D), ctx_raw[:, c, j * KP:(j + 1) * KP],
                                  m_vo[:, c, :], start=(c == 0), stop=(c == C - 1))
                    if j:
                        last.then_inc(z_psum, 1)
                at(l_tanh, C, C - 1)
                for k in range(LK):
                    for m in range(C):
                        last = mm(view(2, T, LK - 1 - k, 1), l_t[:, m, k, :], col("v", m),
                                  start=(m == 0), stop=(m == C - 1))
                last.then_inc(l_score, 1)
                at(l_band, 1, 0)
                tr(view(3, T, 0, T), l_a[:, :], T).then_inc(l_at_psum, 1)
                at(l_at, 1, 0)
                mm(view(4, T, 0, D), l_aT[:, :], xn[:, :], start=True, stop=True).then_inc(sub_out, 1)

                normed_T(4)
                at(xt_ready, LNS, 4)
                for m in range(C):
                    for c in range(C):
                        last = mm(view(1, P, m * T, T), m_qk[:, c, m * P:(m + 1) * P], xnT[:, c, :],
                                  start=(c == 0), stop=(c == C - 1))
                last.then_inc(g_psum, 1)
                at(g_ready, 1, 0)
                for j in range(KTILES):
                    for c in range(C):
                        last = mm(view(2, KP, j * T, T), ctx_raw[:, c, j * KP:(j + 1) * KP], m_g[:, c, :],
                                  start=(c == 0), stop=(c == C - 1))
                last.then_inc(ms_psum, 1)
                at(z_ready, 2, 1)
                at(ms_e, 1, 0)
                for j in range(KTILES):
                    last = mm(view(3, T, 0, D), m_e[:, j, :], m_z[:, j, :], start=(j == 0), stop=(j == KTILES - 1))
                last.then_inc(sub_out, 1)

                normed_T(5)
                at(xt_ready, LNS, 5)
                pe.wait_ge(w_c, 48)
                for c in range(C):
                    last = mm(view(1, NE, 0, T), c_wr[:, c, :], xnT[:, c, :], start=(c == 0), stop=(c == C - 1))
                last.then_inc(c_lg, 1)
                at(c_dg, 1, 0)
                mm(view(2, T, 0, T), ones8[:, :],
                   c_diag[:, 0].rearrange("p e j -> p (e j)"), start=True, stop=True)
                mm(view(2, T, T, 1), c_diag[:, 1].rearrange("p e j -> p (e j)"), ones8[:, 0:1],
                   start=True, stop=True).then_inc(c_rpsum, 1)
                at(c_hots, 1, 0)
                for c in range(C):
                    mm(view(3, P, c * T, T), xn[:, c * P:(c + 1) * P], c_hot[:, :], start=True, stop=True)
                for i in range(2):
                    lo = CONST["rope"][0] + i * ROT
                    mm(view(4, ROT, i * T, T), const[0:T, lo:lo + ROT], c_hot[:, :], start=True, stop=True)
                mm(view(2, T, T + 1, 1), c_hot[:, :], col("iota", 0, 0, T), start=True, stop=True)
                tr(view(5, T, 0, T), c_hot[:, :], T).then_inc(c_gpsum, 1)
                at(c_xg, 1, 0)
                pe.wait_ge(wc_loaded, b * 16 + 16)
                for part in range(3):
                    for e in range(NE):
                        for c in range(C):
                            w = c_wqk[:, part * NE + e, c, :] if part < 2 else c_wv[:, e, c, :]
                            last = mm(view(6 + part // 2, P, part % 2 * T + e * TK, TK), w,
                                      c_xgT[:, c, e * TK:(e + 1) * TK], start=(c == 0), stop=(c == C - 1))
                last.then_inc(c_qkv, 1)
                at(c_vt_ready, 1, 0)
                tr(view(0, T, 0, HP), c_vT[:, :], P).then_inc(c_vpsum, 1)
                at(c_qk_ready, 1, 0)
                mm(view(1, T, T, T), c_qk[:, 0, :], c_qk[:, 1, :], start=True, stop=True).then_inc(c_spsum, 1)
                at(c_en2, 1, 0)
                tr(view(2, T, 128, T), c_e[:, :], T).then_inc(c_etp, 1)
                at(c_et, 1, 0)
                at(c_v_ready, 1, 0)
                mm(view(3, P, 0, T), c_v[:, :], c_eT[:, :], start=True, stop=True).then_inc(c_avp, 1)
                at(c_av, 1, 0)
                for m in range(C):
                    for e in range(NE):
                        last = mm(view(4, P, m * T + e * TK, TK), c_wo[:, e, m * P:(m + 1) * P],
                                  c_avT[:, e * TK:(e + 1) * TK], start=True, stop=True)
                last.then_inc(c_xpp, 1)
                at(c_xps, 1, 0)
                for m in range(C):
                    last = tr(view(5, T, m * P, P), c_xpT[:, m, :], P)
                last.then_inc(c_xqp, 1)
                at(c_xqs, 1, 0)
                mm(view(6, T, 0, D), c_hotT[:, :], c_xp[:, :], start=True, stop=True).then_inc(sub_out, 1)

        @block.scalar
        def _(act):
            af = nc.scalar.activation
            act.wait_ge(w_small, 48)
            with act.Fori(0, B) as b:
                def at(s, per, k):
                    act.wait_ge(s, b * per + (k + 1))

                for c in range(C):
                    at(ctxt_psum, C, c)
                    af(ctxnT[:, c, :], bank[4 + c][:, 0:S], ACT.Identity, bias=col("ctx_b", c),
                       scale=col("ctx_w", c)).then_inc(ctxt_ready, 1)
                at(ret_g, 1, 0)
                af(eg[:, :], view(2, T, 0, D), ACT.Exp, scale=-1.0).then_inc(ret_eg, 1)
                act.wait_ge(consts_made, 1)
                for n in range(NKV):
                    at(kv_psum, NKV, n)
                    bk = 6 + n % 2
                    if n < IT:
                        ins = af(x_kT[:, n, :], bank[bk][:, 0:S], ACT.Copy)
                    else:
                        j, half = (n - IT) // 2, (n - IT) % 2
                        ins = af(x_v[:, j, half * 8:half * 8 + 8, 0:XD], view(bk, KP, 0, 8, XD), ACT.Copy)
                    ins.then_inc(kv_ready, 1)

                for i in range(2):
                    at(xq_psum, 2, i)
                    af(x_qT[:, 4 * i:4 * i + 4, :], view(1 + i, P, 0, 4, T), ACT.Copy).then_inc(xq_ready, 1)
                for h in range(XH):
                    at(xs_psum, XH, h)
                    if h >= 3:
                        at(xs_pv, XH, h - 3)
                    af(x_p[:, h % 3], view(3 + h % 2, KP, 0, KTILES, T), ACT.Exp, scale=XD ** -0.5
                       ).then_inc(xs_exp, 1)
                for i in range(2):
                    at(xot_psum, 2, i)
                    af(x_oT[:, 4 * i:4 * i + 4, :], view(1 + i, P, 0, 4, T), ACT.Copy).then_inc(xot_ready, 1)

                for s in range(NE + 2):
                    if s < NE:
                        at(eqk_psum, NE, s)
                        at(eq_ready, NE, s)
                        for m in range(C):
                            af(e_k[:, s % 2, m, :], view(5, P, (C + m) * T, T), ACT.Identity,
                               bias=col("kb", s * C + m))
                            ins = af(e_kb[:, m, :], view(5, P, (C + m) * T, T), ACT.Identity,
                                     bias=col("kb", s * C + m))
                        ins.then_inc(ek_ready, 1)
                    if s >= 2:
                        at(evo_psum, NE + 2, s)
                        if s < NE:
                            at(ev_ready, NE, s)
                        af(e_oT[:, :, :], view(6, P, D, C, T), ACT.Copy).then_inc(eot_ready, 1)
                    if s == 0:
                        at(r_nm, 1, 0)
                        af(pr[:, :], lg[:, :], ACT.Exp, bias=sc1[0:T, 0:1], accum_out=sc1[0:T, 1:2]
                           ).then_inc(r_exp, 1)
                    if 1 <= s <= NE:
                        for g in range(4):
                            n = 4 * (s - 1) + g
                            at(est_psum, 4 * NE, n)
                            if n >= 2:
                                at(epv, 4 * NE, n - 2)
                            af(e_p[:, g % 2], view(3 + g % 2, T, 0, 4, T), ACT.Exp, scale=ED ** -0.5
                               ).then_inc(est_exp, 1)

                for i, (lo, n) in enumerate(((0, 2), (2, 1))):
                    at(z_psum, 2, i)
                    af(m_z[:, lo:lo + n, :], view(5 + i, KP, 0, n, D), ACT.Copy).then_inc(z_ready, 1)
                for m in range(C):
                    at(l_sum, C, m)
                    af(l_t[:, m], l_t[:, m], ACT.Tanh).then_inc(l_tanh, 1)
                at(l_nm, 1, 0)
                af(l_w16[:, :], view(2, T, 0, LK), ACT.Exp, bias=sc1[0:T, 2:3], accum_out=sc1[0:T, 3:4]
                   ).then_inc(l_exp, 1)

                at(ms_nm, 1, 0)
                for j in range(KTILES):
                    af(m_e[:, j, :], view(2, KP, j * T, T), ACT.Exp, bias=m_nm[:, j:j + 1], scale=XD ** -0.5,
                       accum_out=m_sum[:, j:j + 1]).then_inc(ms_exp, 1)

                at(c_lg, 1, 0)
                af(c_s[:, :], view(1, NE, 0, T), ACT.Exp, scale=-1.0).then_inc(c_en, 1)
                at(c_gpsum, 1, 0)
                af(c_xgT[:, :, :], view(3, P, 0, C, T), ACT.Copy).then_inc(c_xg, 1)
                at(c_qkv, 1, 0)
                af(c_vT[:, :], view(7, P, 0, T), ACT.Copy).then_inc(c_vt_ready, 1)
                at(c_vpsum, 1, 0)
                af(c_v[:, :], view(0, T, 0, HP), ACT.Copy).then_inc(c_v_ready, 1)
                at(c_nm, 1, 0)
                af(c_e[:, :], c_pen[:, :], ACT.Exp, bias=sc1[0:T, 4:5], scale=HP ** -0.5,
                   accum_out=sc1[0:T, 5:6]).then_inc(c_exp, 1)

        @block.vector
        def _(dve):
            v = nc.vector
            dve.wait_ge(w_small, 48)
            v.tensor_copy(ident_b[:, :], ident)
            v.tensor_copy(sel_b[:, :, :], cst("sel").rearrange("p (r t) -> p r t", r=4))
            v.memset(e_max[:, :, :], 0.0)
            v.memset(l_proj[:, :, :], 0.0)
            v.memset(e_v[:, :, :, ED:ED + 1], 1.0)
            v.memset(x_v[:, :, :, XD:XD + 1], 1.0)
            v.memset(ones8[:, :], 1.0).then_inc(consts_made, 1)
            for i, m in enumerate((m_qk, m_vo)):
                dve.wait_ge(m_psum, i + 1)
                v.tensor_copy(m[:, :, :], bank[1 + i][:, :].rearrange("p (c n) -> p c n", c=C)).then_inc(m_made, 1)
            dve.wait_ge(consts_made, 1)

            with dve.Fori(0, B) as b:
                count = [0]

                def at(s, per, k):
                    dve.wait_ge(s, b * per + (k + 1))

                def alone():
                    v.memset(idle[:, :], 0.0)

                def link(ins):
                    count[0] += 1
                    ins.then_inc(dve_done, 1)
                    dve.wait_ge(dve_done, b * DVE_STEPS + count[0])

                norms = [0]

                def normalise_each(pairs, n):
                    k = len(pairs)
                    for j, (_, src) in enumerate(pairs):
                        ins = v.bn_stats(stats[0:n, j, :], src)
                    link(ins)
                    alone()
                    for j in range(k):
                        ins = v.bn_aggr(mv[0:n, j, :], stats[0:n, j, :])
                    link(ins)
                    v.tensor_scalar(var[0:n, 0:k], mv[0:n, 0:k, 1], EPS, None, ALU.add).then_inc(var_ready, 1)
                    at(rstd_ready, NORMS, norms[0])
                    norms[0] += 1
                    for j, (dst, src) in enumerate(pairs):
                        ins = v.tensor_scalar(dst, src, mv[0:n, j, 0:1], rstd[0:n, j:j + 1], ALU.subtract, ALU.mult)
                    return ins

                def normalise(dst, src, n):
                    return normalise_each([(dst, src)], n)

                def xT_copy(s):
                    at(xt_psum, LNS, s)
                    v.tensor_copy(xnT[:, :, :], view(0, P, 0, C, T)).then_inc(xt_ready, 1)

                def add_to_x(s, bk, src=None):
                    at(sub_out, LNS, s)
                    v.tensor_tensor((x_out if s == LNS - 1 else x)[:, :], (x if src is None else src)[:, :],
                                    view(bk, T, 0, D), ALU.add).then_inc(x_done, 1)
                    at(x_done, LNS, s)

                dve.wait_ge(x_loaded, 16 * b + 16)
                normalise(xn[:, :], x_in[:, :], T).then_inc(xn_ready, 1)
                dve.wait_ge(ctx_loaded, 16 * b + 16)
                normalise_each([(ctxn[:, j, :], ctx_tok[:, j, :]) for j in range(KTILES)], KP
                               ).then_inc(ctxn_ready, 1)
                xT_copy(0)
                at(ret_qv, 1, 0)
                for m in range(C):
                    link(v.tensor_tensor_scan(state[:, m, :], col("lam", m).to_broadcast([P, T]),
                                              view(1, P, (C + m) * T, T), 0.0, ALU.mult, ALU.add))
                v.tensor_tensor(yT[:, :, :], state[:, :, :], view(1, P, 0, C, T), ALU.mult).then_inc(ret_y, 1)
                at(ret_eg, 1, 0)
                link(v.tensor_scalar(eg[:, :], eg[:, :], 1.0, None, ALU.add))
                link(v.reciprocal(eg[:, :], eg[:, :]))
                link(v.tensor_tensor(gate[:, :], eg[:, :], view(2, T, 0, D), ALU.mult))
                at(ret_yt, 1, 0)
                link(normalise(y2[:, :], view(3, T, 0, D), T))
                link(v.tensor_tensor(y2[:, :], y2[:, :], row("ret_g"), ALU.mult))
                link(v.tensor_tensor(y2[:, :], y2[:, :], row("ret_b"), ALU.add))
                v.tensor_tensor(y2[:, :], y2[:, :], gate[:, :], ALU.mult).then_inc(ret_y2, 1)
                at(ret_y2t_psum, 1, 0)
                v.tensor_copy(y2T[:, :, :], view(0, P, 0, C, T)).then_inc(ret_y2t, 1)
                add_to_x(0, 1, x_in)

                link(normalise(y2[:, :], x[:, :], T))
                normalise(xn[:, :], y2[:, :], T).then_inc(xn_ready, 1)
                at(xt_psum, LNS, 1)
                link(v.tensor_scalar(xnT[:, 0, :], view(0, P, 0, T), col("lat_w", 0), col("lat_b", 0),
                                     ALU.mult, ALU.add))
                v.tensor_scalar(xnT[:, 1, :], view(0, P, T, T), col("lat_w", 1), col("lat_b", 1),
                                ALU.mult, ALU.add).then_inc(xt_ready, 1)

                def x_norm(g):
                    at(xs_pv, XH, 4 * g + 3)
                    o = view(5 + g % 2, T, 0, 4, XD + 1)
                    link(v.reciprocal(x_rc[:, :, :], o[:, :, XD:XD + 1]))
                    v.tensor_tensor(x_o[:, g * 4 * XD:(g + 1) * 4 * XD].rearrange("p (h d) -> p h d", h=4),
                                    o[:, :, 0:XD], x_rc[:, :, :].to_broadcast([T, 4, XD]), ALU.mult
                                    ).then_inc(xo_ready, 1)

                for h in range(XH):
                    at(xs_exp, XH, h)
                    v.tensor_scalar(x_p[:, h % 3], x_p[:, h % 3], float(np.exp(CLIP)), float(np.exp(-CLIP)),
                                    ALU.min, ALU.max).then_inc(xs_clip, 1)
                    if h % 4 == 1 and h > 4:
                        x_norm(h // 4 - 1)
                x_norm(3)
                at(sub_out, LNS, 1)
                link(v.tensor_tensor(x[:, :], x[:, :], row("bo"), ALU.add))
                add_to_x(1, 0)

                normalise(xn[:, :], x[:, :], T).then_inc(xn_ready, 1)
                xT_copy(2)
                at(r_h, 1, 0)
                link(v.tensor_tensor(h1[:, :], view(1, T, 0, R1), row("rb1"), ALU.add))
                link(normalise(h1[:, :], h1[:, :], T))
                link(v.tensor_tensor(h1[:, :], h1[:, :], row("ffn_g"), ALU.mult))
                link(v.tensor_tensor(h1[:, :], h1[:, :], row("ffn_b"), ALU.add))
                v.tensor_scalar(h1[:, :], h1[:, :], 0.0, None, ALU.max).then_inc(r_hn, 1)
                at(r_ht_psum, 1, 0)
                v.tensor_copy(h1T[:, :], view(2, P, 0, T)).then_inc(r_ht, 1)
                at(r_lg, 1, 0)
                link(v.tensor_tensor(lg[:, :], view(1, T, R1, NE), row("rb2"), ALU.add))
                v.tensor_reduce(sc1[0:T, 0:1], lg[:, :], AX.X, ALU.max, negate=True).then_inc(r_nm, 1)

                def q_v(e):
                    at(eqk_psum, NE, e)
                    for m in range(C):
                        for o, keep in enumerate(("even", "odd")):
                            ins = v.tensor_scalar(e_q[:, e % 2, m, o, :], view(5, P, m * T, T), col("qb", e * C + m),
                                                  col(keep), ALU.add, ALU.mult)
                    link(ins)
                    v.tensor_copy(e_qb[:, :, :, :], e_q[:, e % 2]).then_inc(eq_ready, 1)
                    at(evo_psum, NE + 2, e)
                    v.tensor_tensor(e_v[:, e % 2, :, 0:ED], view(6, T, 0, EH, ED),
                                    row("vb", T, e * D, D).rearrange("p (h d) -> p h d", h=EH), ALU.add
                                    ).then_inc(ev_ready, 1)

                def router():
                    at(r_exp, 1, 0)
                    link(v.reciprocal(sc1[0:T, 1:2], sc1[0:T, 1:2]))
                    link(v.tensor_scalar(pr[:, :], pr[:, :], sc1[0:T, 1:2], None, ALU.mult))
                    alone()
                    link(v.max(top[:, :], pr[:, :]))
                    alone()
                    link(v.max_index(topi[:, :], top[:, :], pr[:, :]))
                    link(v.tensor_copy(topf[:, :], topi[:, :]))
                    link(v.tensor_tensor(sc1[0:T, 6:7], top[:, 0:1], top[:, 1:2], ALU.add))
                    link(v.reciprocal(sc1[0:T, 6:7], sc1[0:T, 6:7]))
                    link(v.tensor_scalar(top[:, 0:2], top[:, 0:2], sc1[0:T, 6:7], None, ALU.mult))
                    for r in range(2):
                        link(v.tensor_scalar(g01[:, r, :], const[0:T, CONST["iota8"][0]:CONST["iota8"][1]],
                                             topf[:, r:r + 1], top[:, r:r + 1], ALU.is_equal, ALU.mult))
                    v.tensor_tensor(gates[:, :], g01[:, 0, :], g01[:, 1, :], ALU.add).then_inc(r_gates, 1)
                    at(r_gt_psum, 1, 0)
                    v.tensor_copy(gatesT[:, :], view(3, NE, 0, T)).then_inc(r_gt, 1)

                def e_norm(e):
                    at(epv, 4 * NE, 4 * e + 3)
                    o = view(7, T, 0, EH, ED + 1)
                    link(v.reciprocal(e_rc[:, :, :], o[:, :, ED:ED + 1]))
                    link(v.tensor_scalar(e_rc[:, :, :], e_rc[:, :, :], gates[:, e:e + 1], None, ALU.mult))
                    v.tensor_tensor(e_o[:, :, :], o[:, :, 0:ED], e_rc[:, :, :].to_broadcast([T, EH, ED]), ALU.mult
                                    ).then_inc(eo_ready, 1)

                for s in range(NE + 2):
                    if s >= 2:
                        e_norm(s - 2)
                    if 1 <= s <= NE:
                        at(emt_psum, NE, s - 1)
                        v.tensor_copy(e_maxT[:, :], bank[7][:, 288:288 + T // 2].bitcast(BF16)).then_inc(emt_ready, 1)
                    if s < NE:
                        q_v(s)
                        for g in range(4):
                            at(es_psum, 4 * NE, 4 * s + g)
                            v.tensor_reduce(e_max[:, g, 0:4], view(1 + g % 2, T, 0, 4, T), AX.X, ALU.max
                                            ).then_inc(es_max, 1)
                    if s == 0:
                        router()
                add_to_x(2, 0)

                normalise(xn[:, :], x[:, :], T).then_inc(xn_ready, 1)
                xT_copy(3)
                at(l_psum, 1, 0)
                v.tensor_copy(l_q[:, :, :], view(1, P, 0, C, T))
                link(v.tensor_copy(l_proj[:, :, LPAD:LPAD + T], view(1, P, C * T, C, T)))
                for m in range(C):
                    v.tensor_tensor(l_t[:, m], windows(l_proj[:, m, :], (1, LK), (1, T)),
                                    windows(l_q[:, m, :], (0, LK), (1, T)), ALU.add).then_inc(l_sum, 1)
                at(l_score, 1, 0)
                v.tensor_reduce(sc1[0:T, 2:3], view(2, T, 0, LK), AX.X, ALU.max, negate=True).then_inc(l_nm, 1)
                at(l_exp, 1, 0)
                link(v.reciprocal(sc1[0:T, 3:4], sc1[0:T, 3:4]))
                link(v.tensor_scalar(l_w16[:, :], l_w16[:, :], sc1[0:T, 3:4], None, ALU.mult))
                spread = l_t[0:T, 0].rearrange("p k t -> p (k t)").rearrange("p (t k) -> p t k", k=LK)
                link(v.tensor_tensor(spread, windows(const[0:T, CONST["band"][0]:CONST["band"][1]], (1, T), (1, LK)),
                                     windows(l_w16[:, :], (0, T), (1, LK)), ALU.mult))
                v.tensor_reduce(l_a[:, :], spread, AX.X, ALU.add).then_inc(l_band, 1)
                at(l_at_psum, 1, 0)
                v.tensor_copy(l_aT[:, :], view(3, T, 0, T)).then_inc(l_at, 1)
                add_to_x(3, 4)

                normalise(xn[:, :], x[:, :], T).then_inc(xn_ready, 1)
                xT_copy(4)
                at(g_psum, 1, 0)
                v.tensor_copy(m_g[:, :, :], view(1, P, 0, C, T)).then_inc(g_ready, 1)
                at(ms_psum, 1, 0)
                link(v.tensor_reduce(m_nm[:, :], view(2, KP, 0, KTILES, T), AX.X, ALU.max, negate=True))
                v.tensor_scalar(m_nm[:, :], m_nm[:, :], XD ** -0.5, None, ALU.mult).then_inc(ms_nm, 1)
                at(ms_exp, KTILES, KTILES - 1)
                link(v.reciprocal(m_sum[:, :], m_sum[:, :]))
                v.tensor_tensor(m_e[:, :, :], m_e[:, :, :], windows(m_sum[:, :], (1, KTILES), (0, T)), ALU.mult
                                ).then_inc(ms_e, 1)
                add_to_x(4, 3)

                normalise(xn[:, :], x[:, :], T).then_inc(xn_ready, 1)
                xT_copy(5)
                at(c_en, 1, 0)
                link(v.tensor_scalar(c_s[:, :], c_s[:, :], 1.0, None, ALU.add))
                link(v.reciprocal(c_s[:, :], c_s[:, :]))
                alone()
                link(v.max(c_top[:, 0:8], c_s[:, :]))
                alone()
                link(v.max_index(c_idx[:, 0:8], c_top[:, 0:8], c_s[:, :]))
                alone()
                link(v.match_replace(c_s2[:, :], c_top[:, 0:8], c_s[:, :], -1.0))
                alone()
                link(v.max(c_top[:, 8:16], c_s2[:, :]))
                alone()
                link(v.max_index(c_idx[:, 8:16], c_top[:, 8:16], c_s2[:, :]))
                link(v.tensor_copy(c_idxf[:, :], c_idx[:, :]))
                own = const[0:NE, CONST["own"][0]:CONST["own"][1]].rearrange("p (e j) -> p e j", e=NE)
                v.tensor_tensor(c_diag[:, 0], own, windows(c_idxf[:, 0:TK], (0, NE), (1, TK)), ALU.mult)
                v.tensor_tensor(c_diag[:, 1], own, windows(c_top[:, 0:TK], (0, NE), (1, TK)), ALU.mult
                                ).then_inc(c_dg, 1)
                at(c_rpsum, 1, 0)
                link(v.tensor_copy(c_pos[:, :], view(2, T, 0, T)))
                v.tensor_scalar(c_hot[:, :], c_pos[:, :], col("iota", 0, 0, T), None, ALU.is_equal
                                ).then_inc(c_hots, 1)
                at(c_gpsum, 1, 0)
                v.tensor_copy(c_hotT[:, :], view(5, T, 0, T))
                v.tensor_copy(c_cs[:, :, :], view(4, ROT, 0, 2, T))
                link(v.tensor_copy(c_iv[:, :], view(2, T, T, 2)))
                link(v.tensor_scalar(c_pen[:, :], c_pos[:, :], c_iv[:, 1:2], None, ALU.is_le))
                link(v.tensor_tensor(c_pen[:, :], c_pen[:, :], const[0:T, CONST["block"][0]:CONST["block"][1]], ALU.mult))
                link(v.tensor_scalar(c_pen[:, :], c_pen[:, :], 1e30, -1e30, ALU.mult, ALU.add))
                at(c_qkv, 1, 0)
                link(v.tensor_copy(c_qk[:, :, :], view(6, P, 0, 2, T)))
                half = ROT // 2
                for lo, to in ((0, half), (half, 0)):
                    link(v.tensor_tensor(c_rot[to:to + half], c_qk[lo:lo + half],
                                         windows(c_cs[lo:lo + half, 1, :], (0, 2), (1, T)), ALU.mult))
                link(v.tensor_tensor(c_qk[0:ROT], c_qk[0:ROT], windows(c_cs[:, 0, :], (0, 2), (1, T)), ALU.mult))
                v.tensor_tensor(c_qk[0:ROT], c_qk[0:ROT], c_rot[:, :, :], ALU.add).then_inc(c_qk_ready, 1)
                at(c_spsum, 1, 0)
                link(v.tensor_tensor(c_pen[:, :], c_pen[:, :], view(1, T, T, T), ALU.add))
                link(v.tensor_reduce(sc1[0:T, 4:5], c_pen[:, :], AX.X, ALU.max, negate=True))
                v.tensor_scalar(sc1[0:T, 4:5], sc1[0:T, 4:5], HP ** -0.5, None, ALU.mult).then_inc(c_nm, 1)
                at(c_exp, 1, 0)
                link(v.reciprocal(sc1[0:T, 5:6], sc1[0:T, 5:6]))
                v.tensor_scalar(c_e[:, :], c_e[:, :], sc1[0:T, 5:6], c_iv[:, 0:1], ALU.mult, ALU.mult
                                ).then_inc(c_en2, 1)
                at(c_etp, 1, 0)
                v.tensor_copy(c_eT[:, :], view(2, T, 128, T)).then_inc(c_et, 1)
                at(c_avp, 1, 0)
                v.tensor_copy(c_avT[:, :], view(3, P, 0, T)).then_inc(c_av, 1)
                at(c_xpp, 1, 0)
                v.tensor_copy(c_xpT[:, :, :], view(4, P, 0, C, T)).then_inc(c_xps, 1)
                at(c_xqp, 1, 0)
                v.tensor_copy(c_xp[:, :], view(5, T, 0, D)).then_inc(c_xqs, 1)
                at(x_out_free, 1, 0)
                add_to_x(5, 6)
                assert count[0] == DVE_STEPS and norms[0] == NORMS, (count[0], norms[0])


def rope_tables():
    half = ROT // 2
    inv = (np.float32(1.0) / np.power(np.float32(10000.0), np.arange(half, dtype=np.float32) * np.float32(2.0)
                                      / np.float32(ROT))).astype(np.float32)
    ang = (np.arange(T, dtype=np.float32)[:, None] * inv).astype(np.float32)
    sin, cos = np.sin(ang).astype(np.float32), np.cos(ang).astype(np.float32)
    return np.concatenate([cos, cos, sin, -sin], axis=1)


def const_table():
    c = np.zeros((P, NCONST), np.float32)

    def part(name):
        lo, hi = CONST[name]
        return c[:, lo:hi]

    part("ident")[:] = np.eye(P)
    for t in range(T):
        if t + LK - 1 - LPAD < T + LK - 1:
            part("band")[t, t + LK - 1 - LPAD] = 1.0
    for e in range(NE):
        part("own")[e, e * TK:(e + 1) * TK] = 1.0
        part("block")[e * TK:(e + 1) * TK, e * TK:(e + 1) * TK] = 1.0
    part("rope")[:T] = rope_tables()
    part("iota8")[:] = np.arange(NE)
    for g in range(4):
        for r in range(4):
            part("sel")[32 * g + r, r * T:(r + 1) * T] = -1.0
    return c


def tiles(v):
    return v.reshape(-1, P).T


def kernel(**inputs):
    import concourse.bacc as bacc
    from concourse.bass_utils import run_bass_kernel_spmd

    i = {k: np.asarray(v) for k, v in inputs.items()}
    cols = np.zeros((P, NCOLS), np.float32)
    parts = np.arange(P)
    for name, v in (("lat_w", i["L0_xattn_ln_l_w"]), ("lat_b", i["L0_xattn_ln_l_b"]), ("ctx_w", i["L0_xattn_ln_c_w"]),
                    ("ctx_b", i["L0_xattn_ln_c_b"]), ("qb", i["L0_ffn_qb"].reshape(-1)),
                    ("kb", i["L0_ffn_kb"].reshape(-1)), ("lam", np.repeat(i["L0_attn_decay"][:, 1, 0], D // 16)),
                    ("v", i["L1_attn_v"][:, 0]), ("iota", parts), ("even", parts // ED % 2 == 0),
                    ("odd", parts // ED % 2 == 1)):
        t = tiles(v)
        cols[:, COLS[name]:COLS[name] + t.shape[1]] = t
    rows = np.concatenate([i[k].reshape(-1) for k in (
        "L0_attn_ln_g", "L0_attn_ln_b", "L0_xattn_bo", "L0_ffn_rb1", "L0_ffn_ln_g", "L0_ffn_ln_b", "L0_ffn_rb2",
        "L0_ffn_vb")])
    arrays = {
        "x": i["x"], "ctx": i["ctx_1024"], "ctxT": i["ctx_1024"].transpose(0, 2, 1),
        "cols": cols, "rows": rows, "const": const_table(),
        "ret_q": i["L0_attn_Wq"].T, "ret_v": i["L0_attn_Wv"].T, "ret_g": i["L0_attn_Wg"].T, "ret_o": i["L0_attn_Wo"].T,
        "x_q": i["L0_xattn_Wq"], "x_kv": i["L0_xattn_Wkv"], "x_o": i["L0_xattn_Wo"],
        "r_w1": i["L0_ffn_rW1"].T, "r_w2": i["L0_ffn_rW2"].T, "e_bo": i["L0_ffn_ob"],
        "e_q": i["L0_ffn_qW"].transpose(0, 2, 1), "e_k": i["L0_ffn_kW"].transpose(0, 2, 1),
        "e_v": i["L0_ffn_vW"].transpose(0, 2, 1), "e_o": i["L0_ffn_oW"].transpose(0, 2, 1),
        "l_w1": i["L1_attn_w1"], "l_w2": i["L1_attn_w2"],
        "m_q": i["L1_xattn_Wq"].T, "m_k": i["L1_xattn_Wk"].T, "m_v": i["L1_xattn_Wv"].T, "m_o": i["L1_xattn_Wo"],
        "c_r": i["L1_ffn_Wr"].T, 
        "c_qk": i["L1_ffn_Wqkv"][:, :, :2 * HP].reshape(NE, D, 2, HP).transpose(2, 0, 1, 3).reshape(2 * NE, D, HP),
        "c_v": i["L1_ffn_Wqkv"][:, :, 2 * HP:], "c_o": i["L1_ffn_Wo"],
    }
    for k, v in arrays.items():
        if k not in ("x", "ctx", "ctxT", "cols", "rows", "const", "r_w2", "e_bo"):
            v = v.reshape(*v.shape[:-2], -1, P, v.shape[-1])
            arrays[k] = np.moveaxis(v, -2, 0)
    arrays["c_o"] = arrays["c_o"][:, :, 0]
    arrays = {f"in_{k}": np.ascontiguousarray(v) for k, v in arrays.items()}
    nc = bacc.Bacc("TRN2", target_bir_lowering=False, num_devices=1)
    aps = {k[3:]: nc.dram_tensor(k, v.shape, mybir.dt.from_np(v.dtype), kind="ExternalInput").ap()
           for k, v in arrays.items()}
    out = nc.dram_tensor("out", (B, T, D), F32, kind="ExternalOutput").ap()
    build(nc, aps, out)
    r = run_bass_kernel_spmd(nc, [arrays], core_ids=[0])
    return r.results[0]["out"]
```

```python
from contextlib import ExitStack

import numpy as np
import concourse.bass as bass
from concourse import mybir

F32 = mybir.dt.float32
BF16 = mybir.dt.bfloat16
U32 = mybir.dt.uint32
ALU = mybir.AluOpType
ACT = mybir.ActivationFunctionType
AX = mybir.AxisListType

B, T, D = 8, 112, 256
S, KP = 375, 125
KTILES = S // KP
P = 128
C = D // P
XH, XD = 16, 64
INNER = XH * XD
IT = INNER // P
NE = 8
EH, ED = 16, 16
R1 = 128
LK, LPAD = 16, 7
TK = max(T // 8, 2)
HP = 128
ROT = 64
EPS = 1e-5
CLIP = 11.0
SUBS = 3
FRONT_NORMS, TAIL_NORMS = 7, 3
FRONT_STEPS, TAIL_STEPS = 50, 28
REGION = 9984

(L_NORM, L_XT, L_PROJ, L_Z, L_Z2, L_TANH, L_SCORE, L_BAND_T, L_OUT, M_XT, M_QUERY, M_SCORE, M_OUT, C_XT,
 C_ROUTE, C_POS, C_GATHER, C_QK, C_V, C_SCORE, C_PROB_T, C_AV, C_UP, C_UP_T, C_OUT) = range(25)
PLACES = [L_NORM, L_XT, L_PROJ, L_Z, L_Z2, L_TANH, None, L_SCORE, None, None, L_BAND_T, L_OUT, M_XT, M_QUERY,
          M_SCORE, None, M_OUT, C_XT, C_ROUTE, None, C_POS, C_GATHER, None, C_QK, C_V, None, C_SCORE, None,
          C_PROB_T, C_AV, C_UP, C_UP_T, C_OUT]
PER_SLOT = 5

COLS = {}
_n = 0
for _name, _w in (("lat_w", C), ("lat_b", C), ("ctx_w", C), ("ctx_b", C), ("qb", NE * C), ("kb", NE * C),
                  ("vb", NE * C),
                  ("ret_g", C), ("ret_b", C), ("ffn_g", 1), ("ffn_b", 1),
                  ("lam", C), ("v", C), ("iota", 1), ("even", 1), ("odd", 1)):
    COLS[_name] = _n
    _n += _w
NCOLS = _n
ROWS = {}
_n = 0
for _name, _w in (("bo", D), ("rb1", R1), ("rb2", NE)):
    ROWS[_name] = (_n, _n + _w)
    _n += _w
NROWS = _n
CONST = {}
_n = 0
for _name, _w in (("ident", P), ("band", T + LK - 1), ("own", NE * TK), ("block", NE * TK), ("rope", 2 * ROT),
                  ("iota8", NE)):
    CONST[_name] = (_n, _n + _w)
    _n += _w
NCONST = _n




def build(nc, a, out):
    with ExitStack() as ctx:
        def sb(name, shape, dt=F32):
            return ctx.enter_context(nc.sbuf_tensor(name, shape, dt))

        def sem(name):
            return ctx.enter_context(nc.semaphore(name))

        bank = [ctx.enter_context(nc.psum_tensor(f"bank{i}", [P, 512], F32)) for i in range(8)]

        ret_w = sb("ret_w", [P, 4, C, D])
        turns_w = sb("turns_w", [P, 2 * C * INNER])
        x_wq = turns_w[:, 0:C * INNER].rearrange("p (c n) -> p c n", c=C)
        x_wo = turns_w[:, C * INNER:].rearrange("p (i n) -> p i n", i=IT)
        c_wqk = turns_w[:, :].rearrange("p (q c n) -> p q c n", q=2 * NE, c=C)
        x_wkv = sb("x_wkv", [P, C, 2 * INNER])
        r_w1 = sb("r_w1", [P, C, R1])
        r_w2 = sb("r_w2", [P, NE])
        e_wq = sb("e_wq", [P, NE, C, D])
        e_wk = sb("e_wk", [P, NE, C, D])
        e_wv = sb("e_wv", [P, NE, C, D])
        e_wo = sb("e_wo", [P, NE, C, D])
        e_bo = sb("e_bo", [NE, D])
        l_w = sb("l_w", [P, 2, C, D])
        m_qk = sb("m_qk", [P, C, D])
        m_vo = sb("m_vo", [P, C, D])
        c_wr = sb("c_wr", [P, C, NE])
        c_wv = sb("c_wv", [P, NE, C, HP])
        c_wo = sb("c_wo", [P, NE, D])
        cols = sb("cols", [P, NCOLS])
        rows = sb("rows", [P, NROWS])
        const = sb("const", [P, NCONST])
        ident_b = sb("ident_b", [P, P], BF16)
        sel_b = sb("sel_b", [P, 4, 4, T], BF16)
        e_bo_all = sb("e_bo_all", [NE, D])
        mw_q = e_wq[:, 0:4].rearrange("p a c d -> p (a c) d")
        mw_k = e_wq[:, 4:8].rearrange("p a c d -> p (a c) d")
        mw_v = e_wk[:, 0:4].rearrange("p a c d -> p (a c) d")
        mw_o = e_wk[:, 4:8].rearrange("p a c d -> p (a c) d")

        x_in = sb("x_in", [T, D])
        x = sb("x", [T, D])
        x_out = sb("x_out", [T, D])
        xn = sb("xn", [T, D])
        xnT = sb("xnT", [P, C, T])
        stats = sb("stats", [P, KTILES, 6])
        mv = sb("mv", [P, KTILES, 2])
        var = sb("var", [P, KTILES])
        rstd = sb("rstd", [P, KTILES])
        tx = sb("tx", [T, D])
        txn = sb("txn", [T, D])
        txnT = sb("txnT", [P, C, T])
        tstats = sb("tstats", [P, 1, 6])
        tmv = sb("tmv", [P, 1, 2])
        tvar = sb("tvar", [P, 1])
        trstd = sb("trstd", [P, 1])
        minus_half = sb("minus_half", [P, KTILES])
        ctx_tok = sb("ctx_tok", [KP, KTILES, D])
        ctx_raw = sb("ctx_raw", [P, C, S])
        ctxnT = sb("ctxnT", [P, C, S])
        region = sb("region", [P, REGION])

        def at_word(lo, n, *dims, dt=F32):
            size = int(np.prod(dims))
            if dt == BF16:
                v = region[0:n, lo:lo + (size + 1) // 2].bitcast(BF16)
            elif dt == U32:
                v = region[0:n, lo:lo + size].bitcast(U32)
            else:
                v = region[0:n, lo:lo + size]
            spent[0] = lo + (size if dt != BF16 else (size + 1) // 2)
            tops.append(spent[0])
            names = "abcd"[:len(dims)]
            if len(dims) == 1:
                return v
            return v.rearrange("p (" + " ".join(names) + ") -> p " + " ".join(names),
                               **{k: d for k, d in zip(names, dims)})

        spent, tops = [0], []

        def then(n, *dims, dt=F32):
            return at_word(spent[0], n, *dims, dt=dt)

        x_kT = at_word(0, P, IT, S)
        x_v = then(KP, KTILES, XH, XD + 1)
        after_keys = spent[0]
        state = at_word(after_keys, P, C, T)
        yT = then(P, C, T)
        gateT = then(P, C, T)
        eg = then(P, C, T)
        y2 = then(T, D)
        y2T = then(P, C, T)
        ctxn = then(KP, KTILES, D)
        x_o = at_word(after_keys, T, INNER)
        x_qT = then(P, IT, T)
        x_p = then(KP, 3, KTILES, T)
        x_oT = then(P, IT, T)
        x_rc = sb("x_rc", [T, 4, 1])
        e_k = sb("e_k", [P, 2, C, 4, T])
        e_max = sb("e_max", [T, 4, 32], BF16)
        h1 = at_word(0, T, R1)
        h1T = then(P, T)
        lg = then(T, NE)
        pr = then(T, NE)
        top = then(T, 8)
        topi = then(T, 8, dt=U32)
        topf = then(T, 8)
        g01 = then(T, 2, NE)
        gates = then(T, NE)
        gatesT = then(NE, T)
        e_q = then(P, 2, C * 2 * T).rearrange("p e (c o t) -> p e c o t", c=C, o=2)
        e_qb = then(P, C, 2, T, dt=BF16)
        e_kb = then(P, C, 4, T, dt=BF16)
        e_maxT = then(P, T, dt=BF16)
        e_p = then(T, 2, 4, T)
        e_v = then(T, 2, EH, ED + 1)
        e_rc = then(T, EH, 1)
        e_o = then(T, EH, ED)
        e_oT = then(P, C, T)
        after_experts = spent[0]
        l_proj = sb("l_proj", [P, C, T + LK - 1])
        l_t = at_word(after_experts, P, C, LK, T)
        l_q = then(P, C, T)
        l_w16 = then(T, LK)
        l_a = then(T, T)
        l_aT = then(T, T)
        m_z = then(KP, KTILES, D)
        m_g = at_word(after_experts, P, C, T)
        m_e = then(KP, KTILES, T)
        m_nm = then(KP, KTILES)
        m_sum = then(KP, KTILES)
        c_s = at_word(after_experts, NE, T)
        c_s2 = then(NE, T)
        c_top = then(NE, 16)
        c_idx = then(NE, 16, dt=U32)
        c_idxf = then(NE, 16)
        c_diag = then(NE, 2, NE, TK)
        c_pos = then(T, T)
        c_hot = then(T, T)
        c_hotT = then(T, T)
        c_iv = then(T, 2)
        c_cs = then(ROT, 2, T)
        c_xgT = then(P, C, T)
        c_qk = then(P, 2, T)
        c_rot = then(ROT, 2, T)
        c_vT = then(P, T)
        c_v = then(T, HP)
        c_pen = then(T, T)
        c_e = then(T, T)
        c_eT = then(T, T)
        c_avT = then(P, T)
        c_xpT = then(P, C, T)
        c_xp = then(T, D)
        sc1 = sb("sc1", [P, 16])
        pool_idle = sb("pool_idle", [1, 1])
        idle = sb("idle", [1, 1])
        ones8 = sb("ones8", [NE, T])
        vb_cols = at_word(0, P, NE, C, NE)

        def cst(name):
            lo, hi = CONST[name]
            return const[:, lo:hi]

        def row(name, n=T, at=0, width=None):
            lo, hi = ROWS[name]
            return rows[0:n, lo + at:(lo + at + width) if width else hi]

        def col(name, k=0, lo=0, hi=P):
            return cols[lo:hi, COLS[name] + k:COLS[name] + k + 1]

        ident = cst("ident")

        def view(bk, n, lo, *dims):
            size = int(np.prod(dims))
            v = bank[bk][0:n, lo:lo + size]
            if len(dims) == 1:
                return v
            names = "abc"[:len(dims)]
            return v.rearrange("p (" + " ".join(names) + ") -> p " + " ".join(names),
                               **{k: d for k, d in zip(names, dims)})

        def windows(ap, *dims):
            return bass.AP(ap.tensor, ap.offset, [ap.ap[0]] + [list(d) for d in dims])

        w_small = sem("w_small")
        w_ret = sem("w_ret")
        w_x = sem("w_x")
        wx_loaded = sem("wx_loaded")
        wc_loaded = sem("wc_loaded")
        w_e = sem("w_e")
        w_eqk = sem("w_eqk")
        w_l = sem("w_l")
        w_m = sem("w_m")
        dve_set = sem("dve_set")
        ones_made = sem("ones_made")
        eb_ready = sem("eb_ready")
        c_vq = sem("c_vq")
        w_c = sem("w_c")
        consts_made = sem("consts_made")
        m_psum = sem("m_psum")
        m_made = sem("m_made")
        half_made = sem("half_made")
        x_out_free = sem("x_out_free")
        x_loaded = sem("x_loaded")
        ctx_loaded = sem("ctx_loaded")
        raw_loaded = sem("raw_loaded")
        out_stored = sem("out_stored")
        dve_done = sem("dve_done")
        var_ready = sem("var_ready")
        rstd_ready = sem("rstd_ready")
        tvar_ready = sem("tvar_ready")
        trstd_ready = sem("trstd_ready")
        xn_ready = sem("xn_ready")
        xt_psum = sem("xt_psum")
        xt_ready = sem("xt_ready")
        sub_out = sem("sub_out")
        x_done = sem("x_done")
        txn_ready = sem("txn_ready")
        txt_psum = sem("txt_psum")
        txt_ready = sem("txt_ready")
        tsub_out = sem("tsub_out")
        tx_done = sem("tx_done")
        ctxn_ready = sem("ctxn_ready")
        ctxt_psum = sem("ctxt_psum")
        ctxt_ready = sem("ctxt_ready")
        kv_psum = sem("kv_psum")
        kv_ready = sem("kv_ready")
        ret_qv = sem("ret_qv")
        ret_g = sem("ret_g")
        ret_eg = sem("ret_eg")
        ret_y = sem("ret_y")
        ret_yt = sem("ret_yt")
        ret_y2 = sem("ret_y2")
        ret_y2t_psum = sem("ret_y2t_psum")
        ret_y2t = sem("ret_y2t")
        xq_psum = sem("xq_psum")
        xq_ready = sem("xq_ready")
        xs_psum = sem("xs_psum")
        xs_exp = sem("xs_exp")
        xs_clip = sem("xs_clip")
        xs_pv = sem("xs_pv")
        xo_ready = sem("xo_ready")
        xot_psum = sem("xot_psum")
        xot_ready = sem("xot_ready")
        r_h = sem("r_h")
        r_hn = sem("r_hn")
        r_ht_psum = sem("r_ht_psum")
        r_ht = sem("r_ht")
        r_lg = sem("r_lg")
        r_nm = sem("r_nm")
        bo_psum = sem("bo_psum")
        bo_made = sem("bo_made")
        r_exp = sem("r_exp")
        r_gates = sem("r_gates")
        r_gt_psum = sem("r_gt_psum")
        r_gt = sem("r_gt")
        eqk_psum = sem("eqk_psum")
        evo_psum = sem("evo_psum")
        eq_ready = sem("eq_ready")
        ek_ready = sem("ek_ready")
        ev_ready = sem("ev_ready")
        es_psum = sem("es_psum")
        es_max = sem("es_max")
        emt_psum = sem("emt_psum")
        emt_ready = sem("emt_ready")
        est_psum = sem("est_psum")
        est_exp = sem("est_exp")
        epv = sem("epv")
        eo_ready = sem("eo_ready")
        eot_ready = sem("eot_ready")
        l_psum = sem("l_psum")
        l_sum = sem("l_sum")
        l_tanh = sem("l_tanh")
        l_score = sem("l_score")
        l_nm = sem("l_nm")
        l_exp = sem("l_exp")
        l_band = sem("l_band")
        l_at_psum = sem("l_at_psum")
        l_at = sem("l_at")
        z_psum = sem("z_psum")
        z_ready = sem("z_ready")
        g_psum = sem("g_psum")
        g_ready = sem("g_ready")
        ms_psum = sem("ms_psum")
        ms_nm = sem("ms_nm")
        ms_exp = sem("ms_exp")
        ms_e = sem("ms_e")
        c_lg = sem("c_lg")
        c_en = sem("c_en")
        c_dg = sem("c_dg")
        c_rpsum = sem("c_rpsum")
        c_hots = sem("c_hots")
        c_gpsum = sem("c_gpsum")
        c_xg = sem("c_xg")
        c_qkv = sem("c_qkv")
        c_qk_ready = sem("c_qk_ready")
        c_v_ready = sem("c_v_ready")
        l_read = sem("l_read")
        c_spsum = sem("c_spsum")
        c_nm = sem("c_nm")
        c_exp = sem("c_exp")
        c_en2 = sem("c_en2")
        c_etp = sem("c_etp")
        c_et = sem("c_et")
        c_avp = sem("c_avp")
        c_av = sem("c_av")
        c_xpp = sem("c_xpp")
        c_xps = sem("c_xps")
        c_xqp = sem("c_xqp")
        c_xqs = sem("c_xqs")

        NKV = IT + 2 * KTILES

        assert max(tops) <= REGION
        block = ctx.enter_context(nc.Block())

        @block.sync
        def _(sp):
            sp.dma_start(cols[:, :], a["cols"]).then_inc(w_small, 16)
            sp.dma_start(const[:, :], a["const"]).then_inc(w_small, 16)
            sp.dma_start(x_in[:, :], a["x"][0]).then_inc(x_loaded, 16)
            sp.dma_start(ctx_tok[:, :, :], a["ctx"][0].rearrange("(j p) d -> p j d", p=KP)).then_inc(ctx_loaded, 16)
            for i, name in enumerate(("ret_q", "ret_v", "ret_g", "ret_o")):
                sp.dma_start(ret_w[:, i], a[name]).then_inc(w_ret, 16)
            sp.dma_start(rows[:, :], a["rows"].partition_broadcast(P)).then_inc(w_small, 16)
            sp.dma_start(x_wkv[:, :, :], a["x_kv"]).then_inc(w_x, 16)
            sp.dma_start(x_wq, a["x_q"]).then_inc(wx_loaded, 16)
            sp.dma_start(x_wo, a["x_o"]).then_inc(wx_loaded, 16)
            sp.dma_start(r_w1[:, :, :], a["r_w1"]).then_inc(w_e, 16)
            sp.dma_start(r_w2[:, :], a["r_w2"]).then_inc(w_e, 16)
            sp.dma_start(e_bo[:, :], a["e_bo"]).then_inc(w_e, 16)
            sp.dma_start(e_wv[:, :, :, :], a["e_v"]).then_inc(w_e, 16)
            sp.dma_start(e_wo[:, :, :, :], a["e_o"]).then_inc(w_e, 16)
            sp.dma_start(ctx_raw[:, :, :], a["ctxT"][0].rearrange("(c p) k -> p c k", p=P)).then_inc(raw_loaded, 16)
            sp.dma_start(l_w[:, 0], a["l_w1"]).then_inc(w_l, 16)
            sp.dma_start(l_w[:, 1], a["l_w2"]).then_inc(w_l, 16)
            sp.dma_start(c_wr[:, :, :], a["c_r"]).then_inc(w_c, 16)
            sp.dma_start(c_wv[:, :, :, :], a["c_v"]).then_inc(w_c, 16)
            sp.dma_start(c_wo[:, :, :], a["c_o"]).then_inc(w_c, 16)
            sp.wait_ge(m_made, 2)
            sp.dma_start(e_wq[:, :, :, :], a["e_q"]).then_inc(w_eqk, 16)
            sp.dma_start(e_wk[:, :, :, :], a["e_k"]).then_inc(w_eqk, 16)
            def load_inputs(b):
                sp.wait_ge(x_done, b * SUBS + 1)
                sp.dma_start(x_in[:, :], a["x"][bass.ds(b + 1, 1)].rearrange("a t d -> (a t) d")).then_inc(x_loaded, 16)
                sp.wait_ge(ctxn_ready, b + 1)
                sp.dma_start(ctx_tok[:, :, :], a["ctx"][bass.ds(b + 1, 1)].rearrange("a (j p) d -> p (a j) d", p=KP)
                             ).then_inc(ctx_loaded, 16)

            def load_for_tail(b):
                sp.wait_ge(sub_out, b * SUBS + 2)
                sp.dma_start(c_wqk, a["c_qk"]).then_inc(wc_loaded, 16)
                sp.wait_ge(ms_psum, b)
                sp.dma_start(ctx_raw[:, :, :], a["ctxT"][bass.ds(b, 1)].rearrange("a (c p) k -> p (a c) k", p=P)
                             ).then_inc(raw_loaded, 16)

            load_inputs(0)
            with sp.Fori(1, B - 1) as b:
                load_inputs(b)
                load_for_tail(b)
                sp.wait_ge(c_vq, b)
                sp.dma_start(x_wq, a["x_q"]).then_inc(wx_loaded, 16)
                sp.dma_start(x_wo, a["x_o"]).then_inc(wx_loaded, 16)
            load_for_tail(B - 1)

        @block.gpsimd
        def _(pool):
            for name, dst in (("m_q", mw_q), ("m_k", mw_k), ("m_v", mw_v), ("m_o", mw_o)):
                pool.dma_start(dst, a[name]).then_inc(w_m, 16)
            nc.gpsimd.memset(minus_half[:, :], -0.5).then_inc(half_made, 1)
            nc.gpsimd.memset(pool_idle[:, :], 0.0).then_inc(x_out_free, 1)
            pool.wait_ge(half_made, 1)

            def front(b):
                for k in range(FRONT_NORMS):
                    pool.wait_ge(var_ready, b * FRONT_NORMS + (k + 1))
                    n, w = (KP, KTILES) if k == 1 else (T, 1)
                    nc.gpsimd.tensor_tensor(rstd[0:n, 0:w], var[0:n, 0:w], minus_half[0:n, 0:w], ALU.pow
                                            ).then_inc(rstd_ready, 1)

            def tail(t):
                for k in range(TAIL_NORMS):
                    pool.wait_ge(tvar_ready, t * TAIL_NORMS + (k + 1))
                    nc.gpsimd.tensor_tensor(trstd[0:T, :], tvar[0:T, :], minus_half[0:T, 0:1], ALU.pow
                                            ).then_inc(trstd_ready, 1)
                pool.wait_ge(tx_done, t * SUBS + SUBS)
                pool.dma_start(out[bass.ds(t, 1)].rearrange("a t d -> (a t) d"), x_out[:, :]).then_inc(out_stored, 16)
                pool.wait_ge(out_stored, t * 16 + 16)
                nc.gpsimd.tensor_tensor(pool_idle[:, :], minus_half[0:1, 0:1], minus_half[0:1, 0:1], ALU.mult
                                        ).then_inc(x_out_free, 1)

            front(0)
            with pool.Fori(1, B) as b:
                front(b)
                tail(b - 1)
            tail(B - 1)
            pool.wait_ge(out_stored, 16 * B)

        @block.tensor
        def _(pe):
            mm = nc.tensor.matmul

            def tr(dst, src, n):
                return nc.tensor.transpose(dst, src, ident[0:n, 0:n])

            def front(b, t):
                def at(s, per, k):
                    pe.wait_ge(s, b * per + (k + 1))

                def normed_T(s):
                    at(xn_ready, SUBS, s)
                    for c in range(C):
                        last = tr(view(0, P, c * T, T), xn[:, c * P:(c + 1) * P], T)
                    last.then_inc(xt_psum, 1)
                    at(xt_ready, SUBS, s)

                def kv(n):
                    bk = 6 + n % 2
                    if n >= 2:
                        at(kv_ready, NKV, n - 2)
                    for c in range(C):
                        if n < IT:
                            last = mm(bank[bk][:, 0:S], x_wkv[:, c, n * P:(n + 1) * P], ctxnT[:, c, :],
                                      start=(c == 0), stop=(c == C - 1))
                        else:
                            j, half = (n - IT) // 2, (n - IT) % 2
                            lo = INNER + half * 512
                            last = mm(bank[bk][0:KP, :], ctxnT[:, c, j * KP:(j + 1) * KP], x_wkv[:, c, lo:lo + 512],
                                      start=(c == 0), stop=(c == C - 1))
                    last.then_inc(kv_psum, 1)

                pe.wait_ge(w_ret, 64)
                at(xn_ready, SUBS, 0)
                for c in range(C):
                    last = tr(view(0, P, c * T, T), xn[:, c * P:(c + 1) * P], T)
                last.then_inc(xt_psum, 1)
                at(ctxn_ready, 1, 0)
                for c in range(C):
                    for j in range(KTILES):
                        last = tr(bank[4 + c][:, j * KP:(j + 1) * KP], ctxn[:, j, c * P:(c + 1) * P], KP)
                    last.then_inc(ctxt_psum, 1)
                at(xt_ready, SUBS, 0)
                for i, bk, lo, done in ((1, 1, C * T, None), (0, 1, 0, ret_qv), (2, 2, 0, ret_g)):
                    for m in range(C):
                        for c in range(C):
                            last = mm(view(bk, P, lo + m * T, T), ret_w[:, i, c, m * P:(m + 1) * P], xnT[:, c, :],
                                      start=(c == 0), stop=(c == C - 1))
                    if done is not None:
                        last.then_inc(done, 1)
                pe.wait_ge(w_x, 16)
                at(ctxt_ready, C, C - 1)
                for n in range(0, 3):
                    kv(n)
                at(ret_y, 1, 0)
                for c in range(C):
                    last = tr(view(3, T, c * P, P), yT[:, c, :], P)
                last.then_inc(ret_yt, 1)
                for n in range(3, 7):
                    kv(n)
                at(ret_y2, 1, 0)
                for c in range(C):
                    last = tr(view(0, P, c * T, T), y2[:, c * P:(c + 1) * P], T)
                last.then_inc(ret_y2t_psum, 1)
                kv(7)
                at(ret_y2t, 1, 0)
                for c in range(C):
                    last = mm(view(1, T, 0, D), y2T[:, c, :], ret_w[:, 3, c, :], start=(c == 0), stop=(c == C - 1))
                last.then_inc(sub_out, 1)
                for n in range(8, NKV):
                    kv(n)

                normed_T(1)
                pe.wait_ge(wx_loaded, 32 if isinstance(b, int) else b * 32)
                for m in range(IT):
                    for c in range(C):
                        last = mm(view(1 + m // 4, P, (m % 4) * T, T), x_wq[:, c, m * P:(m + 1) * P], xnT[:, c, :],
                                  start=(c == 0), stop=(c == C - 1))
                    if m % 4 == 3:
                        last.then_inc(xq_psum, 1)
                at(kv_ready, NKV, NKV - 1)
                for i in range(XH + 2):
                    if i < XH:
                        if i % 8 == 0:
                            at(xq_ready, 2, i // 8)
                        if i >= 2:
                            at(xs_exp, XH, i - 2)
                        lo = XD * (i % 2)
                        for j in range(KTILES):
                            last = mm(view(3 + i % 2, KP, j * T, T), x_kT[lo:lo + XD, i // 2, j * KP:(j + 1) * KP],
                                      x_qT[lo:lo + XD, i // 2, :], start=True, stop=True)
                        last.then_inc(xs_psum, 1)
                    if i >= 2:
                        h = i - 2
                        at(xs_clip, XH, h)
                        if h % 4 == 0 and h >= 8:
                            at(xo_ready, 4, h // 4 - 2)
                        for j in range(KTILES):
                            last = mm(view(5 + (h // 4) % 2, T, (h % 4) * (XD + 1), XD + 1), x_p[:, h % 3, j, :],
                                      x_v[:, j, h, :], start=(j == 0), stop=(j == KTILES - 1))
                        last.then_inc(xs_pv, 1)
                for i in range(IT):
                    if i % 4 == 0:
                        at(xo_ready, 4, i // 2 + 1)
                    last = tr(view(1 + i // 4, P, (i % 4) * T, T), x_o[:, i * P:(i + 1) * P], T)
                    if i % 4 == 3:
                        last.then_inc(xot_psum, 1)
                for i in range(IT):
                    if i % 4 == 0:
                        at(xot_ready, 2, i // 4)
                    last = mm(view(0, T, 0, D), x_oT[:, i, :], x_wo[:, i, :], start=(i == 0), stop=(i == IT - 1))
                last.then_inc(sub_out, 1)

                normed_T(2)
                pe.wait_ge(w_e, 80)
                pe.wait_ge(w_eqk, 32)
                for c in range(C):
                    last = mm(view(1, T, 0, R1), xnT[:, c, :], r_w1[:, c, :], start=(c == 0), stop=(c == C - 1))
                last.then_inc(r_h, 1)

                def project_qk(e):
                    if e:
                        at(ek_ready, NE, e - 1)
                    for w, lo in ((e_wq, 0), (e_wk, C * T)):
                        for m in range(C):
                            for c in range(C):
                                last = mm(view(5, P, lo + m * T, T), w[:, e, c, m * P:(m + 1) * P], xnT[:, c, :],
                                          start=(c == 0), stop=(c == C - 1))
                    last.then_inc(eqk_psum, 1)

                def maxima_T(e):
                    at(es_max, 4 * NE, 4 * e + 3)
                    if e:
                        at(eo_ready, NE, e - 1)
                    nc.tensor.transpose(bank[7][:, 288:288 + T // 2].bitcast(BF16),
                                        e_max[:, :, :].rearrange("p g r -> p (g r)"), ident_b[0:T, 0:T]
                                        ).then_inc(emt_psum, 1)

                def project_v(e):
                    if e:
                        at(ev_ready, NE, e - 1)
                    if e >= 3:
                        at(eot_ready, NE, e - 3)
                    for c in range(C):
                        last = mm(view(6, T, 0, D), xnT[:, c, :], e_wv[:, e, c, :], start=(c == 0), stop=(c == C - 1))
                    if e < 2:
                        last.then_inc(evo_psum, 1)

                def max_scores(e, r):
                    if r == 0:
                        at(eb_ready, NE, e)
                    if 4 * e + r >= 1:
                        at(es_max, 4 * NE, 4 * e + r - 1)
                    mm(view(1, T, 0, 4 * T), e_qb[:, r // 2, r % 2, :],
                       e_kb[:, r // 2, :, :].rearrange("p g t -> p (g t)"), start=True, stop=True
                       ).then_inc(es_psum, 1)

                def scores_T(e, g):
                    if 4 * e + g >= 2:
                        at(est_exp, 4 * NE, 4 * e + g - 2)
                    elif g == 1:
                        at(r_nm, 1, 0)
                    for m in range(C):
                        mm(view(3 + g % 2, T, 2 * m * T, 2 * T), e_k[:, e % 2, m, g, :],
                           e_q[:, e % 2, m, :, :].rearrange("p o t -> p (o t)"), start=True, stop=True,
                           skip_group_check=True)
                        if g == 0 and m == 0:
                            at(emt_ready, NE, e)
                        for o in range(2):
                            last = mm(view(3 + g % 2, T, (2 * m + o) * T, T), sel_b[:, 2 * m + o, g, :], e_maxT[:, :],
                                      start=False, stop=True, skip_group_check=True)
                    last.then_inc(est_psum, 1)

                def probs_v(e, g):
                    if g == 0:
                        at(ev_ready, NE, e)
                    at(est_exp, 4 * NE, 4 * e + g)
                    for r in range(4):
                        h = 8 * (r // 2) + 2 * g + r % 2
                        last = mm(view(7, T, h * (ED + 1), ED + 1), e_p[:, g % 2, r, :], e_v[:, e % 2, h, :],
                                  start=True, stop=True)
                    last.then_inc(epv, 1)

                def out_T(e):
                    at(eo_ready, NE, e)
                    if e >= NE - 2:
                        at(eot_ready, NE, e - 1)
                    if e == NE - 2:
                        at(ev_ready, NE, NE - 1)
                    for c in range(C):
                        last = tr(view(6, P, D + c * T, T), e_o[:, 8 * c:8 * c + 8, :].rearrange("p h d -> p (h d)"), T)
                    last.then_inc(evo_psum, 1)

                def out_sum(e):
                    at(eot_ready, NE, e)
                    for c in range(C):
                        mm(view(0, T, 0, D), e_oT[:, c, :], e_wo[:, e, c, :], start=(e == 0 and c == 0), stop=False)

                for s in range(NE + 2):
                    if s < NE:
                        project_qk(s)
                    if 1 <= s <= NE:
                        maxima_T(s - 1)
                    if s < NE:
                        project_v(s)
                    if s >= 2:
                        out_T(s - 2)
                    if s == 0:
                        at(r_hn, 1, 0)
                        tr(view(3, P, 0, T), h1[:, :], T).then_inc(r_ht_psum, 1)
                    for g in range(PER_SLOT):
                        if g < 4 and 1 <= s <= NE:
                            scores_T(s - 1, g)
                        if g >= 1 and s < NE:
                            max_scores(s, g - 1)
                        if g >= 1 and 1 <= s <= NE:
                            probs_v(s - 1, g - 1)
                        if g == 1 and s >= 2:
                            out_sum(s - 2)
                        if g == 2 and s == 0:
                            at(r_ht, 1, 0)
                            mm(view(4, T, 0, NE), h1T[:, :], r_w2[:, :], start=True, stop=True).then_inc(r_lg, 1)
                        if t is not None and 1 <= s <= NE:
                            place = PER_SLOT * (s - 1) + g
                            if place < len(PLACES) and PLACES[place] is not None:
                                tail_step(PLACES[place], t)
                at(r_gates, 1, 0)
                tr(view(3, NE, 0, T), gates[:, :], T).then_inc(r_gt_psum, 1)
                at(r_gt, 1, 0)
                mm(view(0, T, 0, D), gatesT[:, :], e_bo_all[:, :], start=False, stop=True).then_inc(sub_out, 1)

            def tail_step(step, t):
                def at(s, per, k):
                    pe.wait_ge(s, t * per + (k + 1))

                def normed_T(s):
                    at(txn_ready, SUBS, s)
                    for c in range(C):
                        last = tr(view(2, P, c * T, T), txn[:, c * P:(c + 1) * P], T)
                    last.then_inc(txt_psum, 1)

                if step == L_XT:
                    normed_T(0)
                elif step == L_PROJ:
                    at(txt_ready, SUBS, 0)
                    pe.wait_ge(w_l, 32)
                    for i in range(2):
                        for m in range(C):
                            for c in range(C):
                                last = mm(view(2, P, (i * C + m) * T, T), l_w[:, i, c, m * P:(m + 1) * P],
                                          txnT[:, c, :], start=(c == 0), stop=(c == C - 1))
                    last.then_inc(l_psum, 1)
                elif step in (L_Z, L_Z2):
                    if step == L_Z:
                        pe.wait_ge(raw_loaded, t * 16 + 16)
                        at(l_read, 1, 0)
                    else:
                        at(z_ready, 2, 0)
                    for j in ((0, 1) if step == L_Z else (2,)):
                        for c in range(C):
                            last = mm(view(2, KP, (j % 2) * D, D), ctx_raw[:, c, j * KP:(j + 1) * KP],
                                      m_vo[:, c, :], start=(c == 0), stop=(c == C - 1))
                    last.then_inc(z_psum, 1)
                elif step == L_SCORE:
                    at(z_ready, 2, 1)
                    at(l_tanh, C, C - 1)
                    for k in range(LK):
                        for m in range(C):
                            last = mm(view(2, T, LK - 1 - k, 1), l_t[:, m, k, :], col("v", m),
                                      start=(m == 0), stop=(m == C - 1))
                    last.then_inc(l_score, 1)
                elif step == L_BAND_T:
                    at(l_band, 1, 0)
                    tr(view(2, T, 0, T), l_a[:, :], T).then_inc(l_at_psum, 1)
                elif step == L_OUT:
                    at(l_at, 1, 0)
                    mm(view(2, T, 0, D), l_aT[:, :], txn[:, :], start=True, stop=True).then_inc(tsub_out, 1)
                elif step == M_XT:
                    normed_T(1)
                elif step == M_QUERY:
                    at(txt_ready, SUBS, 1)
                    for m in range(C):
                        for c in range(C):
                            last = mm(view(2, P, m * T, T), m_qk[:, c, m * P:(m + 1) * P], txnT[:, c, :],
                                      start=(c == 0), stop=(c == C - 1))
                    last.then_inc(g_psum, 1)
                elif step == M_SCORE:
                    at(g_ready, 1, 0)
                    for j in range(KTILES):
                        for c in range(C):
                            last = mm(view(2, KP, j * T, T), ctx_raw[:, c, j * KP:(j + 1) * KP], m_g[:, c, :],
                                      start=(c == 0), stop=(c == C - 1))
                    last.then_inc(ms_psum, 1)
                elif step == M_OUT:
                    at(ms_e, 1, 0)
                    for j in range(KTILES):
                        last = mm(view(2, T, 0, D), m_e[:, j, :], m_z[:, j, :], start=(j == 0), stop=(j == KTILES - 1))
                    last.then_inc(tsub_out, 1)
                elif step == C_XT:
                    normed_T(2)
                elif step == C_ROUTE:
                    at(txt_ready, SUBS, 2)
                    pe.wait_ge(w_c, 48)
                    for c in range(C):
                        last = mm(view(2, NE, 0, T), c_wr[:, c, :], txnT[:, c, :], start=(c == 0), stop=(c == C - 1))
                    last.then_inc(c_lg, 1)
                elif step == C_POS:
                    at(c_dg, 1, 0)
                    mm(view(2, T, 0, T), ones8[:, :], c_diag[:, 0].rearrange("p e j -> p (e j)"),
                       start=True, stop=True)
                    mm(view(2, T, T, 1), c_diag[:, 1].rearrange("p e j -> p (e j)"), ones8[:, 0:1],
                       start=True, stop=True).then_inc(c_rpsum, 1)
                elif step == C_GATHER:
                    at(c_hots, 1, 0)
                    for c in range(C):
                        mm(view(2, P, c * T, T), txn[:, c * P:(c + 1) * P], c_hot[:, :], start=True, stop=True)
                    for i in range(2):
                        lo = CONST["rope"][0] + i * ROT
                        mm(view(2, ROT, (C + i) * T, T), const[0:T, lo:lo + ROT], c_hot[:, :], start=True, stop=True)
                    mm(view(2, T, (C + 2) * T, 1), c_hot[:, :], col("iota", 0, 0, T), start=True, stop=True
                       ).then_inc(c_gpsum, 1)
                elif step in (C_QK, C_V):
                    if step == C_QK:
                        at(c_xg, 1, 0)
                        pe.wait_ge(wc_loaded, 16 * (B - 1) if isinstance(t, int) else t * 16 + 16)
                    for part in ((0, 1) if step == C_QK else (2,)):
                        for e in range(NE):
                            for c in range(C):
                                w = c_wqk[:, part * NE + e, c, :] if part < 2 else c_wv[:, e, c, :]
                                last = mm(view(2, P, part * T + e * TK, TK), w, c_xgT[:, c, e * TK:(e + 1) * TK],
                                          start=(c == 0), stop=(c == C - 1))
                    if step == C_QK:
                        last.then_inc(c_vq, 1)
                    else:
                        tr(view(2, T, 3 * T, T), c_hot[:, :], T).then_inc(c_qkv, 1)
                elif step == C_SCORE:
                    at(c_qk_ready, 1, 0)
                    tr(view(2, T, T, HP), c_vT[:, :], P)
                    mm(view(2, T, 0, T), c_qk[:, 0, :], c_qk[:, 1, :], start=True, stop=True).then_inc(c_spsum, 1)
                elif step == C_PROB_T:
                    at(c_en2, 1, 0)
                    tr(view(2, T, 0, T), c_e[:, :], T).then_inc(c_etp, 1)
                elif step == C_AV:
                    at(c_et, 1, 0)
                    mm(view(2, P, 0, T), c_v[:, :], c_eT[:, :], start=True, stop=True).then_inc(c_avp, 1)
                elif step == C_UP:
                    at(c_av, 1, 0)
                    for m in range(C):
                        for e in range(NE):
                            last = mm(view(2, P, m * T + e * TK, TK), c_wo[:, e, m * P:(m + 1) * P],
                                      c_avT[:, e * TK:(e + 1) * TK], start=True, stop=True)
                    last.then_inc(c_xpp, 1)
                elif step == C_UP_T:
                    at(c_xps, 1, 0)
                    for m in range(C):
                        last = tr(view(2, T, m * P, P), c_xpT[:, m, :], P)
                    last.then_inc(c_xqp, 1)
                elif step == C_OUT:
                    at(c_xqs, 1, 0)
                    mm(view(2, T, 0, D), c_hotT[:, :], c_xp[:, :], start=True, stop=True).then_inc(tsub_out, 1)

            pe.wait_ge(w_small, 48)
            pe.wait_ge(w_m, 64)
            for bk, l, r in ((1, mw_q, mw_k), (2, mw_v, mw_o)):
                for c in range(C):
                    for i in range(IT):
                        last = mm(bank[bk][:, c * D:(c + 1) * D], l[:, i, c * P:(c + 1) * P], r[:, i, :],
                                  start=(i == 0), stop=(i == IT - 1))
                last.then_inc(m_psum, 1)
            pe.wait_ge(consts_made, 1)
            pe.wait_ge(w_e, 80)
            for e in range(NE):
                for c in range(C):
                    last = mm(view(3, NE, 0, D), vb_cols[:, e, c, :], e_wo[:, e, c, :], start=(e == 0 and c == 0),
                              stop=(e == NE - 1 and c == C - 1))
            last.then_inc(bo_psum, 1)
            pe.wait_ge(m_made, 2)
            pe.wait_ge(bo_made, 1)

            front(0, None)
            with pe.Fori(1, B) as b:
                front(b, b - 1)
            for step in range(C_OUT + 1):
                tail_step(step, B - 1)

        @block.scalar
        def _(act):
            af = nc.scalar.activation

            def front(b, t):
                def at(s, per, k):
                    act.wait_ge(s, b * per + (k + 1))

                for c in range(C):
                    at(ctxt_psum, C, c)
                    af(ctxnT[:, c, :], bank[4 + c][:, 0:S], ACT.Identity, bias=col("ctx_b", c),
                       scale=col("ctx_w", c)).then_inc(ctxt_ready, 1)
                at(ret_g, 1, 0)
                af(eg[:, :, :], view(2, P, 0, C, T), ACT.Exp, scale=-1.0).then_inc(ret_eg, 1)
                at(ones_made, 1, 0)
                for n in range(NKV):
                    at(kv_psum, NKV, n)
                    bk = 6 + n % 2
                    if n < IT:
                        ins = af(x_kT[:, n, :], bank[bk][:, 0:S], ACT.Copy)
                    else:
                        j, half = (n - IT) // 2, (n - IT) % 2
                        ins = af(x_v[:, j, half * 8:half * 8 + 8, 0:XD], view(bk, KP, 0, 8, XD), ACT.Copy)
                    ins.then_inc(kv_ready, 1)

                for i in range(2):
                    at(xq_psum, 2, i)
                    af(x_qT[:, 4 * i:4 * i + 4, :], view(1 + i, P, 0, 4, T), ACT.Copy).then_inc(xq_ready, 1)
                for h in range(XH):
                    at(xs_psum, XH, h)
                    if h >= 3:
                        at(xs_pv, XH, h - 3)
                    af(x_p[:, h % 3], view(3 + h % 2, KP, 0, KTILES, T), ACT.Exp, scale=XD ** -0.5
                       ).then_inc(xs_exp, 1)
                for i in range(2):
                    at(xot_psum, 2, i)
                    af(x_oT[:, 4 * i:4 * i + 4, :], view(1 + i, P, 0, 4, T), ACT.Copy).then_inc(xot_ready, 1)

                for s in range(NE + 2):
                    if s < NE:
                        at(eqk_psum, NE, s)
                        at(eq_ready, NE, s)
                        for m in range(C):
                            for g in range(4):
                                q = slice(32 * g, 32 * g + 32)
                                ins = af(e_k[q, s % 2, m, g, :], bank[5][q, (C + m) * T:(C + m + 1) * T], ACT.Identity,
                                         bias=col("kb", s * C + m, 32 * g, 32 * g + 32))
                        ins.then_inc(ek_ready, 1)
                        at(evo_psum, NE + 2, s)
                        af(e_v[:, s % 2, :, 0:ED], view(6, T, 0, EH, ED), ACT.Copy).then_inc(ev_ready, 1)
                    if s >= 2:
                        at(evo_psum, NE + 2, s)
                        af(e_oT[:, :, :], view(6, P, D, C, T), ACT.Copy).then_inc(eot_ready, 1)
                    if s == 0:
                        at(r_ht_psum, 1, 0)
                        af(h1T[:, :], view(3, P, 0, T), ACT.Relu, bias=col("ffn_b"), scale=col("ffn_g")
                           ).then_inc(r_ht, 1)
                        at(r_nm, 1, 0)
                        af(pr[:, :], lg[:, :], ACT.Exp, bias=sc1[0:T, 0:1], accum_out=sc1[0:T, 1:2]
                           ).then_inc(r_exp, 1)
                    if 1 <= s <= NE:
                        for g in range(PER_SLOT):
                            if g < 4:
                                n = 4 * (s - 1) + g
                                at(est_psum, 4 * NE, n)
                                if n >= 2:
                                    at(epv, 4 * NE, n - 2)
                                af(e_p[:, g % 2], view(3 + g % 2, T, 0, 4, T), ACT.Exp, scale=ED ** -0.5
                                   ).then_inc(est_exp, 1)
                            if t is not None:
                                place = PER_SLOT * (s - 1) + g
                                if place < len(PLACES) and PLACES[place] is not None:
                                    tail_step(PLACES[place], t)

            def tail_step(step, t):
                def at(s, per, k):
                    act.wait_ge(s, t * per + (k + 1))

                if step in (L_Z, L_Z2):
                    i = step - L_Z
                    at(z_psum, 2, i)
                    lo, n = ((0, 2), (2, 1))[i]
                    af(m_z[:, lo:lo + n, :], view(2, KP, 0, n, D), ACT.Copy).then_inc(z_ready, 1)
                if step in (L_Z2, L_TANH):
                    m = step - L_Z2
                    at(l_sum, C, m)
                    af(l_t[:, m], l_t[:, m], ACT.Tanh).then_inc(l_tanh, 1)
                if step == L_SCORE:
                    at(l_nm, 1, 0)
                    af(l_w16[:, :], view(2, T, 0, LK), ACT.Exp, bias=sc1[0:T, 2:3], accum_out=sc1[0:T, 3:4]
                       ).then_inc(l_exp, 1)
                if step == M_SCORE:
                    at(ms_nm, 1, 0)
                    for j in range(KTILES):
                        af(m_e[:, j, :], view(2, KP, j * T, T), ACT.Exp, bias=m_nm[:, j:j + 1], scale=XD ** -0.5,
                           accum_out=m_sum[:, j:j + 1]).then_inc(ms_exp, 1)
                if step == C_ROUTE:
                    at(c_lg, 1, 0)
                    af(c_s[:, :], view(2, NE, 0, T), ACT.Exp, scale=-1.0).then_inc(c_en, 1)
                if step == C_SCORE:
                    at(c_nm, 1, 0)
                    af(c_e[:, :], c_pen[:, :], ACT.Exp, bias=sc1[0:T, 4:5], scale=HP ** -0.5,
                       accum_out=sc1[0:T, 5:6]).then_inc(c_exp, 1)

            act.wait_ge(w_small, 48)
            act.wait_ge(consts_made, 1)
            front(0, None)
            with act.Fori(1, B) as b:
                front(b, b - 1)
            for step in range(C_OUT + 1):
                tail_step(step, B - 1)

        @block.vector
        def _(dve):
            v = nc.vector
            count = [0]
            norms = [0, 0]
            before = [None]

            def alone():
                v.memset(idle[:, :], 0.0)

            def link(ins):
                count[0] += 1
                ins.then_inc(dve_done, 1)
                dve.wait_ge(dve_done, before[0](count[0]))

            def normalise_each(row, pairs, n, tail=False):
                k = len(pairs)
                st, mean, va, rs, ready, back, per = (
                    (tstats, tmv, tvar, trstd, tvar_ready, trstd_ready, TAIL_NORMS) if tail else
                    (stats, mv, var, rstd, var_ready, rstd_ready, FRONT_NORMS))
                for j, (_, src) in enumerate(pairs):
                    ins = v.bn_stats(st[0:n, j, :], src)
                link(ins)
                alone()
                for j in range(k):
                    ins = v.bn_aggr(mean[0:n, j, :], st[0:n, j, :])
                link(ins)
                v.tensor_scalar(va[0:n, 0:k], mean[0:n, 0:k, 1], EPS, None, ALU.add).then_inc(ready, 1)
                norms[tail] += 1
                dve.wait_ge(back, row * per + norms[tail])
                for j, (dst, src) in enumerate(pairs):
                    ins = v.tensor_scalar(dst, src, mean[0:n, j, 0:1], rs[0:n, j:j + 1], ALU.subtract, ALU.mult)
                return ins

            def front(b, t):
                def at(s, per, k):
                    dve.wait_ge(s, b * per + (k + 1))

                def normalise(dst, src, n):
                    return normalise_each(b, [(dst, src)], n)

                def xT_copy(s):
                    at(xt_psum, SUBS, s)
                    v.tensor_copy(xnT[:, :, :], view(0, P, 0, C, T)).then_inc(xt_ready, 1)

                def add_to_x(s, dst, bk, src):
                    at(sub_out, SUBS, s)
                    v.tensor_tensor(dst[:, :], src[:, :], view(bk, T, 0, D), ALU.add).then_inc(x_done, 1)
                    at(x_done, SUBS, s)

                norms[0] = 0
                dve.wait_ge(x_loaded, b * 16 + 16)
                normalise(xn[:, :], x_in[:, :], T).then_inc(xn_ready, 1)
                dve.wait_ge(ctx_loaded, b * 16 + 16)
                normalise_each(b, [(ctxn[:, j, :], ctx_tok[:, j, :]) for j in range(KTILES)], KP
                               ).then_inc(ctxn_ready, 1)
                xT_copy(0)
                v.memset(x_v[:, :, :, XD:XD + 1], 1.0).then_inc(ones_made, 1)
                at(ret_qv, 1, 0)
                for m in range(C):
                    ins = v.tensor_tensor_scan(state[:, m, :], col("lam", m).to_broadcast([P, T]),
                                               view(1, P, (C + m) * T, T), 0.0, ALU.mult, ALU.add)
                link(ins)
                v.tensor_tensor(yT[:, :, :], state[:, :, :], view(1, P, 0, C, T), ALU.mult).then_inc(ret_y, 1)
                at(ret_eg, 1, 0)
                link(v.tensor_scalar(eg[:, :, :], eg[:, :, :], 1.0, None, ALU.add))
                link(v.reciprocal(eg[:, :, :], eg[:, :, :]))
                v.tensor_tensor(gateT[:, :, :], eg[:, :, :], view(2, P, 0, C, T), ALU.mult)
                at(ret_yt, 1, 0)
                normalise(y2[:, :], view(3, T, 0, D), T).then_inc(ret_y2, 1)
                at(ret_y2t_psum, 1, 0)
                for m in range(C):
                    ins = v.tensor_scalar(y2T[:, m, :], view(0, P, m * T, T), col("ret_g", m), col("ret_b", m),
                                          ALU.mult, ALU.add)
                link(ins)
                v.tensor_tensor(y2T[:, :, :], y2T[:, :, :], gateT[:, :, :], ALU.mult).then_inc(ret_y2t, 1)
                add_to_x(0, x, 1, x_in)

                link(normalise(y2[:, :], x[:, :], T))
                normalise(xn[:, :], y2[:, :], T).then_inc(xn_ready, 1)
                link(v.tensor_tensor(x[:, :], x[:, :], row("bo"), ALU.add))
                at(xt_psum, SUBS, 1)
                for m in range(C):
                    ins = v.tensor_scalar(xnT[:, m, :], view(0, P, m * T, T), col("lat_w", m), col("lat_b", m),
                                          ALU.mult, ALU.add)
                ins.then_inc(xt_ready, 1)

                def x_norm(g):
                    at(xs_pv, XH, 4 * g + 3)
                    o = view(5 + g % 2, T, 0, 4, XD + 1)
                    link(v.reciprocal(x_rc[:, :, :], o[:, :, XD:XD + 1]))
                    v.tensor_tensor(x_o[:, g * 4 * XD:(g + 1) * 4 * XD].rearrange("p (h d) -> p h d", h=4),
                                    o[:, :, 0:XD], x_rc[:, :, :].to_broadcast([T, 4, XD]), ALU.mult
                                    ).then_inc(xo_ready, 1)

                for h in range(XH):
                    at(xs_exp, XH, h)
                    v.tensor_scalar(x_p[:, h % 3], x_p[:, h % 3], float(np.exp(CLIP)), float(np.exp(-CLIP)),
                                    ALU.min, ALU.max).then_inc(xs_clip, 1)
                    if h % 4 == 1 and h > 4:
                        x_norm(h // 4 - 1)
                x_norm(3)
                add_to_x(1, x, 0, x)

                normalise(xn[:, :], x[:, :], T).then_inc(xn_ready, 1)
                xT_copy(2)
                v.memset(e_v[:, :, :, ED:ED + 1], 1.0)
                at(r_h, 1, 0)
                link(v.tensor_tensor(h1[:, :], view(1, T, 0, R1), row("rb1"), ALU.add))
                normalise(h1[:, :], h1[:, :], T).then_inc(r_hn, 1)

                def queries(e):
                    at(eqk_psum, NE, e)
                    for m in range(C):
                        for o, keep in enumerate(("even", "odd")):
                            ins = v.tensor_scalar(e_q[:, e % 2, m, o, :], view(5, P, m * T, T), col("qb", e * C + m),
                                                  col(keep), ALU.add, ALU.mult)
                    ins.then_inc(eq_ready, 1)
                    at(eq_ready, NE, e)
                    v.tensor_copy(e_qb[:, :, :, :], e_q[:, e % 2])
                    at(ek_ready, NE, e)
                    v.tensor_copy(e_kb[:, :, :, :], e_k[:, e % 2]).then_inc(eb_ready, 1)

                def router_logits():
                    at(r_lg, 1, 0)
                    link(v.tensor_tensor(lg[:, :], view(4, T, 0, NE), row("rb2"), ALU.add))
                    v.tensor_reduce(sc1[0:T, 0:1], lg[:, :], AX.X, ALU.max, negate=True).then_inc(r_nm, 1)

                def router():
                    at(r_exp, 1, 0)
                    link(v.reciprocal(sc1[0:T, 1:2], sc1[0:T, 1:2]))
                    link(v.tensor_scalar(pr[:, :], pr[:, :], sc1[0:T, 1:2], None, ALU.mult))
                    alone()
                    link(v.max(top[:, :], pr[:, :]))
                    alone()
                    link(v.max_index(topi[:, :], top[:, :], pr[:, :]))
                    v.tensor_copy(topf[:, :], topi[:, :])
                    link(v.tensor_tensor(sc1[0:T, 6:7], top[:, 0:1], top[:, 1:2], ALU.add))
                    link(v.reciprocal(sc1[0:T, 6:7], sc1[0:T, 6:7]))
                    link(v.tensor_scalar(top[:, 0:2], top[:, 0:2], sc1[0:T, 6:7], None, ALU.mult))
                    for r in range(2):
                        ins = v.tensor_scalar(g01[:, r, :], const[0:T, CONST["iota8"][0]:CONST["iota8"][1]],
                                              topf[:, r:r + 1], top[:, r:r + 1], ALU.is_equal, ALU.mult)
                    link(ins)
                    v.tensor_tensor(gates[:, :], g01[:, 0, :], g01[:, 1, :], ALU.add).then_inc(r_gates, 1)
                    at(r_gates, 1, 0)

                def output(e):
                    at(epv, 4 * NE, 4 * e + 3)
                    o = view(7, T, 0, EH, ED + 1)
                    link(v.reciprocal(e_rc[:, :, :], o[:, :, ED:ED + 1]))
                    link(v.tensor_scalar(e_rc[:, :, :], e_rc[:, :, :], gates[:, e:e + 1], None, ALU.mult))
                    v.tensor_tensor(e_o[:, :, :], o[:, :, 0:ED], e_rc[:, :, :].to_broadcast([T, EH, ED]), ALU.mult
                                    ).then_inc(eo_ready, 1)

                for s in range(NE + 2):
                    if s >= 2:
                        output(s - 2)
                    if 1 <= s <= NE:
                        at(emt_psum, NE, s - 1)
                        v.tensor_copy(e_maxT[:, :], bank[7][:, 288:288 + T // 2].bitcast(BF16)).then_inc(emt_ready, 1)
                    if s < NE:
                        queries(s)
                    for g in range(PER_SLOT):
                        if g >= 1 and s < NE:
                            r = g - 1
                            at(es_psum, 4 * NE, 4 * s + r)
                            v.tensor_reduce(e_max[:, r, 0:4], view(1, T, 0, 4, T), AX.X, ALU.max
                                            ).then_inc(es_max, 1)
                        if s == 0 and g == 3:
                            router_logits()
                        if s == 0 and g == 4:
                            router()
                        if t is not None and 1 <= s <= NE:
                            place = PER_SLOT * (s - 1) + g
                            if place < len(PLACES) and PLACES[place] is not None:
                                tail_step(PLACES[place], t)
                at(r_gt_psum, 1, 0)
                v.tensor_copy(gatesT[:, :], view(3, NE, 0, T)).then_inc(r_gt, 1)
                add_to_x(2, tx, 0, x)

            def tail_step(step, t):
                def at(s, per, k):
                    dve.wait_ge(s, t * per + (k + 1))

                def norm_x(s):
                    normalise_each(t, [(txn[:, :], tx[:, :])], T, tail=True).then_inc(txn_ready, 1)

                def xT_copy(s):
                    at(txt_psum, SUBS, s)
                    v.tensor_copy(txnT[:, :, :], view(2, P, 0, C, T)).then_inc(txt_ready, 1)

                def add_to_x(s, dst):
                    at(tsub_out, SUBS, s)
                    v.tensor_tensor(dst[:, :], tx[:, :], view(2, T, 0, D), ALU.add).then_inc(tx_done, 1)
                    at(tx_done, SUBS, s)

                def local_sum(m):
                    v.tensor_tensor(l_t[:, m], windows(l_proj[:, m, :], (1, LK), (1, T)),
                                    windows(l_q[:, m, :], (0, LK), (1, T)), ALU.add).then_inc(l_sum, 1)

                if step == L_NORM:
                    norms[1] = 0
                    norm_x(0)
                elif step == L_XT:
                    xT_copy(0)
                elif step == L_PROJ:
                    at(l_psum, 1, 0)
                    v.tensor_copy(l_q[:, :, :], view(2, P, 0, C, T))
                    v.tensor_copy(l_proj[:, :, LPAD:LPAD + T], view(2, P, C * T, C, T)).then_inc(l_read, 1)
                    at(l_read, 1, 0)
                    local_sum(0)
                elif step == L_Z:
                    local_sum(1)
                elif step == L_SCORE:
                    at(l_score, 1, 0)
                    v.tensor_reduce(sc1[0:T, 2:3], view(2, T, 0, LK), AX.X, ALU.max, negate=True).then_inc(l_nm, 1)
                    at(l_exp, 1, 0)
                    link(v.reciprocal(sc1[0:T, 3:4], sc1[0:T, 3:4]))
                    link(v.tensor_scalar(l_w16[:, :], l_w16[:, :], sc1[0:T, 3:4], None, ALU.mult))
                    spread = l_t[0:T, 0].rearrange("p k t -> p (k t)").rearrange("p (t k) -> p t k", k=LK)
                    link(v.tensor_tensor(spread, windows(const[0:T, CONST["band"][0]:CONST["band"][1]],
                                                         (1, T), (1, LK)), windows(l_w16[:, :], (0, T), (1, LK)),
                                         ALU.mult))
                    v.tensor_reduce(l_a[:, :], spread, AX.X, ALU.add).then_inc(l_band, 1)
                elif step == L_BAND_T:
                    at(l_at_psum, 1, 0)
                    v.tensor_copy(l_aT[:, :], view(2, T, 0, T)).then_inc(l_at, 1)
                elif step == L_OUT:
                    add_to_x(0, tx)
                    norm_x(1)
                elif step == M_XT:
                    xT_copy(1)
                elif step == M_QUERY:
                    at(g_psum, 1, 0)
                    v.tensor_copy(m_g[:, :, :], view(2, P, 0, C, T)).then_inc(g_ready, 1)
                elif step == M_SCORE:
                    at(ms_psum, 1, 0)
                    link(v.tensor_reduce(m_nm[:, :], view(2, KP, 0, KTILES, T), AX.X, ALU.max, negate=True))
                    v.tensor_scalar(m_nm[:, :], m_nm[:, :], XD ** -0.5, None, ALU.mult).then_inc(ms_nm, 1)
                    at(ms_exp, KTILES, KTILES - 1)
                    link(v.reciprocal(m_sum[:, :], m_sum[:, :]))
                    v.tensor_tensor(m_e[:, :, :], m_e[:, :, :], windows(m_sum[:, :], (1, KTILES), (0, T)), ALU.mult
                                    ).then_inc(ms_e, 1)
                elif step == M_OUT:
                    add_to_x(1, tx)
                    norm_x(2)
                elif step == C_XT:
                    xT_copy(2)
                elif step == C_ROUTE:
                    at(c_en, 1, 0)
                    link(v.tensor_scalar(c_s[:, :], c_s[:, :], 1.0, None, ALU.add))
                    link(v.reciprocal(c_s[:, :], c_s[:, :]))
                    alone()
                    link(v.max(c_top[:, 0:8], c_s[:, :]))
                    alone()
                    v.max_index(c_idx[:, 0:8], c_top[:, 0:8], c_s[:, :])
                    link(v.match_replace(c_s2[:, :], c_top[:, 0:8], c_s[:, :], -1.0))
                    alone()
                    link(v.max(c_top[:, 8:16], c_s2[:, :]))
                    alone()
                    link(v.max_index(c_idx[:, 8:16], c_top[:, 8:16], c_s2[:, :]))
                    link(v.tensor_copy(c_idxf[:, :], c_idx[:, :]))
                    own = const[0:NE, CONST["own"][0]:CONST["own"][1]].rearrange("p (e j) -> p e j", e=NE)
                    v.tensor_tensor(c_diag[:, 0], own, windows(c_idxf[:, 0:TK], (0, NE), (1, TK)), ALU.mult)
                    v.tensor_tensor(c_diag[:, 1], own, windows(c_top[:, 0:TK], (0, NE), (1, TK)), ALU.mult
                                    ).then_inc(c_dg, 1)
                elif step == C_POS:
                    at(c_rpsum, 1, 0)
                    v.tensor_copy(c_iv[:, 0:1], view(2, T, T, 1))
                    link(v.tensor_copy(c_pos[:, :], view(2, T, 0, T)))
                    v.tensor_scalar(c_hot[:, :], c_pos[:, :], col("iota", 0, 0, T), None, ALU.is_equal
                                    ).then_inc(c_hots, 1)
                elif step == C_GATHER:
                    at(c_gpsum, 1, 0)
                    v.tensor_copy(c_cs[:, :, :], view(2, ROT, C * T, 2, T))
                    v.tensor_copy(c_iv[:, 1:2], view(2, T, (C + 2) * T, 1))
                    v.tensor_copy(c_xgT[:, :, :], view(2, P, 0, C, T)).then_inc(c_xg, 1)
                    at(c_xg, 1, 0)
                    link(v.tensor_scalar(c_pen[:, :], c_pos[:, :], c_iv[:, 1:2], None, ALU.is_le))
                    link(v.tensor_tensor(c_pen[:, :], c_pen[:, :], const[0:T, CONST["block"][0]:CONST["block"][1]],
                                         ALU.mult))
                    link(v.tensor_scalar(c_pen[:, :], c_pen[:, :], 1e30, -1e30, ALU.mult, ALU.add))
                elif step == C_V:
                    at(c_qkv, 1, 0)
                    v.tensor_copy(c_vT[:, :], view(2, P, 2 * T, T))
                    v.tensor_copy(c_hotT[:, :], view(2, T, 3 * T, T))
                    link(v.tensor_copy(c_qk[:, :, :], view(2, P, 0, 2, T)))
                    half = ROT // 2
                    for lo, to in ((0, half), (half, 0)):
                        ins = v.tensor_tensor(c_rot[to:to + half], c_qk[lo:lo + half],
                                              windows(c_cs[lo:lo + half, 1, :], (0, 2), (1, T)), ALU.mult)
                    link(ins)
                    link(v.tensor_tensor(c_qk[0:ROT], c_qk[0:ROT], windows(c_cs[:, 0, :], (0, 2), (1, T)), ALU.mult))
                    v.tensor_tensor(c_qk[0:ROT], c_qk[0:ROT], c_rot[:, :, :], ALU.add).then_inc(c_qk_ready, 1)
                elif step == C_SCORE:
                    at(c_spsum, 1, 0)
                    v.tensor_copy(c_v[:, :], view(2, T, T, HP))
                    link(v.tensor_tensor(c_pen[:, :], c_pen[:, :], view(2, T, 0, T), ALU.add))
                    link(v.tensor_reduce(sc1[0:T, 4:5], c_pen[:, :], AX.X, ALU.max, negate=True))
                    v.tensor_scalar(sc1[0:T, 4:5], sc1[0:T, 4:5], HP ** -0.5, None, ALU.mult).then_inc(c_nm, 1)
                    at(c_exp, 1, 0)
                    link(v.reciprocal(sc1[0:T, 5:6], sc1[0:T, 5:6]))
                    v.tensor_scalar(c_e[:, :], c_e[:, :], sc1[0:T, 5:6], c_iv[:, 0:1], ALU.mult, ALU.mult
                                    ).then_inc(c_en2, 1)
                elif step == C_PROB_T:
                    at(c_etp, 1, 0)
                    v.tensor_copy(c_eT[:, :], view(2, T, 0, T)).then_inc(c_et, 1)
                elif step == C_AV:
                    at(c_avp, 1, 0)
                    v.tensor_copy(c_avT[:, :], view(2, P, 0, T)).then_inc(c_av, 1)
                elif step == C_UP:
                    at(c_xpp, 1, 0)
                    v.tensor_copy(c_xpT[:, :, :], view(2, P, 0, C, T)).then_inc(c_xps, 1)
                elif step == C_UP_T:
                    at(c_xqp, 1, 0)
                    v.tensor_copy(c_xp[:, :], view(2, T, 0, D)).then_inc(c_xqs, 1)
                elif step == C_OUT:
                    at(x_out_free, 1, 0)
                    add_to_x(2, x_out)

            dve.wait_ge(w_small, 48)
            v.tensor_copy(ident_b[:, :], ident)
            for r in range(4):
                for g in range(4):
                    v.tensor_scalar(sel_b[:, r, g, :], windows(ident[:, 32 * r + g:32 * r + g + 1], (0, T)), -1.0, None,
                                    ALU.mult)
            v.memset(e_max[:, :, :], 0.0)
            v.memset(e_k[:, :, :, :, :], 0.0)
            v.memset(l_proj[:, :, :], 0.0)
            v.memset(ones8[:, :], 1.0)
            v.memset(vb_cols, 0.0).then_inc(dve_set, 1)
            dve.wait_ge(dve_set, 1)
            for e in range(NE):
                ins = v.tensor_copy(vb_cols[:, e, :, e], cols[:, COLS["vb"] + e * C:COLS["vb"] + (e + 1) * C])
            ins.then_inc(consts_made, 1)
            for i, m in enumerate((m_qk, m_vo)):
                dve.wait_ge(m_psum, i + 1)
                v.tensor_copy(m[:, :, :], bank[1 + i][:, :].rearrange("p (c n) -> p c n", c=C)).then_inc(m_made, 1)
            dve.wait_ge(bo_psum, 1)
            v.tensor_tensor(e_bo_all[:, :], e_bo[:, :], view(3, NE, 0, D), ALU.add).then_inc(bo_made, 1)
            dve.wait_ge(consts_made, 1)

            both = FRONT_STEPS + TAIL_STEPS
            before[0] = lambda n: n
            front(0, None)
            assert (count[0], norms[0]) == (FRONT_STEPS, FRONT_NORMS), (count[0], norms[0])
            count[0] = 0
            with dve.Fori(1, B) as b:
                before[0] = lambda n: b * both + (n - TAIL_STEPS)
                front(b, b - 1)
                assert (count[0], norms[1]) == (both, TAIL_NORMS), (count[0], norms[1])
            count[0] = 0
            before[0] = lambda n: B * both + (n - TAIL_STEPS)
            for step in range(C_OUT + 1):
                tail_step(step, B - 1)


def rope_tables():
    half = ROT // 2
    inv = (np.float32(1.0) / np.power(np.float32(10000.0), np.arange(half, dtype=np.float32) * np.float32(2.0)
                                      / np.float32(ROT))).astype(np.float32)
    ang = (np.arange(T, dtype=np.float32)[:, None] * inv).astype(np.float32)
    sin, cos = np.sin(ang).astype(np.float32), np.cos(ang).astype(np.float32)
    return np.concatenate([cos, cos, sin, -sin], axis=1)


def const_table():
    c = np.zeros((P, NCONST), np.float32)

    def part(name):
        lo, hi = CONST[name]
        return c[:, lo:hi]

    part("ident")[:] = np.eye(P)
    for t in range(T):
        if t + LK - 1 - LPAD < T + LK - 1:
            part("band")[t, t + LK - 1 - LPAD] = 1.0
    for e in range(NE):
        part("own")[e, e * TK:(e + 1) * TK] = 1.0
        part("block")[e * TK:(e + 1) * TK, e * TK:(e + 1) * TK] = 1.0
    part("rope")[:T] = rope_tables()
    part("iota8")[:] = np.arange(NE)
    return c


def tiles(v):
    return v.reshape(-1, P).T


def kernel(**inputs):
    import concourse.bacc as bacc
    from concourse.bass_utils import run_bass_kernel_spmd

    i = {k: np.asarray(v) for k, v in inputs.items()}
    cols = np.zeros((P, NCOLS), np.float32)
    parts = np.arange(P)
    for name, v in (("lat_w", i["L0_xattn_ln_l_w"]), ("lat_b", i["L0_xattn_ln_l_b"]), ("ctx_w", i["L0_xattn_ln_c_w"]),
                    ("ctx_b", i["L0_xattn_ln_c_b"]), ("qb", i["L0_ffn_qb"].reshape(-1)),
                    ("kb", i["L0_ffn_kb"].reshape(-1)), ("vb", i["L0_ffn_vb"].reshape(-1)),
                    ("ret_g", i["L0_attn_ln_g"]), ("ret_b", i["L0_attn_ln_b"]), ("ffn_g", i["L0_ffn_ln_g"]),
                    ("ffn_b", i["L0_ffn_ln_b"]),
                    ("lam", np.repeat(i["L0_attn_decay"][:, 1, 0], D // 16)),
                    ("v", i["L1_attn_v"][:, 0]), ("iota", parts), ("even", parts // ED % 2 == 0),
                    ("odd", parts // ED % 2 == 1)):
        t = tiles(v)
        cols[:, COLS[name]:COLS[name] + t.shape[1]] = t
    rows = np.concatenate([i[k].reshape(-1) for k in ("L0_xattn_bo", "L0_ffn_rb1", "L0_ffn_rb2")])
    arrays = {
        "x": i["x"], "ctx": i["ctx_1024"], "ctxT": i["ctx_1024"].transpose(0, 2, 1),
        "cols": cols, "rows": rows, "const": const_table(),
        "ret_q": i["L0_attn_Wq"].T, "ret_v": i["L0_attn_Wv"].T, "ret_g": i["L0_attn_Wg"].T, "ret_o": i["L0_attn_Wo"].T,
        "x_q": i["L0_xattn_Wq"], "x_kv": i["L0_xattn_Wkv"], "x_o": i["L0_xattn_Wo"],
        "r_w1": i["L0_ffn_rW1"].T, "r_w2": i["L0_ffn_rW2"].T, "e_bo": i["L0_ffn_ob"],
        "e_q": i["L0_ffn_qW"].transpose(0, 2, 1), "e_k": i["L0_ffn_kW"].transpose(0, 2, 1),
        "e_v": i["L0_ffn_vW"].transpose(0, 2, 1), "e_o": i["L0_ffn_oW"].transpose(0, 2, 1),
        "l_w1": i["L1_attn_w1"], "l_w2": i["L1_attn_w2"],
        "m_q": i["L1_xattn_Wq"].T, "m_k": i["L1_xattn_Wk"].T, "m_v": i["L1_xattn_Wv"].T, "m_o": i["L1_xattn_Wo"],
        "c_r": i["L1_ffn_Wr"].T, 
        "c_qk": i["L1_ffn_Wqkv"][:, :, :2 * HP].reshape(NE, D, 2, HP).transpose(2, 0, 1, 3).reshape(2 * NE, D, HP),
        "c_v": i["L1_ffn_Wqkv"][:, :, 2 * HP:], "c_o": i["L1_ffn_Wo"],
    }
    for k, v in arrays.items():
        if k not in ("x", "ctx", "ctxT", "cols", "rows", "const", "r_w2", "e_bo"):
            v = v.reshape(*v.shape[:-2], -1, P, v.shape[-1])
            arrays[k] = np.moveaxis(v, -2, 0)
    arrays["c_o"] = arrays["c_o"][:, :, 0]
    arrays = {f"in_{k}": np.ascontiguousarray(v) for k, v in arrays.items()}
    nc = bacc.Bacc("TRN2", target_bir_lowering=False, num_devices=1)
    aps = {k[3:]: nc.dram_tensor(k, v.shape, mybir.dt.from_np(v.dtype), kind="ExternalInput").ap()
           for k, v in arrays.items()}
    out = nc.dram_tensor("out", (B, T, D), F32, kind="ExternalOutput").ap()
    build(nc, aps, out)
    r = run_bass_kernel_spmd(nc, [arrays], core_ids=[0])
    return r.results[0]["out"]
```

```python
from contextlib import ExitStack

import numpy as np
import concourse.bass as bass
from concourse import mybir

F32 = mybir.dt.float32
BF16 = mybir.dt.bfloat16
U32 = mybir.dt.uint32
ALU = mybir.AluOpType
ACT = mybir.ActivationFunctionType
AX = mybir.AxisListType

B, T, D = 8, 112, 256
S, KP = 375, 125
KTILES = S // KP
P = 128
C = D // P
XH, XD = 16, 64
INNER = XH * XD
IT = INNER // P
NE = 8
EH, ED = 16, 16
R1 = 128
LK, LPAD = 16, 7
TK = max(T // 8, 2)
HP = 128
ROT = 64
EPS = 1e-5
CLIP = 11.0
SUBS = 3
FRONT_NORMS, TAIL_NORMS = 7, 3
PREPARED = 2
FRONT_STEPS, TAIL_STEPS = 50, 27
FIRST_STEPS = 4
REGION = 9984

TANH_STEPS, L_STEPS, QKV_STEPS, UP_STEPS = 4, 4, 12, 4
L_NORM, L_XT, L_PROJ, L_Z, L_Z2, L_TANH = range(6)
L_SCALE, L_MIX, L_MIX2, L_SCORE = range(L_TANH + TANH_STEPS, L_TANH + TANH_STEPS + 4)
L_SCORED = L_SCORE + L_STEPS - 1
(L_BAND, L_BAND2, L_BAND_T, L_OUT, M_XT, M_QUERY, M_SCORE, M_EXP, M_NORM, M_OUT, C_XT, C_ROUTE, C_ROUTE2, C_ROUTE3,
 C_POS, C_GATHER, C_QKV) = range(L_SCORED + 1, L_SCORED + 18)
C_QKVED = C_QKV + QKV_STEPS - 1
C_SCORE, C_EXP, C_NORM, C_PROB_T, C_AV, C_UP = range(C_QKVED + 1, C_QKVED + 7)
C_UPPED = C_UP + UP_STEPS - 1
C_UP_T, C_OUT = C_UPPED + 1, C_UPPED + 2
GROUPS = 5
PER_SLOT = GROUPS + 1
PLACES = [
    (L_Z,), (), (L_Z2,), (L_TANH,), (L_TANH + 1,), (L_TANH + 2,),
    (L_TANH + 3,), (L_SCALE,), (L_MIX,), (L_MIX2,), (L_SCORE,), (L_SCORE + 1,),
    (L_SCORE + 2,), (L_SCORE + 3,), (), (), (L_BAND,), (L_BAND2,),
    (L_BAND_T,), (), (L_OUT,), (), (M_XT,), (M_QUERY,),
    (M_SCORE,), (M_EXP, M_NORM), (M_OUT,), (), (C_XT,), (C_ROUTE,),
    (C_ROUTE2,), (C_ROUTE3,), (), (C_POS,), (C_GATHER,), (C_QKV,),
    (C_QKV + 1, C_QKV + 2), (C_QKV + 3,), (C_QKV + 4,), (C_QKV + 5,), (C_QKV + 6,), (C_QKV + 7,),
    (C_QKV + 8, C_QKV + 9), (C_QKV + 10,), (C_QKV + 11,), (), (C_SCORE,), (C_EXP,),
    (C_NORM,), (C_PROB_T,), (C_AV,), (C_UP, C_UP + 1), (C_UP + 2, C_UP + 3), (C_UP_T,),
    (C_OUT,), (), (), (), (), ()]
SETUP_BIAS, SETUP_QK, SETUP_VO = range(3)
SETUP_PLACES = {2: SETUP_BIAS, 2 * PER_SLOT + 1: SETUP_QK, 5 * PER_SLOT + 1: SETUP_VO}

COLS = {}
_n = 0
for _name, _w in (("lat_w", C), ("lat_b", C), ("ctx_w", C), ("ctx_b", C), ("qb", NE * C), ("kb", NE * C),
                  ("vb", NE * C),
                  ("ret_g", C), ("ret_b", C), ("ffn_g", 1), ("ffn_b", 1),
                  ("lam", C), ("v", C), ("iota", 1), ("even", 1), ("odd", 1), ("one", 1)):
    COLS[_name] = _n
    _n += _w
NCOLS = _n
ROWS = {}
_n = 0
for _name, _w in (("bo", D), ("rb1", R1), ("rb2", NE)):
    ROWS[_name] = (_n, _n + _w)
    _n += _w
NROWS = _n
CONST = {}
_n = 0
for _name, _w in (("ident", P), ("band", T + LK - 1), ("own", NE * TK), ("block", NE * TK), ("rope", 2 * ROT),
                  ("iota8", NE)):
    CONST[_name] = (_n, _n + _w)
    _n += _w
NCONST = _n




def build(nc, a, out):
    with ExitStack() as ctx:
        def sb(name, shape, dt=F32):
            return ctx.enter_context(nc.sbuf_tensor(name, shape, dt))

        def sem(name):
            return ctx.enter_context(nc.semaphore(name))

        bank = [ctx.enter_context(nc.psum_tensor(f"bank{i}", [P, 512], F32)) for i in range(8)]

        ret_w = sb("ret_w", [P, 4, C, D])
        turns_w = sb("turns_w", [P, 2 * C * INNER])
        x_wq = turns_w[:, 0:C * INNER].rearrange("p (c n) -> p c n", c=C)
        x_wo = turns_w[:, C * INNER:].rearrange("p (i n) -> p i n", i=IT)
        c_wqk = turns_w[:, :].rearrange("p (q c n) -> p q c n", q=2 * NE, c=C)
        x_wkv = sb("x_wkv", [P, C, 2 * INNER])
        r_w1 = sb("r_w1", [P, C, R1])
        r_w2 = sb("r_w2", [P, NE])
        e_wq = sb("e_wq", [P, NE, C, D])
        e_wk = sb("e_wk", [P, NE, C, D])
        e_wv = sb("e_wv", [P, NE, C, D])
        e_wo = sb("e_wo", [P, NE, C, D])
        e_bo = sb("e_bo", [NE, D])
        l_w = sb("l_w", [P, 2, C, D])
        m_qk = sb("m_qk", [P, C, D])
        m_vo = sb("m_vo", [P, C, D])
        c_wr = sb("c_wr", [P, C, NE])
        c_wv = sb("c_wv", [P, NE, C, HP])
        c_wo = sb("c_wo", [P, NE, D])
        cols = sb("cols", [P, NCOLS])
        rows = sb("rows", [P, NROWS])
        const = sb("const", [P, NCONST])
        ident_b = sb("ident_b", [P, P], BF16)
        sel_b = sb("sel_b", [P, 4, 4, T], BF16)
        e_bo_all = sb("e_bo_all", [NE, D])
        mw_l = c_wv[:, :, :, :].rearrange("p e c n -> p (e c n)").rearrange("p (i d) -> p i d", i=IT)
        mw_r = c_wo[:, :, :]

        x_in = sb("x_in", [T, D])
        x = sb("x", [T, D])
        x_out = sb("x_out", [T, D])
        xn = sb("xn", [T, D])
        xnT = sb("xnT", [P, C, T])
        stats = sb("stats", [P, KTILES, 6])
        mv = sb("mv", [P, KTILES, 2])
        var = sb("var", [P, KTILES])
        rstd = sb("rstd", [P, KTILES])
        tx = sb("tx", [T, D])
        txn = sb("txn", [T, D])
        txnT = sb("txnT", [P, C, T])
        tstats = sb("tstats", [P, 1, 6])
        tmv = sb("tmv", [P, 1, 2])
        tvar = sb("tvar", [P, 1])
        trstd = sb("trstd", [P, 1])
        minus_half = sb("minus_half", [P, KTILES])
        ctx_tok = sb("ctx_tok", [KP, KTILES, D])
        ctx_raw = sb("ctx_raw", [P, C, S])
        ctxnT = sb("ctxnT", [P, C, S])
        ctxn = sb("ctxn", [KP, KTILES, D])
        region = sb("region", [P, REGION])

        def at_word(lo, n, *dims, dt=F32):
            size = int(np.prod(dims))
            if dt == BF16:
                v = region[0:n, lo:lo + (size + 1) // 2].bitcast(BF16)
            elif dt == U32:
                v = region[0:n, lo:lo + size].bitcast(U32)
            else:
                v = region[0:n, lo:lo + size]
            spent[0] = lo + (size if dt != BF16 else (size + 1) // 2)
            tops.append(spent[0])
            names = "abcd"[:len(dims)]
            if len(dims) == 1:
                return v
            return v.rearrange("p (" + " ".join(names) + ") -> p " + " ".join(names),
                               **{k: d for k, d in zip(names, dims)})

        spent, tops = [0], []

        def then(n, *dims, dt=F32):
            return at_word(spent[0], n, *dims, dt=dt)

        x_kT = at_word(REGION - IT * S, P, IT, S)
        x_v = at_word(0, KP, KTILES, XH, XD + 1)
        after_values = spent[0]
        state = at_word(after_values, P, C, T)
        yT = then(P, C, T)
        gateT = then(P, C, T)
        eg = then(P, C, T)
        y2 = then(T, D)
        y2T = then(P, C, T)
        x_o = at_word(after_values, T, INNER)
        x_qT = then(P, IT, T)
        x_p = then(KP, 3, KTILES, T)
        x_oT = then(P, IT, T)
        assert spent[0] <= REGION - IT * S
        x_rc = sb("x_rc", [T, 4, 1])
        e_k = sb("e_k", [P, 2, C, 4, T])
        e_max = sb("e_max", [T, 4, 32], BF16)
        h1 = at_word(0, T, R1)
        h1T = then(P, T)
        lg = then(T, NE)
        pr = then(T, NE)
        top = then(T, 8)
        topi = then(T, 8, dt=U32)
        topf = then(T, 8)
        g01 = then(T, 2, NE)
        gates = then(T, NE)
        gatesT = then(NE, T)
        e_q = then(P, 2, C * 2 * T).rearrange("p e (c o t) -> p e c o t", c=C, o=2)
        e_qb = then(P, C, 2, T, dt=BF16)
        e_kb = then(P, C, 4, T, dt=BF16)
        e_maxT = then(P, T, dt=BF16)
        e_p = then(T, 2, 4, T)
        e_v = then(T, 2, EH, ED + 1)
        e_rc = then(T, EH, 1)
        e_o = then(T, EH, ED)
        e_oT = then(P, C, T)
        after_experts = spent[0]
        l_proj = sb("l_proj", [P, C, T + LK - 1])
        l_t = at_word(after_experts, P, C, LK, T)
        l_q = then(P, C, T)
        spread = l_t[0:T, 0].rearrange("p k t -> p (k t)").rearrange("p (t k) -> p t k", k=LK)
        l_w16 = then(T, LK)
        l_a = then(T, T)
        l_aT = then(T, T)
        m_z = then(KP, KTILES, D)
        m_g = at_word(after_experts, P, C, T)
        m_e = then(KP, KTILES, T)
        m_nm = then(KP, KTILES)
        m_sum = then(KP, KTILES)
        c_hotT = at_word(after_experts, T, T)
        c_iv = then(T, 2)
        c_v = then(T, HP)
        c_pen = then(T, T)
        c_e = then(T, T)
        c_eT = then(T, T)
        c_avT = then(P, T)
        c_xpT = then(P, C, T)
        c_xp = then(T, D)
        assert spent[0] <= REGION - IT * S
        c_s = then(NE, T)
        c_s2 = then(NE, T)
        c_top = then(NE, 16)
        c_idx = then(NE, 16, dt=U32)
        c_idxf = then(NE, 16)
        c_diag = then(NE, 2, NE, TK)
        c_pos = then(T, T)
        c_hot = then(T, T)
        c_cs = then(ROT, 2, T)
        c_xgT = then(P, C, T)
        c_qk = then(P, 2, T)
        c_rot = then(ROT, 2, T)
        c_vT = then(P, T)
        sc1 = sb("sc1", [P, 16])
        pool_idle = sb("pool_idle", [1, 1])
        idle = sb("idle", [1, 1])
        ones8 = sb("ones8", [NE, T])
        vb_cols = sb("vb_cols", [P, NE, C, NE])

        def cst(name):
            lo, hi = CONST[name]
            return const[:, lo:hi]

        def row(name, n=T, at=0, width=None):
            lo, hi = ROWS[name]
            return rows[0:n, lo + at:(lo + at + width) if width else hi]

        def col(name, k=0, lo=0, hi=P):
            return cols[lo:hi, COLS[name] + k:COLS[name] + k + 1]

        ident = cst("ident")

        def view(bk, n, lo, *dims):
            size = int(np.prod(dims))
            v = bank[bk][0:n, lo:lo + size]
            if len(dims) == 1:
                return v
            names = "abc"[:len(dims)]
            return v.rearrange("p (" + " ".join(names) + ") -> p " + " ".join(names),
                               **{k: d for k, d in zip(names, dims)})

        def windows(ap, *dims):
            return bass.AP(ap.tensor, ap.offset, [ap.ap[0]] + [list(d) for d in dims])

        w_small = sem("w_small")
        w_ret = sem("w_ret")
        w_x = sem("w_x")
        wx_loaded = sem("wx_loaded")
        wc_loaded = sem("wc_loaded")
        w_e = sem("w_e")
        w_eqk = sem("w_eqk")
        w_l = sem("w_l")
        w_mqk = sem("w_mqk")
        w_mvo = sem("w_mvo")
        zeros_made = sem("zeros_made")
        ones_made = sem("ones_made")
        eb_ready = sem("eb_ready")
        c_vq = sem("c_vq")
        w_c = sem("w_c")
        consts_made = sem("consts_made")
        m_psum = sem("m_psum")
        m_made = sem("m_made")
        half_made = sem("half_made")
        x_out_free = sem("x_out_free")
        x_loaded = sem("x_loaded")
        ctx_loaded = sem("ctx_loaded")
        raw_loaded = sem("raw_loaded")
        out_stored = sem("out_stored")
        dve_done = sem("dve_done")
        var_ready = sem("var_ready")
        rstd_ready = sem("rstd_ready")
        tvar_ready = sem("tvar_ready")
        trstd_ready = sem("trstd_ready")
        xn_ready = sem("xn_ready")
        xt_psum = sem("xt_psum")
        xt_ready = sem("xt_ready")
        sub_out = sem("sub_out")
        x_done = sem("x_done")
        txn_ready = sem("txn_ready")
        txt_psum = sem("txt_psum")
        txt_ready = sem("txt_ready")
        tsub_out = sem("tsub_out")
        tx_done = sem("tx_done")
        ctxn_ready = sem("ctxn_ready")
        ctxt_psum = sem("ctxt_psum")
        ctxt_ready = sem("ctxt_ready")
        kv_psum = sem("kv_psum")
        kv_ready = sem("kv_ready")
        ret_qv = sem("ret_qv")
        ret_g = sem("ret_g")
        ret_eg = sem("ret_eg")
        ret_y = sem("ret_y")
        ret_yt = sem("ret_yt")
        ret_y2 = sem("ret_y2")
        ret_y2t_psum = sem("ret_y2t_psum")
        ret_y2t = sem("ret_y2t")
        xq_psum = sem("xq_psum")
        xq_ready = sem("xq_ready")
        xs_psum = sem("xs_psum")
        xs_exp = sem("xs_exp")
        xs_clip = sem("xs_clip")
        xs_pv = sem("xs_pv")
        xo_ready = sem("xo_ready")
        xot_psum = sem("xot_psum")
        xot_ready = sem("xot_ready")
        r_h = sem("r_h")
        r_hn = sem("r_hn")
        r_ht_psum = sem("r_ht_psum")
        r_ht = sem("r_ht")
        r_lg = sem("r_lg")
        r_nm = sem("r_nm")
        bo_psum = sem("bo_psum")
        bo_made = sem("bo_made")
        r_exp = sem("r_exp")
        r_gates = sem("r_gates")
        r_gt_psum = sem("r_gt_psum")
        r_gt = sem("r_gt")
        ek_psum = sem("ek_psum")
        eqv_psum = sem("eqv_psum")
        eot_psum = sem("eot_psum")
        eq_ready = sem("eq_ready")
        ek_ready = sem("ek_ready")
        ev_ready = sem("ev_ready")
        es_psum = sem("es_psum")
        es_max = sem("es_max")
        emt_psum = sem("emt_psum")
        emt_ready = sem("emt_ready")
        est_psum = sem("est_psum")
        est_exp = sem("est_exp")
        epv = sem("epv")
        eo_ready = sem("eo_ready")
        eot_ready = sem("eot_ready")
        l_psum = sem("l_psum")
        l_sum = sem("l_sum")
        l_tanh = sem("l_tanh")
        l_mixed = sem("l_mixed")
        l_score = sem("l_score")
        l_soft = sem("l_soft")
        l_spread = sem("l_spread")
        l_nm = sem("l_nm")
        l_exp = sem("l_exp")
        l_band = sem("l_band")
        l_at_psum = sem("l_at_psum")
        l_at = sem("l_at")
        z_psum = sem("z_psum")
        z_ready = sem("z_ready")
        g_psum = sem("g_psum")
        g_ready = sem("g_ready")
        ms_psum = sem("ms_psum")
        ms_nm = sem("ms_nm")
        ms_exp = sem("ms_exp")
        ms_e = sem("ms_e")
        c_lg = sem("c_lg")
        c_en = sem("c_en")
        c_dg = sem("c_dg")
        c_rpsum = sem("c_rpsum")
        c_hots = sem("c_hots")
        c_gpsum = sem("c_gpsum")
        c_xg = sem("c_xg")
        c_qkv = sem("c_qkv")
        c_qk_ready = sem("c_qk_ready")
        l_read = sem("l_read")
        c_spsum = sem("c_spsum")
        c_nm = sem("c_nm")
        c_exp = sem("c_exp")
        c_en2 = sem("c_en2")
        c_etp = sem("c_etp")
        c_et = sem("c_et")
        c_avp = sem("c_avp")
        c_av = sem("c_av")
        c_xpp = sem("c_xpp")
        c_xps = sem("c_xps")
        c_xqp = sem("c_xqp")
        c_xqs = sem("c_xqs")

        NKV = IT + 2 * KTILES

        def kv_bank(n):
            return (5 if n < IT else 6) + n % 2

        def keys_after(s, g):
            if s == NE and 1 <= g <= 3:
                return (2 * g - 2, 2 * g - 1)
            return (IT - 2,) if (s, g) == (NE, 4) else ()

        assert max(tops) <= REGION
        block = ctx.enter_context(nc.Block())

        @block.sync
        def _(sp):
            sp.dma_start(ctx_tok[:, :, :], a["ctx"][0].rearrange("(j p) d -> p j d", p=KP)).then_inc(ctx_loaded, 16)
            sp.dma_start(const[:, :], a["const"]).then_inc(w_small, 16)
            sp.dma_start(cols[:, :], a["cols"]).then_inc(w_small, 16)
            sp.dma_start(x_in[:, :], a["x"][0]).then_inc(x_loaded, 16)
            sp.dma_start(rows[:, :], a["rows"].partition_broadcast(P)).then_inc(w_small, 16)
            for i, name in enumerate(("ret_q", "ret_v", "ret_g", "ret_o")):
                sp.dma_start(ret_w[:, i], a[name]).then_inc(w_ret, 16)
            sp.dma_start(x_wkv[:, :, :], a["x_kv"]).then_inc(w_x, 16)
            sp.dma_start(x_wq, a["x_q"]).then_inc(wx_loaded, 16)
            sp.dma_start(x_wo, a["x_o"]).then_inc(wx_loaded, 16)
            sp.dma_start(r_w1[:, :, :], a["r_w1"]).then_inc(w_e, 16)
            sp.dma_start(r_w2[:, :], a["r_w2"]).then_inc(w_e, 16)
            sp.dma_start(e_bo[:, :], a["e_bo"]).then_inc(w_e, 16)
            sp.dma_start(e_wk[:, :, :, :], a["e_k"]).then_inc(w_eqk, 16)
            sp.dma_start(e_wq[:, :, :, :], a["e_q"]).then_inc(w_eqk, 16)
            sp.dma_start(e_wv[:, :, :, :], a["e_v"]).then_inc(w_e, 16)
            sp.dma_start(e_wo[:, :, :, :], a["e_o"]).then_inc(w_e, 16)
            sp.dma_start(mw_l, a["m_q"]).then_inc(w_mqk, 16)
            sp.dma_start(mw_r, a["m_k"]).then_inc(w_mqk, 16)
            sp.dma_start(ctx_raw[:, :, :], a["ctxT"][0].rearrange("(c p) k -> p c k", p=P)).then_inc(raw_loaded, 16)
            sp.dma_start(l_w[:, 0], a["l_w1"]).then_inc(w_l, 16)
            sp.dma_start(l_w[:, 1], a["l_w2"]).then_inc(w_l, 16)
            sp.dma_start(c_wr[:, :, :], a["c_r"]).then_inc(w_c, 16)
            def load_inputs(b):
                sp.wait_ge(x_done, b * SUBS + 1)
                sp.dma_start(x_in[:, :], a["x"][bass.ds(b + 1, 1)].rearrange("a t d -> (a t) d")).then_inc(x_loaded, 16)
                sp.wait_ge(ctxn_ready, b + 1)
                sp.dma_start(ctx_tok[:, :, :], a["ctx"][bass.ds(b + 1, 1)].rearrange("a (j p) d -> p (a j) d", p=KP)
                             ).then_inc(ctx_loaded, 16)

            def load_for_tail(b):
                sp.wait_ge(sub_out, b * SUBS + 2)
                sp.dma_start(c_wqk, a["c_qk"]).then_inc(wc_loaded, 16)
                sp.wait_ge(ms_psum, b)
                sp.dma_start(ctx_raw[:, :, :], a["ctxT"][bass.ds(b, 1)].rearrange("a (c p) k -> p (a c) k", p=P)
                             ).then_inc(raw_loaded, 16)

            load_inputs(0)
            sp.wait_ge(m_made, 1)
            sp.dma_start(mw_l, a["m_v"]).then_inc(w_mvo, 16)
            sp.dma_start(mw_r, a["m_o"]).then_inc(w_mvo, 16)
            sp.wait_ge(m_made, 2)
            sp.dma_start(c_wv[:, :, :, :], a["c_v"]).then_inc(w_c, 16)
            sp.dma_start(c_wo[:, :, :], a["c_o"]).then_inc(w_c, 16)
            with sp.Fori(1, B - 1) as b:
                load_inputs(b)
                load_for_tail(b)
                sp.wait_ge(c_vq, b)
                sp.dma_start(x_wq, a["x_q"]).then_inc(wx_loaded, 16)
                sp.dma_start(x_wo, a["x_o"]).then_inc(wx_loaded, 16)
            load_for_tail(B - 1)
            sp.wait_ge(x_done, (B - 1) * SUBS + 1)
            sp.dma_start(x_in[0:1, :], a["x"][B - 1, 0:1]).then_inc(x_loaded, 16)
            sp.wait_ge(ctxn_ready, B)
            sp.dma_start(ctx_tok[0:1, 0, :], a["ctx"][B - 1, 0:1]).then_inc(ctx_loaded, 16)

        @block.gpsimd
        def _(pool):
            nc.gpsimd.memset(minus_half[:, :], -0.5).then_inc(half_made, 1)
            nc.gpsimd.memset(pool_idle[:, :], 0.0).then_inc(x_out_free, 1)
            pool.wait_ge(half_made, 1)

            def power(b, k):
                pool.wait_ge(var_ready, b * FRONT_NORMS + (k + 1))
                n, w = (KP, KTILES) if k == 0 else (T, 1)
                nc.gpsimd.tensor_tensor(rstd[0:n, 0:w], var[0:n, 0:w], minus_half[0:n, 0:w], ALU.pow
                                        ).then_inc(rstd_ready, 1)

            def tail_power(t, k):
                pool.wait_ge(tvar_ready, t * TAIL_NORMS + (k + 1))
                nc.gpsimd.tensor_tensor(trstd[0:T, :], tvar[0:T, :], minus_half[0:T, 0:1], ALU.pow
                                        ).then_inc(trstd_ready, 1)

            def tail(t):
                pool.wait_ge(l_read, t + 1)
                for m in range(C):
                    nc.gpsimd.tensor_tensor(l_t[:, m], windows(l_proj[:, m, :], (1, LK), (1, T)),
                                            windows(l_q[:, m, :], (0, LK), (1, T)), ALU.add).then_inc(l_sum, 1)
                pool.wait_ge(l_soft, t + 1)
                nc.gpsimd.tensor_tensor(spread, windows(const[0:T, CONST["band"][0]:CONST["band"][1]],
                                                        (1, T), (1, LK)), windows(l_w16[:, :], (0, T), (1, LK)),
                                        ALU.mult).then_inc(l_spread, 1)
                for k in range(1, TAIL_NORMS):
                    tail_power(t, k)

            def store(t):
                pool.wait_ge(tx_done, t * SUBS + SUBS)
                pool.dma_start(out[bass.ds(t, 1)].rearrange("a t d -> (a t) d"), x_out[:, :]).then_inc(out_stored, 16)
                pool.wait_ge(out_stored, t * 16 + 16)
                nc.gpsimd.tensor_tensor(pool_idle[:, :], minus_half[0:1, 0:1], minus_half[0:1, 0:1], ALU.mult
                                        ).then_inc(x_out_free, 1)

            for k in range(PREPARED):
                power(0, k)
            nc.gpsimd.memset(e_max[:, :, :], 0.0)
            nc.gpsimd.memset(l_proj[:, :, :], 0.0)
            nc.gpsimd.memset(ones8[:, :], 1.0)
            nc.gpsimd.memset(vb_cols[:, :, :, :], 0.0)
            nc.gpsimd.memset(e_k[:, :, :, :, :], 0.0).then_inc(zeros_made, 1)
            for k in range(PREPARED, FRONT_NORMS):
                power(0, k)
            for k in range(PREPARED):
                power(1, k)
            with pool.Fori(1, B) as b:
                tail_power(b - 1, 0)
                for k in range(PREPARED, FRONT_NORMS):
                    power(b, k)
                tail(b - 1)
                for k in range(PREPARED):
                    power(b + 1, k)
                store(b - 1)
            for k in range(TAIL_NORMS):
                tail_power(B - 1, k)
            store(B - 1)
            pool.wait_ge(out_stored, 16 * B)

        @block.tensor
        def _(pe):
            mm = nc.tensor.matmul

            def tr(dst, src, n):
                return nc.tensor.transpose(dst, src, ident[0:n, 0:n])

            def ctx_T(b):
                pe.wait_ge(ctxn_ready, b + 1)
                if not (isinstance(b, int) and b == 0):
                    pe.wait_ge(ev_ready, b * NE)
                for c in range(C):
                    for j in range(KTILES):
                        last = tr(bank[5 + c][:, j * KP:(j + 1) * KP], ctxn[:, j, c * P:(c + 1) * P], KP)
                    last.then_inc(ctxt_psum, 1)

            def kv(b, n):
                if n == 0:
                    pe.wait_ge(w_x, 16)
                    pe.wait_ge(ctxt_ready, b * C + C)
                elif n >= 2:
                    pe.wait_ge(kv_ready, b * NKV + (n if n == IT else n - 1))
                bk = kv_bank(n)
                for c in range(C):
                    if n < IT:
                        last = mm(bank[bk][:, 0:S], x_wkv[:, c, n * P:(n + 1) * P], ctxnT[:, c, :],
                                  start=(c == 0), stop=(c == C - 1))
                    else:
                        j, half = (n - IT) // 2, (n - IT) % 2
                        lo = INNER + half * 512
                        last = mm(bank[bk][0:KP, :], ctxnT[:, c, j * KP:(j + 1) * KP], x_wkv[:, c, lo:lo + 512],
                                  start=(c == 0), stop=(c == C - 1))
                last.then_inc(kv_psum, 1)

            def front(b, t):
                def at(s, per, k):
                    pe.wait_ge(s, b * per + (k + 1))

                def normed_T(s):
                    at(xn_ready, SUBS, s)
                    for c in range(C):
                        last = tr(view(0, P, c * T, T), xn[:, c * P:(c + 1) * P], T)
                    last.then_inc(xt_psum, 1)
                    at(xt_ready, SUBS, s)

                pe.wait_ge(w_ret, 64)
                at(xn_ready, SUBS, 0)
                for c in range(C):
                    last = tr(view(1, P, c * T, T), xn[:, c * P:(c + 1) * P], T)
                last.then_inc(xt_psum, 1)
                if t is not None:
                    kv(b, IT - 1)
                at(xt_ready, SUBS, 0)
                for i, bk, lo, done in ((1, 1, C * T, None), (0, 1, 0, ret_qv), (2, 2, 0, ret_g)):
                    for m in range(C):
                        for c in range(C):
                            last = mm(view(bk, P, lo + m * T, T), ret_w[:, i, c, m * P:(m + 1) * P], xnT[:, c, :],
                                      start=(c == 0), stop=(c == C - 1))
                    if done is not None:
                        last.then_inc(done, 1)
                if t is None:
                    ctx_T(0)
                    for n in range(IT):
                        kv(0, n)
                kv(b, IT)
                at(ret_y, 1, 0)
                for c in range(C):
                    last = tr(view(3, T, c * P, P), yT[:, c, :], P)
                last.then_inc(ret_yt, 1)
                kv(b, IT + 1)
                at(ret_y2, 1, 0)
                for c in range(C):
                    last = tr(view(0, P, c * T, T), y2[:, c * P:(c + 1) * P], T)
                last.then_inc(ret_y2t_psum, 1)
                kv(b, IT + 2)
                at(ret_y2t, 1, 0)
                for c in range(C):
                    last = mm(view(1, T, 0, D), y2T[:, c, :], ret_w[:, 3, c, :], start=(c == 0), stop=(c == C - 1))
                last.then_inc(sub_out, 1)
                for n in range(IT + 3, NKV):
                    kv(b, n)

                at(xn_ready, SUBS, 1)
                for c in range(C):
                    last = tr(view(0, P, c * T, T), xn[:, c * P:(c + 1) * P], T)
                last.then_inc(xt_psum, 1)
                if t is not None:
                    tail_step(L_XT, t)
                at(xt_ready, SUBS, 1)
                pe.wait_ge(wx_loaded, 32 if isinstance(b, int) else b * 32)
                for m in range(IT):
                    if m == 4 and t is not None:
                        pe.wait_ge(txt_ready, t * SUBS + 1)
                    for c in range(C):
                        last = mm(view(1 + m // 4, P, (m % 4) * T, T), x_wq[:, c, m * P:(m + 1) * P], xnT[:, c, :],
                                  start=(c == 0), stop=(c == C - 1))
                    if m % 4 == 3:
                        last.then_inc(xq_psum, 1)
                at(kv_ready, NKV, NKV - 1)
                for i in range(XH + 2):
                    if i < XH:
                        if i % 8 == 0:
                            at(xq_ready, 2, i // 8)
                        if i >= 2:
                            at(xs_exp, XH, i - 2)
                        lo = XD * (i % 2)
                        for j in range(KTILES):
                            last = mm(view(3 + i % 2, KP, j * T, T), x_kT[lo:lo + XD, i // 2, j * KP:(j + 1) * KP],
                                      x_qT[lo:lo + XD, i // 2, :], start=True, stop=True)
                        last.then_inc(xs_psum, 1)
                    if i >= 2:
                        h = i - 2
                        at(xs_clip, XH, h)
                        if h % 4 == 0 and h >= 8:
                            at(xo_ready, 4, h // 4 - 2)
                        for j in range(KTILES):
                            last = mm(view(5 + (h // 4) % 2, T, (h % 4) * (XD + 1), XD + 1), x_p[:, h % 3, j, :],
                                      x_v[:, j, h, :], start=(j == 0), stop=(j == KTILES - 1))
                        last.then_inc(xs_pv, 1)
                for i in range(IT):
                    if i % 4 == 0:
                        at(xo_ready, 4, i // 2 + 1)
                    last = tr(view(1 + i // 4, P, (i % 4) * T, T), x_o[:, i * P:(i + 1) * P], T)
                    if i % 4 == 3:
                        last.then_inc(xot_psum, 1)
                for i in range(IT):
                    if i % 4 == 0:
                        at(xot_ready, 2, i // 4)
                    last = mm(view(0, T, 0, D), x_oT[:, i, :], x_wo[:, i, :], start=(i == 0), stop=(i == IT - 1))
                last.then_inc(sub_out, 1)
                if t is not None:
                    tail_step(L_PROJ, t)

                normed_T(2)
                pe.wait_ge(w_e, 80)
                pe.wait_ge(w_eqk, 32)
                for c in range(C):
                    last = mm(view(1, T, 0, R1), xnT[:, c, :], r_w1[:, c, :], start=(c == 0), stop=(c == C - 1))
                last.then_inc(r_h, 1)

                def project_k(e):
                    if e:
                        at(ek_ready, NE, e - 1)
                    for m in range(C):
                        for c in range(C):
                            last = mm(view(5, P, m * T, T), e_wk[:, e, c, m * P:(m + 1) * P], xnT[:, c, :],
                                      start=(c == 0), stop=(c == C - 1))
                    last.then_inc(ek_psum, 1)

                def maxima_T(e):
                    at(es_max, 4 * NE, 4 * e + 3)
                    if e:
                        at(eo_ready, NE, e - 1)
                    nc.tensor.transpose(bank[7][:, 288:288 + T // 2].bitcast(BF16),
                                        e_max[:, :, :].rearrange("p g r -> p (g r)"), ident_b[0:T, 0:T]
                                        ).then_inc(emt_psum, 1)

                def project_q(e):
                    if e:
                        at(ev_ready, NE, e - 1)
                    for m in range(C):
                        for c in range(C):
                            mm(view(6, P, m * T, T), e_wq[:, e, c, m * P:(m + 1) * P], xnT[:, c, :],
                               start=(c == 0), stop=(c == C - 1))

                def project_v(e):
                    for c in range(C):
                        last = mm(view(6, T, C * T, D), xnT[:, c, :], e_wv[:, e, c, :],
                                  start=(c == 0), stop=(c == C - 1))
                    last.then_inc(eqv_psum, 1)

                def max_scores(e, r):
                    if r == 0:
                        at(eb_ready, NE, e)
                    if 4 * e + r >= 1:
                        at(es_max, 4 * NE, 4 * e + r - 1)
                    mm(view(1, T, 0, 4 * T), e_qb[:, r // 2, r % 2, :],
                       e_kb[:, r // 2, :, :].rearrange("p g t -> p (g t)"), start=True, stop=True
                       ).then_inc(es_psum, 1)

                def scores_T(e, g):
                    if 4 * e + g >= 2:
                        at(est_exp, 4 * NE, 4 * e + g - 2)
                    elif g == 1:
                        at(r_nm, 1, 0)
                    for m in range(C):
                        mm(view(3 + g % 2, T, 2 * m * T, 2 * T), e_k[:, e % 2, m, g, :],
                           e_q[:, e % 2, m, :, :].rearrange("p o t -> p (o t)"), start=True, stop=True,
                           skip_group_check=True)
                        if g == 0 and m == 0:
                            at(emt_ready, NE, e)
                        for o in range(2):
                            last = mm(view(3 + g % 2, T, (2 * m + o) * T, T), sel_b[:, 2 * m + o, g, :], e_maxT[:, :],
                                      start=False, stop=True, skip_group_check=True)
                    last.then_inc(est_psum, 1)

                def probs_v(e, g):
                    if g == 0:
                        at(ev_ready, NE, e)
                        if e:
                            at(eot_ready, NE, e - 1)
                    at(est_exp, 4 * NE, 4 * e + g)
                    for r in range(4):
                        h = 8 * (r // 2) + 2 * g + r % 2
                        last = mm(view(7, T, h * (ED + 1), ED + 1), e_p[:, g % 2, r, :], e_v[:, e % 2, h, :],
                                  start=True, stop=True)
                    last.then_inc(epv, 1)

                def out_T(e):
                    at(eo_ready, NE, e)
                    for c in range(C):
                        last = tr(view(7, P, c * T, T), e_o[:, 8 * c:8 * c + 8, :].rearrange("p h d -> p (h d)"), T)
                    last.then_inc(eot_psum, 1)

                def out_sum(e):
                    at(eot_ready, NE, e)
                    for c in range(C):
                        last = mm(view(0, T, 0, D), e_oT[:, c, :], e_wo[:, e, c, :], start=False,
                                  stop=(e == NE - 1 and c == C - 1))
                    if e == NE - 1:
                        last.then_inc(sub_out, 1)

                def place(s, k):
                    if t is not None:
                        for step in PLACES[PER_SLOT * s + k]:
                            tail_step(step, t)
                    elif PER_SLOT * s + k in SETUP_PLACES:
                        setup_step(SETUP_PLACES[PER_SLOT * s + k])

                for s in range(NE + 2):
                    if s < NE:
                        project_k(s)
                        project_q(s)
                    if s == NE:
                        ctx_T(b + 1)
                    if 1 <= s <= NE:
                        maxima_T(s - 1)
                    if s >= 2:
                        out_T(s - 2)
                    if s < NE:
                        project_v(s)
                    if s == 0:
                        at(r_hn, 1, 0)
                        tr(view(3, P, 0, T), h1[:, :], T).then_inc(r_ht_psum, 1)
                    for g in range(GROUPS):
                        if g == 0:
                            place(s, 0)
                        if g < 4 and 1 <= s <= NE:
                            scores_T(s - 1, g)
                        if g >= 1 and s < NE:
                            max_scores(s, g - 1)
                        if g >= 1 and 1 <= s <= NE:
                            probs_v(s - 1, g - 1)
                        if g == 0 and s == 1:
                            at(r_gates, 1, 0)
                            tr(view(0, NE, 0, T), gates[:, :], T).then_inc(r_gt_psum, 1)
                        if g == 0 and s == 2:
                            at(r_gt, 1, 0)
                            mm(view(0, T, 0, D), gatesT[:, :], e_bo_all[:, :], start=True, stop=False)
                        if g == 1 and s >= 2:
                            out_sum(s - 2)
                        if g == 2 and s == 0:
                            at(r_ht, 1, 0)
                            mm(view(4, T, 0, NE), h1T[:, :], r_w2[:, :], start=True, stop=True).then_inc(r_lg, 1)
                        place(s, g + 1)
                        for n in keys_after(s, g):
                            kv(b + 1, n)

            def setup_step(step):
                if step == SETUP_BIAS:
                    pe.wait_ge(consts_made, 1)
                    for e in range(NE):
                        for c in range(C):
                            last = mm(view(2, NE, 0, D), vb_cols[:, e, c, :], e_wo[:, e, c, :],
                                      start=(e == 0 and c == 0), stop=(e == NE - 1 and c == C - 1))
                    last.then_inc(bo_psum, 1)
                else:
                    if step == SETUP_QK:
                        pe.wait_ge(bo_made, 1)
                        pe.wait_ge(w_mqk, 32)
                    else:
                        pe.wait_ge(w_mvo, 32)
                    for c in range(C):
                        for i in range(IT):
                            last = mm(view(2, P, c * D, D), mw_l[:, i, c * P:(c + 1) * P], mw_r[:, i, :],
                                      start=(i == 0), stop=(i == IT - 1))
                    last.then_inc(m_psum, 1)

            def tail_step(step, t):
                def at(s, per, k):
                    pe.wait_ge(s, t * per + (k + 1))

                def normed_T(s):
                    at(txn_ready, SUBS, s)
                    for c in range(C):
                        last = tr(view(2, P, c * T, T), txn[:, c * P:(c + 1) * P], T)
                    last.then_inc(txt_psum, 1)

                if step == L_XT:
                    normed_T(0)
                elif step == L_PROJ:
                    at(txt_ready, SUBS, 0)
                    pe.wait_ge(w_l, 32)
                    for i in range(2):
                        for m in range(C):
                            for c in range(C):
                                last = mm(view(2, P, (i * C + m) * T, T), l_w[:, i, c, m * P:(m + 1) * P],
                                          txnT[:, c, :], start=(c == 0), stop=(c == C - 1))
                    last.then_inc(l_psum, 1)
                elif step in (L_Z, L_Z2):
                    if step == L_Z:
                        pe.wait_ge(raw_loaded, t * 16 + 16)
                        at(l_read, 1, 0)
                    else:
                        at(z_ready, 2, 0)
                    for j in ((0, 1) if step == L_Z else (2,)):
                        for c in range(C):
                            last = mm(view(2, KP, (j % 2) * D, D), ctx_raw[:, c, j * KP:(j + 1) * KP],
                                      m_vo[:, c, :], start=(c == 0), stop=(c == C - 1))
                    last.then_inc(z_psum, 1)
                elif L_SCORE <= step <= L_SCORED:
                    if step == L_SCORE:
                        at(z_ready, 2, 1)
                        at(l_mixed, 2, 1)
                    for k in range((step - L_SCORE) * LK // L_STEPS, (step - L_SCORE + 1) * LK // L_STEPS):
                        last = mm(view(2, T, LK - 1 - k, 1), l_t[:, 0, k, :], col("one"), start=True, stop=True)
                    if step == L_SCORED:
                        last.then_inc(l_score, 1)
                elif step == L_BAND_T:
                    at(l_band, 2, 1)
                    tr(view(2, T, 0, T), l_a[:, :], T).then_inc(l_at_psum, 1)
                elif step == L_OUT:
                    at(l_at, 1, 0)
                    mm(view(2, T, 0, D), l_aT[:, :], txn[:, :], start=True, stop=True).then_inc(tsub_out, 1)
                elif step == M_XT:
                    normed_T(1)
                elif step == M_QUERY:
                    at(txt_ready, SUBS, 1)
                    for m in range(C):
                        for c in range(C):
                            last = mm(view(2, P, m * T, T), m_qk[:, c, m * P:(m + 1) * P], txnT[:, c, :],
                                      start=(c == 0), stop=(c == C - 1))
                    last.then_inc(g_psum, 1)
                elif step == M_SCORE:
                    at(g_ready, 1, 0)
                    for j in range(KTILES):
                        for c in range(C):
                            last = mm(view(2, KP, j * T, T), ctx_raw[:, c, j * KP:(j + 1) * KP], m_g[:, c, :],
                                      start=(c == 0), stop=(c == C - 1))
                    last.then_inc(ms_psum, 1)
                elif step == M_OUT:
                    at(ms_e, 1, 0)
                    for j in range(KTILES):
                        last = mm(view(2, T, 0, D), m_e[:, j, :], m_z[:, j, :], start=(j == 0), stop=(j == KTILES - 1))
                    last.then_inc(tsub_out, 1)
                elif step == C_XT:
                    normed_T(2)
                elif step == C_ROUTE:
                    at(txt_ready, SUBS, 2)
                    pe.wait_ge(w_c, 48)
                    for c in range(C):
                        last = mm(view(2, NE, 0, T), c_wr[:, c, :], txnT[:, c, :], start=(c == 0), stop=(c == C - 1))
                    last.then_inc(c_lg, 1)
                elif step == C_POS:
                    at(c_dg, 1, 0)
                    mm(view(2, T, 0, T), ones8[:, :], c_diag[:, 0].rearrange("p e j -> p (e j)"),
                       start=True, stop=True)
                    mm(view(2, T, T, 1), c_diag[:, 1].rearrange("p e j -> p (e j)"), ones8[:, 0:1],
                       start=True, stop=True).then_inc(c_rpsum, 1)
                elif step == C_GATHER:
                    at(c_hots, 1, 0)
                    for c in range(C):
                        mm(view(2, P, c * T, T), txn[:, c * P:(c + 1) * P], c_hot[:, :], start=True, stop=True)
                    for i in range(2):
                        lo = CONST["rope"][0] + i * ROT
                        mm(view(2, ROT, (C + i) * T, T), const[0:T, lo:lo + ROT], c_hot[:, :], start=True, stop=True)
                    mm(view(2, T, (C + 2) * T, 1), c_hot[:, :], col("iota", 0, 0, T), start=True, stop=True
                       ).then_inc(c_gpsum, 1)
                elif C_QKV <= step <= C_QKVED:
                    if step == C_QKV:
                        at(c_xg, 1, 0)
                        pe.wait_ge(wc_loaded, 16 * (B - 1) if isinstance(t, int) else t * 16 + 16)
                    for n in range((step - C_QKV) * 3 * NE // QKV_STEPS, (step - C_QKV + 1) * 3 * NE // QKV_STEPS):
                        part, e = n // NE, n % NE
                        for c in range(C):
                            w = c_wqk[:, n, c, :] if part < 2 else c_wv[:, e, c, :]
                            last = mm(view(2, P, part * T + e * TK, TK), w, c_xgT[:, c, e * TK:(e + 1) * TK],
                                      start=(c == 0), stop=(c == C - 1))
                        if n == 2 * NE - 1:
                            last.then_inc(c_vq, 1)
                    if step == C_QKVED:
                        tr(view(2, T, 3 * T, T), c_hot[:, :], T).then_inc(c_qkv, 1)
                elif step == C_SCORE:
                    at(c_qk_ready, 1, 0)
                    tr(view(2, T, T, HP), c_vT[:, :], P)
                    mm(view(2, T, 0, T), c_qk[:, 0, :], c_qk[:, 1, :], start=True, stop=True).then_inc(c_spsum, 1)
                elif step == C_PROB_T:
                    at(c_en2, 1, 0)
                    tr(view(2, T, 0, T), c_e[:, :], T).then_inc(c_etp, 1)
                elif step == C_AV:
                    at(c_et, 1, 0)
                    mm(view(2, P, 0, T), c_v[:, :], c_eT[:, :], start=True, stop=True).then_inc(c_avp, 1)
                elif C_UP <= step <= C_UPPED:
                    if step == C_UP:
                        at(c_av, 1, 0)
                    for n in range((step - C_UP) * C * NE // UP_STEPS, (step - C_UP + 1) * C * NE // UP_STEPS):
                        m, e = n // NE, n % NE
                        last = mm(view(2, P, m * T + e * TK, TK), c_wo[:, e, m * P:(m + 1) * P],
                                  c_avT[:, e * TK:(e + 1) * TK], start=True, stop=True)
                    if step == C_UPPED:
                        last.then_inc(c_xpp, 1)
                elif step == C_UP_T:
                    at(c_xps, 1, 0)
                    for m in range(C):
                        last = tr(view(2, T, m * P, P), c_xpT[:, m, :], P)
                    last.then_inc(c_xqp, 1)
                elif step == C_OUT:
                    at(c_xqs, 1, 0)
                    mm(view(2, T, 0, D), c_hotT[:, :], c_xp[:, :], start=True, stop=True).then_inc(tsub_out, 1)

            pe.wait_ge(w_small, 48)
            front(0, None)
            with pe.Fori(1, B) as b:
                front(b, b - 1)
            for step in range(C_OUT + 1):
                tail_step(step, B - 1)

        @block.scalar
        def _(act):
            af = nc.scalar.activation

            def ctx_T(b):
                for c in range(C):
                    act.wait_ge(ctxt_psum, b * C + (c + 1))
                    af(ctxnT[:, c, :], bank[5 + c][:, 0:S], ACT.Identity, bias=col("ctx_b", c),
                       scale=col("ctx_w", c)).then_inc(ctxt_ready, 1)

            def kv(b, n):
                act.wait_ge(kv_psum, b * NKV + (n + 1))
                if n < IT:
                    ins = af(x_kT[:, n, :], bank[kv_bank(n)][:, 0:S], ACT.Copy)
                else:
                    j, half = (n - IT) // 2, (n - IT) % 2
                    ins = af(x_v[:, j, half * 8:half * 8 + 8, 0:XD], view(kv_bank(n), KP, 0, 8, XD), ACT.Copy)
                ins.then_inc(kv_ready, 1)

            def front(b, t):
                def at(s, per, k):
                    act.wait_ge(s, b * per + (k + 1))

                if t is not None:
                    kv(b, IT - 1)
                at(ret_g, 1, 0)
                af(eg[:, :, :], view(2, P, 0, C, T), ACT.Exp, scale=-1.0).then_inc(ret_eg, 1)
                if t is None:
                    ctx_T(0)
                    for n in range(IT):
                        kv(0, n)
                at(ones_made, 1, 0)
                for n in range(IT, NKV):
                    kv(b, n)

                for i in range(2):
                    at(xq_psum, 2, i)
                    af(x_qT[:, 4 * i:4 * i + 4, :], view(1 + i, P, 0, 4, T), ACT.Copy).then_inc(xq_ready, 1)
                for h in range(XH):
                    at(xs_psum, XH, h)
                    if h >= 3:
                        at(xs_pv, XH, h - 3)
                    af(x_p[:, h % 3], view(3 + h % 2, KP, 0, KTILES, T), ACT.Exp, scale=XD ** -0.5
                       ).then_inc(xs_exp, 1)
                for i in range(2):
                    at(xot_psum, 2, i)
                    af(x_oT[:, 4 * i:4 * i + 4, :], view(1 + i, P, 0, 4, T), ACT.Copy).then_inc(xot_ready, 1)

                def place(s, k):
                    for step in PLACES[PER_SLOT * s + k] if t is not None else ():
                        tail_step(step, t)

                if t is None:
                    act.wait_ge(zeros_made, 1)
                for s in range(NE + 2):
                    if s == NE:
                        ctx_T(b + 1)
                    if s < NE:
                        at(ek_psum, NE, s)
                        for m in range(C):
                            for g in range(4):
                                q = slice(32 * g, 32 * g + 32)
                                ins = af(e_k[q, s % 2, m, g, :], bank[5][q, m * T:(m + 1) * T], ACT.Identity,
                                         bias=col("kb", s * C + m, 32 * g, 32 * g + 32))
                        ins.then_inc(ek_ready, 1)
                    if s < NE:
                        at(eqv_psum, NE, s)
                        at(eq_ready, NE, s)
                        af(e_v[:, s % 2, :, 0:ED], view(6, T, C * T, EH, ED), ACT.Copy).then_inc(ev_ready, 1)
                    if s == 0:
                        at(r_ht_psum, 1, 0)
                        af(h1T[:, :], view(3, P, 0, T), ACT.Relu, bias=col("ffn_b"), scale=col("ffn_g")
                           ).then_inc(r_ht, 1)
                    for g in range(GROUPS):
                        if g == 0:
                            place(s, 0)
                        if s == 0 and g == GROUPS - 1:
                            at(r_nm, 1, 0)
                            af(pr[:, :], lg[:, :], ACT.Exp, bias=sc1[0:T, 0:1], accum_out=sc1[0:T, 1:2]
                               ).then_inc(r_exp, 1)
                        if g < 4 and 1 <= s <= NE:
                            n = 4 * (s - 1) + g
                            at(est_psum, 4 * NE, n)
                            if n >= 2:
                                at(epv, 4 * NE, n - 2)
                            af(e_p[:, g % 2], view(3 + g % 2, T, 0, 4, T), ACT.Exp, scale=ED ** -0.5
                               ).then_inc(est_exp, 1)
                        place(s, g + 1)
                        for n in keys_after(s, g):
                            kv(b + 1, n)

            def tail_step(step, t):
                def at(s, per, k):
                    act.wait_ge(s, t * per + (k + 1))

                if step in (L_Z, L_Z2):
                    i = step - L_Z
                    at(z_psum, 2, i)
                    lo, n = ((0, 2), (2, 1))[i]
                    af(m_z[:, lo:lo + n, :], view(2, KP, 0, n, D), ACT.Copy).then_inc(z_ready, 1)
                if L_TANH <= step < L_TANH + TANH_STEPS:
                    m, k = (step - L_TANH) // 2, (step - L_TANH) % 2 * (LK // 2)
                    at(l_sum, C, m)
                    af(l_t[:, m, k:k + LK // 2], l_t[:, m, k:k + LK // 2], ACT.Tanh).then_inc(l_tanh, 1)
                if step == L_SCORED:
                    at(l_nm, 1, 0)
                    af(l_w16[:, :], view(2, T, 0, LK), ACT.Exp, bias=sc1[0:T, 2:3], accum_out=sc1[0:T, 3:4]
                       ).then_inc(l_exp, 1)
                if step == M_EXP:
                    at(ms_nm, 1, 0)
                    for j in range(KTILES):
                        af(m_e[:, j, :], view(2, KP, j * T, T), ACT.Exp, bias=m_nm[:, j:j + 1], scale=XD ** -0.5,
                           accum_out=m_sum[:, j:j + 1]).then_inc(ms_exp, 1)
                if step == C_ROUTE:
                    at(c_lg, 1, 0)
                    af(c_s[:, :], view(2, NE, 0, T), ACT.Exp, scale=-1.0).then_inc(c_en, 1)
                if step == C_EXP:
                    at(c_nm, 1, 0)
                    af(c_e[:, :], c_pen[:, :], ACT.Exp, bias=sc1[0:T, 4:5], scale=HP ** -0.5,
                       accum_out=sc1[0:T, 5:6]).then_inc(c_exp, 1)

            act.wait_ge(w_small, 48)
            front(0, None)
            with act.Fori(1, B) as b:
                front(b, b - 1)
            for step in range(C_OUT + 1):
                tail_step(step, B - 1)

        @block.vector
        def _(dve):
            v = nc.vector
            count = [0]
            norms = [0, 0]
            before = [None]

            def alone():
                v.memset(idle[:, :], 0.0)

            def link(ins):
                count[0] += 1
                ins.then_inc(dve_done, 1)
                dve.wait_ge(dve_done, before[0](count[0]))

            def moments(pairs, n, tail=False):
                k = len(pairs)
                st, mean, va, ready = (tstats, tmv, tvar, tvar_ready) if tail else (stats, mv, var, var_ready)
                for j, (_, src) in enumerate(pairs):
                    ins = v.bn_stats(st[0:n, j, :], src)
                link(ins)
                alone()
                for j in range(k):
                    ins = v.bn_aggr(mean[0:n, j, :], st[0:n, j, :])
                link(ins)
                v.tensor_scalar(va[0:n, 0:k], mean[0:n, 0:k, 1], EPS, None, ALU.add).then_inc(ready, 1)
                norms[tail] += 1

            def scaled(row, pairs, n, tail=False):
                mean, rs, back, per = (tmv, trstd, trstd_ready, TAIL_NORMS) if tail else (
                    mv, rstd, rstd_ready, FRONT_NORMS)
                dve.wait_ge(back, row * per + norms[tail])
                for j, (dst, src) in enumerate(pairs):
                    ins = v.tensor_scalar(dst, src, mean[0:n, j, 0:1], rs[0:n, j:j + 1], ALU.subtract, ALU.mult)
                return ins

            def normalise_each(row, pairs, n, tail=False):
                moments(pairs, n, tail)
                return scaled(row, pairs, n, tail)

            def prepare_x(b):
                dve.wait_ge(x_loaded, b * 16 + 16)
                normalise_each(b, [(xn[:, :], x_in[:, :])], T).then_inc(xn_ready, 1)

            ctx_pairs = [(ctxn[:, j, :], ctx_tok[:, j, :]) for j in range(KTILES)]

            def ctx_moments(b):
                norms[0] = 0
                dve.wait_ge(ctx_loaded, b * 16 + 16)
                moments(ctx_pairs, KP)

            def prepare_ctx(b):
                dve.wait_ge(ctxt_psum, b * C)
                scaled(b, ctx_pairs, KP).then_inc(ctxn_ready, 1)

            def front(b, t):
                def at(s, per, k):
                    dve.wait_ge(s, b * per + (k + 1))

                def normalise(dst, src, n):
                    return normalise_each(b, [(dst, src)], n)

                def xT_copy(s):
                    at(xt_psum, SUBS, s)
                    v.tensor_copy(xnT[:, :, :], view(0, P, 0, C, T)).then_inc(xt_ready, 1)

                def add_to_x(s, dst, bk, src):
                    at(sub_out, SUBS, s)
                    v.tensor_tensor(dst[:, :], src[:, :], view(bk, T, 0, D), ALU.add).then_inc(x_done, 1)
                    at(x_done, SUBS, s)

                norms[0] = 2
                at(xt_psum, SUBS, 0)
                v.tensor_copy(xnT[:, :, :], view(1, P, 0, C, T)).then_inc(xt_ready, 1)
                v.memset(x_v[:, :, :, XD:XD + 1], 1.0).then_inc(ones_made, 1)
                if t is not None:
                    tail_step(L_NORM, t)
                at(ret_qv, 1, 0)
                for m in range(C):
                    ins = v.tensor_tensor_scan(state[:, m, :], col("lam", m).to_broadcast([P, T]),
                                               view(1, P, (C + m) * T, T), 0.0, ALU.mult, ALU.add)
                link(ins)
                v.tensor_tensor(yT[:, :, :], state[:, :, :], view(1, P, 0, C, T), ALU.mult).then_inc(ret_y, 1)
                at(ret_eg, 1, 0)
                link(v.tensor_scalar(eg[:, :, :], eg[:, :, :], 1.0, None, ALU.add))
                link(v.reciprocal(eg[:, :, :], eg[:, :, :]))
                v.tensor_tensor(gateT[:, :, :], eg[:, :, :], view(2, P, 0, C, T), ALU.mult)
                at(ret_yt, 1, 0)
                normalise(y2[:, :], view(3, T, 0, D), T).then_inc(ret_y2, 1)
                at(ret_y2t_psum, 1, 0)
                for m in range(C):
                    ins = v.tensor_scalar(y2T[:, m, :], view(0, P, m * T, T), col("ret_g", m), col("ret_b", m),
                                          ALU.mult, ALU.add)
                link(ins)
                v.tensor_tensor(y2T[:, :, :], y2T[:, :, :], gateT[:, :, :], ALU.mult).then_inc(ret_y2t, 1)
                add_to_x(0, x, 1, x_in)

                link(normalise(y2[:, :], x[:, :], T))
                normalise(xn[:, :], y2[:, :], T).then_inc(xn_ready, 1)
                link(v.tensor_tensor(x[:, :], x[:, :], row("bo"), ALU.add))
                at(xt_psum, SUBS, 1)
                for m in range(C):
                    ins = v.tensor_scalar(xnT[:, m, :], view(0, P, m * T, T), col("lat_w", m), col("lat_b", m),
                                          ALU.mult, ALU.add)
                ins.then_inc(xt_ready, 1)
                if t is not None:
                    tail_step(L_XT, t)

                def x_norm(g):
                    at(xs_pv, XH, 4 * g + 3)
                    o = view(5 + g % 2, T, 0, 4, XD + 1)
                    link(v.reciprocal(x_rc[:, :, :], o[:, :, XD:XD + 1]))
                    v.tensor_tensor(x_o[:, g * 4 * XD:(g + 1) * 4 * XD].rearrange("p (h d) -> p h d", h=4),
                                    o[:, :, 0:XD], x_rc[:, :, :].to_broadcast([T, 4, XD]), ALU.mult
                                    ).then_inc(xo_ready, 1)

                for h in range(XH):
                    at(xs_exp, XH, h)
                    v.tensor_scalar(x_p[:, h % 3], x_p[:, h % 3], float(np.exp(CLIP)), float(np.exp(-CLIP)),
                                    ALU.min, ALU.max).then_inc(xs_clip, 1)
                    if h % 4 == 1 and h > 4:
                        x_norm(h // 4 - 1)
                x_norm(3)
                add_to_x(1, x, 0, x)

                normalise(xn[:, :], x[:, :], T).then_inc(xn_ready, 1)
                xT_copy(2)
                if t is not None:
                    tail_step(L_PROJ, t)
                v.memset(e_v[:, :, :, ED:ED + 1], 1.0)
                at(r_h, 1, 0)
                link(v.tensor_tensor(h1[:, :], view(1, T, 0, R1), row("rb1"), ALU.add))
                normalise(h1[:, :], h1[:, :], T).then_inc(r_hn, 1)

                def place(s, k):
                    if t is not None:
                        for step in PLACES[PER_SLOT * s + k]:
                            tail_step(step, t)
                    elif PER_SLOT * s + k in SETUP_PLACES:
                        setup_step(SETUP_PLACES[PER_SLOT * s + k])

                def queries(e):
                    at(eqv_psum, NE, e)
                    for m in range(C):
                        for o, keep in enumerate(("even", "odd")):
                            ins = v.tensor_scalar(e_q[:, e % 2, m, o, :], view(6, P, m * T, T), col("qb", e * C + m),
                                                  col(keep), ALU.add, ALU.mult)
                    ins.then_inc(eq_ready, 1)
                    at(eq_ready, NE, e)
                    v.tensor_copy(e_qb[:, :, :, :], e_q[:, e % 2])
                    at(ek_ready, NE, e)
                    v.tensor_copy(e_kb[:, :, :, :], e_k[:, e % 2]).then_inc(eb_ready, 1)

                def router_logits():
                    at(r_lg, 1, 0)
                    link(v.tensor_tensor(lg[:, :], view(4, T, 0, NE), row("rb2"), ALU.add))
                    v.tensor_reduce(sc1[0:T, 0:1], lg[:, :], AX.X, ALU.max, negate=True).then_inc(r_nm, 1)

                def router():
                    at(r_exp, 1, 0)
                    link(v.reciprocal(sc1[0:T, 1:2], sc1[0:T, 1:2]))
                    link(v.tensor_scalar(pr[:, :], pr[:, :], sc1[0:T, 1:2], None, ALU.mult))
                    alone()
                    link(v.max(top[:, :], pr[:, :]))
                    alone()
                    link(v.max_index(topi[:, :], top[:, :], pr[:, :]))
                    v.tensor_copy(topf[:, :], topi[:, :])
                    link(v.tensor_tensor(sc1[0:T, 6:7], top[:, 0:1], top[:, 1:2], ALU.add))
                    link(v.reciprocal(sc1[0:T, 6:7], sc1[0:T, 6:7]))
                    link(v.tensor_scalar(top[:, 0:2], top[:, 0:2], sc1[0:T, 6:7], None, ALU.mult))
                    for r in range(2):
                        ins = v.tensor_scalar(g01[:, r, :], const[0:T, CONST["iota8"][0]:CONST["iota8"][1]],
                                              topf[:, r:r + 1], top[:, r:r + 1], ALU.is_equal, ALU.mult)
                    link(ins)
                    v.tensor_tensor(gates[:, :], g01[:, 0, :], g01[:, 1, :], ALU.add).then_inc(r_gates, 1)
                    at(r_gates, 1, 0)

                def output(e):
                    at(epv, 4 * NE, 4 * e + 3)
                    o = view(7, T, 0, EH, ED + 1)
                    link(v.reciprocal(e_rc[:, :, :], o[:, :, ED:ED + 1]))
                    link(v.tensor_scalar(e_rc[:, :, :], e_rc[:, :, :], gates[:, e:e + 1], None, ALU.mult))
                    v.tensor_tensor(e_o[:, :, :], o[:, :, 0:ED], e_rc[:, :, :].to_broadcast([T, EH, ED]), ALU.mult
                                    ).then_inc(eo_ready, 1)

                for s in range(NE + 2):
                    if s >= 2:
                        output(s - 2)
                    if s >= 2:
                        at(eot_psum, NE, s - 2)
                    if 1 <= s <= NE:
                        at(emt_psum, NE, s - 1)
                        v.tensor_copy(e_maxT[:, :], bank[7][:, 288:288 + T // 2].bitcast(BF16)).then_inc(emt_ready, 1)
                    if s >= 2:
                        v.tensor_copy(e_oT[:, :, :], view(7, P, 0, C, T)).then_inc(eot_ready, 1)
                    if s < NE:
                        queries(s)
                    for g in range(GROUPS):
                        if g == 0:
                            place(s, 0)
                        if g >= 1 and s < NE:
                            r = g - 1
                            at(es_psum, 4 * NE, 4 * s + r)
                            v.tensor_reduce(e_max[:, r, 0:4], view(1, T, 0, 4, T), AX.X, ALU.max
                                            ).then_inc(es_max, 1)
                        if s == 1 and g == 1:
                            at(r_gt_psum, 1, 0)
                            v.tensor_copy(gatesT[:, :], view(0, NE, 0, T)).then_inc(r_gt, 1)
                        if s == 0 and g == 3:
                            router_logits()
                        if s == 0 and g == 4:
                            router()
                        if s == NE - 2 and g == 2:
                            ctx_moments(b + 1)
                        if s == NE - 1 and g == 0:
                            prepare_ctx(b + 1)
                        if s == NE and g == 1:
                            prepare_x(b + 1)
                        place(s, g + 1)
                add_to_x(2, tx, 0, x)

            def setup_step(step):
                if step == SETUP_BIAS:
                    dve.wait_ge(bo_psum, 1)
                    v.tensor_tensor(e_bo_all[:, :], e_bo[:, :], view(2, NE, 0, D), ALU.add).then_inc(bo_made, 1)
                else:
                    dve.wait_ge(m_psum, step - SETUP_QK + 1)
                    m = m_qk if step == SETUP_QK else m_vo
                    v.tensor_copy(m[:, :, :], view(2, P, 0, C, D)).then_inc(m_made, 1)

            def tail_step(step, t):
                def at(s, per, k):
                    dve.wait_ge(s, t * per + (k + 1))

                def norm_x(s):
                    normalise_each(t, [(txn[:, :], tx[:, :])], T, tail=True).then_inc(txn_ready, 1)

                def xT_copy(s):
                    at(txt_psum, SUBS, s)
                    v.tensor_copy(txnT[:, :, :], view(2, P, 0, C, T)).then_inc(txt_ready, 1)

                def add_to_x(s, dst):
                    at(tsub_out, SUBS, s)
                    v.tensor_tensor(dst[:, :], tx[:, :], view(2, T, 0, D), ALU.add).then_inc(tx_done, 1)
                    at(tx_done, SUBS, s)

                if step == L_NORM:
                    norms[1] = 0
                    norm_x(0)
                elif step == L_XT:
                    xT_copy(0)
                elif step == L_PROJ:
                    at(l_psum, 1, 0)
                    v.tensor_copy(l_q[:, :, :], view(2, P, 0, C, T))
                    v.tensor_copy(l_proj[:, :, LPAD:LPAD + T], view(2, P, C * T, C, T)).then_inc(l_read, 1)
                    if isinstance(t, int):
                        at(l_read, 1, 0)
                        for m in range(C):
                            v.tensor_tensor(l_t[:, m], windows(l_proj[:, m, :], (1, LK), (1, T)),
                                            windows(l_q[:, m, :], (0, LK), (1, T)), ALU.add).then_inc(l_sum, 1)
                elif step == L_SCALE:
                    at(l_tanh, TANH_STEPS, TANH_STEPS // 2 - 1)
                    link(v.tensor_scalar(l_t[:, 0], l_t[:, 0], col("v", 0), None, ALU.mult))
                elif step in (L_MIX, L_MIX2):
                    k = slice((step - L_MIX) * (LK // 2), (step - L_MIX + 1) * (LK // 2))
                    if step == L_MIX:
                        at(l_tanh, TANH_STEPS, TANH_STEPS - 1)
                    v.scalar_tensor_tensor(l_t[:, 0, k], l_t[:, 1, k], col("v", 1), l_t[:, 0, k], ALU.mult, ALU.add
                                           ).then_inc(l_mixed, 1)
                elif step == L_SCORED:
                    at(l_score, 1, 0)
                    v.tensor_reduce(sc1[0:T, 2:3], view(2, T, 0, LK), AX.X, ALU.max, negate=True).then_inc(l_nm, 1)
                    at(l_exp, 1, 0)
                    link(v.reciprocal(sc1[0:T, 3:4], sc1[0:T, 3:4]))
                    v.tensor_scalar(l_w16[:, :], l_w16[:, :], sc1[0:T, 3:4], None, ALU.mult).then_inc(l_soft, 1)
                    if isinstance(t, int):
                        at(l_soft, 1, 0)
                        v.tensor_tensor(spread, windows(const[0:T, CONST["band"][0]:CONST["band"][1]],
                                                        (1, T), (1, LK)), windows(l_w16[:, :], (0, T), (1, LK)),
                                        ALU.mult).then_inc(l_spread, 1)
                elif step in (L_BAND, L_BAND2):
                    if step == L_BAND:
                        at(l_spread, 1, 0)
                    h = slice((step - L_BAND) * (T // 2), (step - L_BAND + 1) * (T // 2))
                    v.tensor_reduce(l_a[:, h], spread[:, h], AX.X, ALU.add).then_inc(l_band, 1)
                elif step == L_BAND_T:
                    at(l_at_psum, 1, 0)
                    v.tensor_copy(l_aT[:, :], view(2, T, 0, T)).then_inc(l_at, 1)
                elif step == L_OUT:
                    add_to_x(0, tx)
                    norm_x(1)
                elif step == M_XT:
                    xT_copy(1)
                elif step == M_QUERY:
                    at(g_psum, 1, 0)
                    v.tensor_copy(m_g[:, :, :], view(2, P, 0, C, T)).then_inc(g_ready, 1)
                elif step == M_SCORE:
                    at(ms_psum, 1, 0)
                    link(v.tensor_reduce(m_nm[:, :], view(2, KP, 0, KTILES, T), AX.X, ALU.max, negate=True))
                    v.tensor_scalar(m_nm[:, :], m_nm[:, :], XD ** -0.5, None, ALU.mult).then_inc(ms_nm, 1)
                elif step == M_NORM:
                    at(ms_exp, KTILES, KTILES - 1)
                    link(v.reciprocal(m_sum[:, :], m_sum[:, :]))
                    v.tensor_tensor(m_e[:, :, :], m_e[:, :, :], windows(m_sum[:, :], (1, KTILES), (0, T)), ALU.mult
                                    ).then_inc(ms_e, 1)
                elif step == M_OUT:
                    add_to_x(1, tx)
                    norm_x(2)
                elif step == C_XT:
                    xT_copy(2)
                elif step == C_ROUTE:
                    at(c_en, 1, 0)
                    link(v.tensor_scalar(c_s[:, :], c_s[:, :], 1.0, None, ALU.add))
                    link(v.reciprocal(c_s[:, :], c_s[:, :]))
                elif step == C_ROUTE2:
                    alone()
                    link(v.max(c_top[:, 0:8], c_s[:, :]))
                    alone()
                    v.max_index(c_idx[:, 0:8], c_top[:, 0:8], c_s[:, :])
                    link(v.match_replace(c_s2[:, :], c_top[:, 0:8], c_s[:, :], -1.0))
                elif step == C_ROUTE3:
                    alone()
                    link(v.max(c_top[:, 8:16], c_s2[:, :]))
                    alone()
                    link(v.max_index(c_idx[:, 8:16], c_top[:, 8:16], c_s2[:, :]))
                    link(v.tensor_copy(c_idxf[:, :], c_idx[:, :]))
                    own = const[0:NE, CONST["own"][0]:CONST["own"][1]].rearrange("p (e j) -> p e j", e=NE)
                    v.tensor_tensor(c_diag[:, 0], own, windows(c_idxf[:, 0:TK], (0, NE), (1, TK)), ALU.mult)
                    v.tensor_tensor(c_diag[:, 1], own, windows(c_top[:, 0:TK], (0, NE), (1, TK)), ALU.mult
                                    ).then_inc(c_dg, 1)
                elif step == C_POS:
                    at(c_rpsum, 1, 0)
                    v.tensor_copy(c_iv[:, 0:1], view(2, T, T, 1))
                    link(v.tensor_copy(c_pos[:, :], view(2, T, 0, T)))
                    v.tensor_scalar(c_hot[:, :], c_pos[:, :], col("iota", 0, 0, T), None, ALU.is_equal
                                    ).then_inc(c_hots, 1)
                elif step == C_GATHER:
                    at(c_gpsum, 1, 0)
                    v.tensor_copy(c_cs[:, :, :], view(2, ROT, C * T, 2, T))
                    v.tensor_copy(c_iv[:, 1:2], view(2, T, (C + 2) * T, 1))
                    v.tensor_copy(c_xgT[:, :, :], view(2, P, 0, C, T)).then_inc(c_xg, 1)
                    at(c_xg, 1, 0)
                    link(v.tensor_scalar(c_pen[:, :], c_pos[:, :], c_iv[:, 1:2], None, ALU.is_le))
                    link(v.tensor_tensor(c_pen[:, :], c_pen[:, :], const[0:T, CONST["block"][0]:CONST["block"][1]],
                                         ALU.mult))
                    link(v.tensor_scalar(c_pen[:, :], c_pen[:, :], 1e30, -1e30, ALU.mult, ALU.add))
                elif step == C_QKVED:
                    at(c_qkv, 1, 0)
                    v.tensor_copy(c_vT[:, :], view(2, P, 2 * T, T))
                    v.tensor_copy(c_hotT[:, :], view(2, T, 3 * T, T))
                    link(v.tensor_copy(c_qk[:, :, :], view(2, P, 0, 2, T)))
                    half = ROT // 2
                    for lo, to in ((0, half), (half, 0)):
                        ins = v.tensor_tensor(c_rot[to:to + half], c_qk[lo:lo + half],
                                              windows(c_cs[lo:lo + half, 1, :], (0, 2), (1, T)), ALU.mult)
                    link(ins)
                    link(v.tensor_tensor(c_qk[0:ROT], c_qk[0:ROT], windows(c_cs[:, 0, :], (0, 2), (1, T)), ALU.mult))
                    v.tensor_tensor(c_qk[0:ROT], c_qk[0:ROT], c_rot[:, :, :], ALU.add).then_inc(c_qk_ready, 1)
                elif step == C_SCORE:
                    at(c_spsum, 1, 0)
                    v.tensor_copy(c_v[:, :], view(2, T, T, HP))
                    link(v.tensor_tensor(c_pen[:, :], c_pen[:, :], view(2, T, 0, T), ALU.add))
                    link(v.tensor_reduce(sc1[0:T, 4:5], c_pen[:, :], AX.X, ALU.max, negate=True))
                    v.tensor_scalar(sc1[0:T, 4:5], sc1[0:T, 4:5], HP ** -0.5, None, ALU.mult).then_inc(c_nm, 1)
                elif step == C_NORM:
                    at(c_exp, 1, 0)
                    link(v.reciprocal(sc1[0:T, 5:6], sc1[0:T, 5:6]))
                    v.tensor_scalar(c_e[:, :], c_e[:, :], sc1[0:T, 5:6], c_iv[:, 0:1], ALU.mult, ALU.mult
                                    ).then_inc(c_en2, 1)
                elif step == C_PROB_T:
                    at(c_etp, 1, 0)
                    v.tensor_copy(c_eT[:, :], view(2, T, 0, T)).then_inc(c_et, 1)
                elif step == C_AV:
                    at(c_avp, 1, 0)
                    v.tensor_copy(c_avT[:, :], view(2, P, 0, T)).then_inc(c_av, 1)
                elif step == C_UPPED:
                    at(c_xpp, 1, 0)
                    v.tensor_copy(c_xpT[:, :, :], view(2, P, 0, C, T)).then_inc(c_xps, 1)
                elif step == C_UP_T:
                    at(c_xqp, 1, 0)
                    v.tensor_copy(c_xp[:, :], view(2, T, 0, D)).then_inc(c_xqs, 1)
                elif step == C_OUT:
                    at(x_out_free, 1, 0)
                    add_to_x(2, x_out)

            both = FRONT_STEPS + TAIL_STEPS
            before[0] = lambda n: n
            ctx_moments(0)
            prepare_ctx(0)
            prepare_x(0)
            dve.wait_ge(w_small, 48)
            v.tensor_copy(ident_b[:, :], ident)
            for r in range(4):
                for g in range(4):
                    v.tensor_scalar(sel_b[:, r, g, :], windows(ident[:, 32 * r + g:32 * r + g + 1], (0, T)), -1.0, None,
                                    ALU.mult)
            dve.wait_ge(zeros_made, 1)
            for e in range(NE):
                ins = v.tensor_copy(vb_cols[:, e, :, e], cols[:, COLS["vb"] + e * C:COLS["vb"] + (e + 1) * C])
            ins.then_inc(consts_made, 1)
            dve.wait_ge(consts_made, 1)
            assert count[0] == FIRST_STEPS
            front(0, None)
            assert count[0] == FIRST_STEPS + FRONT_STEPS, count[0]
            count[0] = 0
            with dve.Fori(1, B) as b:
                before[0] = lambda n: b * both + (n + FIRST_STEPS - TAIL_STEPS)
                front(b, b - 1)
                assert (count[0], norms[1]) == (both, TAIL_NORMS), (count[0], norms[1])
            count[0] = 0
            before[0] = lambda n: B * both + (n + FIRST_STEPS - TAIL_STEPS)
            for step in range(C_OUT + 1):
                tail_step(step, B - 1)


def rope_tables():
    half = ROT // 2
    inv = (np.float32(1.0) / np.power(np.float32(10000.0), np.arange(half, dtype=np.float32) * np.float32(2.0)
                                      / np.float32(ROT))).astype(np.float32)
    ang = (np.arange(T, dtype=np.float32)[:, None] * inv).astype(np.float32)
    sin, cos = np.sin(ang).astype(np.float32), np.cos(ang).astype(np.float32)
    return np.concatenate([cos, cos, sin, -sin], axis=1)


def const_table():
    c = np.zeros((P, NCONST), np.float32)

    def part(name):
        lo, hi = CONST[name]
        return c[:, lo:hi]

    part("ident")[:] = np.eye(P)
    for t in range(T):
        if t + LK - 1 - LPAD < T + LK - 1:
            part("band")[t, t + LK - 1 - LPAD] = 1.0
    for e in range(NE):
        part("own")[e, e * TK:(e + 1) * TK] = 1.0
        part("block")[e * TK:(e + 1) * TK, e * TK:(e + 1) * TK] = 1.0
    part("rope")[:T] = rope_tables()
    part("iota8")[:] = np.arange(NE)
    return c


def tiles(v):
    return v.reshape(-1, P).T


def kernel(**inputs):
    import concourse.bacc as bacc
    from concourse.bass_utils import run_bass_kernel_spmd

    i = {k: np.asarray(v) for k, v in inputs.items()}
    cols = np.zeros((P, NCOLS), np.float32)
    parts = np.arange(P)
    for name, v in (("lat_w", i["L0_xattn_ln_l_w"]), ("lat_b", i["L0_xattn_ln_l_b"]), ("ctx_w", i["L0_xattn_ln_c_w"]),
                    ("ctx_b", i["L0_xattn_ln_c_b"]), ("qb", i["L0_ffn_qb"].reshape(-1)),
                    ("kb", i["L0_ffn_kb"].reshape(-1)), ("vb", i["L0_ffn_vb"].reshape(-1)),
                    ("ret_g", i["L0_attn_ln_g"]), ("ret_b", i["L0_attn_ln_b"]), ("ffn_g", i["L0_ffn_ln_g"]),
                    ("ffn_b", i["L0_ffn_ln_b"]),
                    ("lam", np.repeat(i["L0_attn_decay"][:, 1, 0], D // 16)),
                    ("v", i["L1_attn_v"][:, 0]), ("iota", parts), ("even", parts // ED % 2 == 0),
                    ("odd", parts // ED % 2 == 1), ("one", np.ones(P))):
        t = tiles(v)
        cols[:, COLS[name]:COLS[name] + t.shape[1]] = t
    rows = np.concatenate([i[k].reshape(-1) for k in ("L0_xattn_bo", "L0_ffn_rb1", "L0_ffn_rb2")])
    arrays = {
        "x": i["x"], "ctx": i["ctx_1024"], "ctxT": i["ctx_1024"].transpose(0, 2, 1),
        "cols": cols, "rows": rows, "const": const_table(),
        "ret_q": i["L0_attn_Wq"].T, "ret_v": i["L0_attn_Wv"].T, "ret_g": i["L0_attn_Wg"].T, "ret_o": i["L0_attn_Wo"].T,
        "x_q": i["L0_xattn_Wq"], "x_kv": i["L0_xattn_Wkv"], "x_o": i["L0_xattn_Wo"],
        "r_w1": i["L0_ffn_rW1"].T, "r_w2": i["L0_ffn_rW2"].T, "e_bo": i["L0_ffn_ob"],
        "e_q": i["L0_ffn_qW"].transpose(0, 2, 1), "e_k": i["L0_ffn_kW"].transpose(0, 2, 1),
        "e_v": i["L0_ffn_vW"].transpose(0, 2, 1), "e_o": i["L0_ffn_oW"].transpose(0, 2, 1),
        "l_w1": i["L1_attn_w1"], "l_w2": i["L1_attn_w2"],
        "m_q": i["L1_xattn_Wq"].T, "m_k": i["L1_xattn_Wk"].T, "m_v": i["L1_xattn_Wv"].T, "m_o": i["L1_xattn_Wo"],
        "c_r": i["L1_ffn_Wr"].T, 
        "c_qk": i["L1_ffn_Wqkv"][:, :, :2 * HP].reshape(NE, D, 2, HP).transpose(2, 0, 1, 3).reshape(2 * NE, D, HP),
        "c_v": i["L1_ffn_Wqkv"][:, :, 2 * HP:], "c_o": i["L1_ffn_Wo"],
    }
    for k, v in arrays.items():
        if k not in ("x", "ctx", "ctxT", "cols", "rows", "const", "r_w2", "e_bo"):
            v = v.reshape(*v.shape[:-2], -1, P, v.shape[-1])
            arrays[k] = np.moveaxis(v, -2, 0)
    arrays["c_o"] = arrays["c_o"][:, :, 0]
    arrays = {f"in_{k}": np.ascontiguousarray(v) for k, v in arrays.items()}
    nc = bacc.Bacc("TRN2", target_bir_lowering=False, num_devices=1)
    aps = {k[3:]: nc.dram_tensor(k, v.shape, mybir.dt.from_np(v.dtype), kind="ExternalInput").ap()
           for k, v in arrays.items()}
    out = nc.dram_tensor("out", (B, T, D), F32, kind="ExternalOutput").ap()
    build(nc, aps, out)
    r = run_bass_kernel_spmd(nc, [arrays], core_ids=[0])
    return r.results[0]["out"]
```
